# Optimizing a Trainium2 kernel written in Bass

```python
import numpy as np
import jax
import jax.numpy as jnp

def _softmax(x, axis=-1):
    return jax.nn.softmax(x, axis=axis)

def _gelu(x):
    return jax.nn.gelu(x, approximate=True)

def _silu(x):
    return jax.nn.silu(x)

def _sigmoid(x):
    return jax.nn.sigmoid(x)

def _layernorm(x, axis=-1, eps=1e-05):
    m = jnp.mean(x, axis=axis, keepdims=True)
    v = jnp.var(x, axis=axis, keepdims=True)
    return (x - m) / jnp.sqrt(v + eps)

def _scatter_add(tgt, idx, src, axis=0):
    return tgt.at[idx].add(src)

def _segment_sum(src, seg, n):
    return jax.ops.segment_sum(src, seg, n)
kernel_name = 'mk_decoder_postln_d2_seqx_r8_1f58c5'

def setup_inputs(seed: int=0):
    np.random.seed(seed)
    _w = jnp.asarray

    def _rec_inputs():
        import jax
        import jax.numpy as jnp
        _rk = jax.random.key(seed)
        x = -0.000125 + 0.9999 * jax.random.normal(jax.random.fold_in(_rk, 1), (8, 128, 256), jnp.float32)
        _lenS = 128 - jax.random.randint(jax.random.fold_in(_rk, 7), (8,), 0, max(1, 128 // 4) + 1, jnp.int32)
        _lenS2 = 128 - jax.random.randint(jax.random.fold_in(_rk, 8), (8,), 0, max(1, 128 // 4) + 1, jnp.int32)
        _ctx_2048P = jax.random.normal(jax.random.fold_in(_rk, 11), (8, 16, 256), jnp.float32)
        _ctx_2048c = jax.random.dirichlet(jax.random.fold_in(_rk, 511), 0.3 * jnp.ones((16,), jnp.float32), (8, 128))
        _ctx_2048t = jnp.einsum('bsk,bkd->bsd', _ctx_2048c, _ctx_2048P)
        _ctx_2048t = _ctx_2048t * jax.lax.rsqrt(jnp.mean(jnp.square(_ctx_2048t)) + 1e-12) * 0.953939
        ctx_2048 = -1.52775e-05 + 0.999936 * (_ctx_2048t + 0.3 * jax.random.normal(jax.random.fold_in(_rk, 611), (8, 128, 256), jnp.float32))
        _validS = jnp.arange(128)[None, :] < _lenS[:, None]
        _validS2 = jnp.arange(128)[None, :] < _lenS2[:, None]
        _causal = jnp.tril(jnp.ones((128, 128), dtype=bool))
        mask_BxS2_ff1 = jnp.where(jnp.ones((8, 128), dtype=bool), 1.0, 0.0).astype(jnp.float32)
        return (x, ctx_2048, mask_BxS2_ff1)
    x, ctx_2048, mask_BxS2_ff1 = _rec_inputs()

    def _L0_attn_setup():
        import jax, jax.numpy as jnp
        import numpy as np
        B, T, D_MODEL = (4, 512, 256)
        D_LATENT = 64
        D_COMP = 32
        THETA = 10000.0
        LN_EPS = 1e-05

        def _rope_tables(seq_len: int, dim: int):
            inv_freq = 1.0 / THETA ** (jnp.arange(0, dim, 2, dtype=jnp.float32) / dim)
            freqs = jnp.arange(seq_len, dtype=jnp.float32)[:, None] * inv_freq[None, :]
            cos = jnp.concatenate([jnp.cos(freqs), jnp.cos(freqs)], axis=-1)
            sin = jnp.concatenate([jnp.sin(freqs), jnp.sin(freqs)], axis=-1)
            return (cos, sin)

        def _rotate_half(x):
            x1, x2 = jnp.split(x, 2, axis=-1)
            return jnp.concatenate([-x2, x1], axis=-1)
        key = jax.random.key(seed)
        ks = jax.random.split(key, 8)
        s = 0.02
        return {'x': jax.random.normal(ks[0], (B, T, D_MODEL), dtype=jnp.float32), 'W_to_kv': jax.random.normal(ks[1], (D_LATENT, D_MODEL), dtype=jnp.float32) * s, 'W_compress': jax.random.normal(ks[2], (D_COMP, D_LATENT), dtype=jnp.float32) * s, 'ln_gamma': jnp.ones((D_COMP,), dtype=jnp.float32), 'ln_beta': jnp.zeros((D_COMP,), dtype=jnp.float32), 'W_q_comp': jax.random.normal(ks[3], (D_COMP, D_COMP), dtype=jnp.float32) * s, 'W_kv_comp': jax.random.normal(ks[4], (2 * D_COMP, D_COMP), dtype=jnp.float32) * s, 'W_comp2lat': jax.random.normal(ks[5], (D_LATENT, D_COMP), dtype=jnp.float32) * s, 'W_out_res': jnp.zeros((D_MODEL, D_LATENT), dtype=jnp.float32), 'b_out_res': jnp.zeros((D_MODEL,), dtype=jnp.float32)}
    _L0_attn_all = _L0_attn_setup()
    _L0_attn_in = {k: v for k, v in _L0_attn_all.items() if k in ('W_to_kv', 'W_compress', 'ln_gamma', 'ln_beta', 'W_q_comp', 'W_kv_comp', 'W_comp2lat', 'W_out_res', 'b_out_res')}
    del _L0_attn_all

    def _L0_xattn_setup():
        import jax, jax.numpy as jnp
        import numpy as np
        H = 256
        NH = 16
        HD = H // NH
        FD = 64
        key = jax.random.key(seed)
        ks = jax.random.split(key, 12)
        B, S = (4, 512)
        s = 1.0 / np.sqrt(H)
        sf = 1.0 / np.sqrt(HD)
        return {'query': jax.random.normal(ks[0], (B, S, H), jnp.float32), 'key': jax.random.normal(ks[1], (B, S, H), jnp.float32), 'value': jax.random.normal(ks[2], (B, S, H), jnp.float32), 'attention_mask': jnp.ones((B, S), jnp.float32), 'Wq': jax.random.normal(ks[3], (H, H), jnp.float32) * s, 'bq': jnp.zeros((H,), jnp.float32), 'Wk': jax.random.normal(ks[4], (H, H), jnp.float32) * s, 'bk': jnp.zeros((H,), jnp.float32), 'Wv': jax.random.normal(ks[5], (H, H), jnp.float32) * s, 'bv': jnp.zeros((H,), jnp.float32), 'Wqf': jax.random.normal(ks[6], (FD, HD), jnp.float32) * sf, 'Wkf': jax.random.normal(ks[7], (FD, HD), jnp.float32) * sf, 'Wo': jax.random.normal(ks[8], (H, H), jnp.float32) * s, 'bo': jnp.zeros((H,), jnp.float32)}
    _L0_xattn_all = _L0_xattn_setup()
    _L0_xattn_in = {k: v for k, v in _L0_xattn_all.items() if k in ('Wq', 'bq', 'Wk', 'bk', 'Wv', 'bv', 'Wqf', 'Wkf', 'Wo', 'bo')}
    del _L0_xattn_all

    def _L0_ffn_setup():
        import jax, jax.numpy as jnp
        import numpy as np
        NUM_EXPERTS = 8
        HIDDEN = 256
        INTER = 256
        TOP_K = 2
        key = jax.random.key(seed)
        ks = jax.random.split(key, 7)
        hidden_states = jax.random.normal(ks[0], (4, 256, HIDDEN), dtype=jnp.float32)
        gate_w = jax.random.normal(ks[1], (HIDDEN, NUM_EXPERTS), dtype=jnp.float32) * 0.02
        fc1_w = jax.random.normal(ks[2], (NUM_EXPERTS, HIDDEN, INTER), dtype=jnp.float32) * 0.02
        fc1_b = jnp.zeros((NUM_EXPERTS, INTER), dtype=jnp.float32)
        fc2_w = jax.random.normal(ks[3], (NUM_EXPERTS, INTER, HIDDEN), dtype=jnp.float32) * 0.02
        fc2_b = jnp.zeros((NUM_EXPERTS, HIDDEN), dtype=jnp.float32)
        alpha = jax.random.normal(ks[4], (NUM_EXPERTS,), dtype=jnp.float32)
        return {'hidden_states': hidden_states, 'gate_w': gate_w, 'fc1_w': fc1_w, 'fc1_b': fc1_b, 'fc2_w': fc2_w, 'fc2_b': fc2_b, 'alpha': alpha}
    _L0_ffn_all = _L0_ffn_setup()
    _L0_ffn_in = {k: v for k, v in _L0_ffn_all.items() if k in ('gate_w', 'fc1_w', 'fc1_b', 'fc2_w', 'fc2_b', 'alpha')}
    del _L0_ffn_all

    def _L1_attn_setup():
        import jax, jax.numpy as jnp
        import numpy as np
        HIDDEN = 256
        NUM_HEADS = 32
        HEAD_DIM = 64
        NUM_KV = 8
        GROUP = NUM_HEADS // NUM_KV
        SCALE = HEAD_DIM ** (-0.5)
        ROPE_BASE = 10000.0

        def apply_rope(t):
            S, D = (t.shape[-2], t.shape[-1])
            inv_freq = 1.0 / ROPE_BASE ** (jnp.arange(0, D, 2, dtype=jnp.float32) / D)
            ang = jnp.arange(S, dtype=jnp.float32)[:, None] * inv_freq[None, :]
            cos, sin = (jnp.cos(ang), jnp.sin(ang))
            x1, x2 = (t[..., :D // 2], t[..., D // 2:])
            return jnp.concatenate([x1 * cos - x2 * sin, x2 * cos + x1 * sin], axis=-1)
        key = jax.random.key(seed)
        ks = jax.random.split(key, 10)
        B, S = (2, 256)
        s_in = HIDDEN ** (-0.5)
        s_o = (NUM_HEADS * HEAD_DIM) ** (-0.5)
        return {'x': jax.random.normal(ks[0], (B, S, HIDDEN), jnp.float32), 'Wq': jax.random.normal(ks[1], (NUM_HEADS * HEAD_DIM, HIDDEN), jnp.float32) * s_in, 'bq': jnp.zeros((NUM_HEADS * HEAD_DIM,), jnp.float32), 'Wk': jax.random.normal(ks[2], (NUM_KV * HEAD_DIM, HIDDEN), jnp.float32) * s_in, 'bk': jnp.zeros((NUM_KV * HEAD_DIM,), jnp.float32), 'Wv': jax.random.normal(ks[3], (NUM_KV * HEAD_DIM, HIDDEN), jnp.float32) * s_in, 'bv': jnp.zeros((NUM_KV * HEAD_DIM,), jnp.float32), 'Wo': jax.random.normal(ks[4], (HIDDEN, NUM_HEADS * HEAD_DIM), jnp.float32) * s_o, 'bo': jnp.zeros((HIDDEN,), jnp.float32), 'key_weights': jax.random.normal(ks[5], (NUM_HEADS,), jnp.float32)}
    _L1_attn_all = _L1_attn_setup()
    _L1_attn_in = {k: v for k, v in _L1_attn_all.items() if k in ('Wq', 'bq', 'Wk', 'bk', 'Wv', 'bv', 'Wo', 'bo', 'key_weights')}
    del _L1_attn_all

    def _L1_xattn_setup():
        import jax, jax.numpy as jnp
        import numpy as np
        D_MODEL = 256
        NUM_HEADS = 16
        HEAD_DIM = D_MODEL // NUM_HEADS

        def _fq_sym(x, axis):
            s = jnp.max(jnp.abs(x), axis=axis, keepdims=True) / 127.0
            s = jnp.maximum(s, 1e-08)
            q = jnp.clip(jnp.round(x / s), -127.0, 127.0) * s
            return x + jax.lax.stop_gradient(q - x)

        def _fq_unsigned(x, axis):
            s = jnp.max(x, axis=axis, keepdims=True) / 255.0
            s = jnp.maximum(s, 1e-08)
            q = jnp.clip(jnp.round(x / s), 0.0, 255.0) * s
            return x + jax.lax.stop_gradient(q - x)
        key = jax.random.key(seed)
        ks = jax.random.split(key, 8)
        B, N, M, C = (2, 256, 64, D_MODEL)
        return {'x': jax.random.normal(ks[0], (B, N, C), jnp.float32), 'cond': jax.random.normal(ks[1], (B, M, C), jnp.float32), 'Wq': jax.random.normal(ks[2], (C, C), jnp.float32) * 0.02, 'bq': jnp.zeros((C,), jnp.float32), 'Wkv': jax.random.normal(ks[3], (C, 2 * C), jnp.float32) * 0.02, 'bkv': jnp.zeros((2 * C,), jnp.float32), 'Wp': jax.random.normal(ks[4], (C, C), jnp.float32) * 0.02, 'bp': jnp.zeros((C,), jnp.float32)}
    _L1_xattn_all = _L1_xattn_setup()
    _L1_xattn_in = {k: v for k, v in _L1_xattn_all.items() if k in ('Wq', 'bq', 'Wkv', 'bkv', 'Wp', 'bp')}
    del _L1_xattn_all

    def _L1_ffn_setup():
        import jax, jax.numpy as jnp
        import numpy as np
        E, H, I = (8, 256, 512)
        TOP_K = 1
        B, S = (1, 256)
        key = jax.random.key(seed)
        ks = jax.random.split(key, 7)
        std = 0.02
        return {'hidden_states': jax.random.normal(ks[0], (B, S, H), dtype=jnp.float32), 'router_w': jax.random.normal(ks[1], (E, H), dtype=jnp.float32) * std, 'gate_up_proj': jax.random.normal(ks[2], (E, H, 2 * I), dtype=jnp.float32) * std, 'down_proj': jax.random.normal(ks[3], (E, I, H), dtype=jnp.float32) * std, 'shared_gate_w': jax.random.normal(ks[4], (H, I), dtype=jnp.float32) * std, 'shared_up_w': jax.random.normal(ks[5], (H, I), dtype=jnp.float32) * std, 'shared_down_w': jax.random.normal(ks[6], (I, H), dtype=jnp.float32) * std}
    _L1_ffn_all = _L1_ffn_setup()
    _L1_ffn_in = {k: v for k, v in _L1_ffn_all.items() if k in ('router_w', 'gate_up_proj', 'down_proj', 'shared_gate_w', 'shared_up_w', 'shared_down_w')}
    del _L1_ffn_all
    return {'x': x, 'ctx_2048': ctx_2048, 'mask_BxS2_ff1': mask_BxS2_ff1, 'L0_attn_W_to_kv': _L0_attn_in['W_to_kv'], 'L0_attn_W_compress': _L0_attn_in['W_compress'], 'L0_attn_ln_gamma': _L0_attn_in['ln_gamma'], 'L0_attn_ln_beta': _L0_attn_in['ln_beta'], 'L0_attn_W_q_comp': _L0_attn_in['W_q_comp'], 'L0_attn_W_kv_comp': _L0_attn_in['W_kv_comp'], 'L0_attn_W_comp2lat': _L0_attn_in['W_comp2lat'], 'L0_attn_W_out_res': _L0_attn_in['W_out_res'], 'L0_attn_b_out_res': _L0_attn_in['b_out_res'], 'L0_xattn_Wq': _L0_xattn_in['Wq'], 'L0_xattn_bq': _L0_xattn_in['bq'], 'L0_xattn_Wk': _L0_xattn_in['Wk'], 'L0_xattn_bk': _L0_xattn_in['bk'], 'L0_xattn_Wv': _L0_xattn_in['Wv'], 'L0_xattn_bv': _L0_xattn_in['bv'], 'L0_xattn_Wqf': _L0_xattn_in['Wqf'], 'L0_xattn_Wkf': _L0_xattn_in['Wkf'], 'L0_xattn_Wo': _L0_xattn_in['Wo'], 'L0_xattn_bo': _L0_xattn_in['bo'], 'L0_ffn_gate_w': _L0_ffn_in['gate_w'], 'L0_ffn_fc1_w': _L0_ffn_in['fc1_w'], 'L0_ffn_fc1_b': _L0_ffn_in['fc1_b'], 'L0_ffn_fc2_w': _L0_ffn_in['fc2_w'], 'L0_ffn_fc2_b': _L0_ffn_in['fc2_b'], 'L0_ffn_alpha': _L0_ffn_in['alpha'], 'L1_attn_Wq': _L1_attn_in['Wq'], 'L1_attn_bq': _L1_attn_in['bq'], 'L1_attn_Wk': _L1_attn_in['Wk'], 'L1_attn_bk': _L1_attn_in['bk'], 'L1_attn_Wv': _L1_attn_in['Wv'], 'L1_attn_bv': _L1_attn_in['bv'], 'L1_attn_Wo': _L1_attn_in['Wo'], 'L1_attn_bo': _L1_attn_in['bo'], 'L1_attn_key_weights': _L1_attn_in['key_weights'], 'L1_xattn_Wq': _L1_xattn_in['Wq'], 'L1_xattn_bq': _L1_xattn_in['bq'], 'L1_xattn_Wkv': _L1_xattn_in['Wkv'], 'L1_xattn_bkv': _L1_xattn_in['bkv'], 'L1_xattn_Wp': _L1_xattn_in['Wp'], 'L1_xattn_bp': _L1_xattn_in['bp'], 'L1_ffn_router_w': _L1_ffn_in['router_w'], 'L1_ffn_gate_up_proj': _L1_ffn_in['gate_up_proj'], 'L1_ffn_down_proj': _L1_ffn_in['down_proj'], 'L1_ffn_shared_gate_w': _L1_ffn_in['shared_gate_w'], 'L1_ffn_shared_up_w': _L1_ffn_in['shared_up_w'], 'L1_ffn_shared_down_w': _L1_ffn_in['shared_down_w']}

def reference(x, ctx_2048, mask_BxS2_ff1, L0_attn_W_to_kv, L0_attn_W_compress, L0_attn_ln_gamma, L0_attn_ln_beta, L0_attn_W_q_comp, L0_attn_W_kv_comp, L0_attn_W_comp2lat, L0_attn_W_out_res, L0_attn_b_out_res, L0_xattn_Wq, L0_xattn_bq, L0_xattn_Wk, L0_xattn_bk, L0_xattn_Wv, L0_xattn_bv, L0_xattn_Wqf, L0_xattn_Wkf, L0_xattn_Wo, L0_xattn_bo, L0_ffn_gate_w, L0_ffn_fc1_w, L0_ffn_fc1_b, L0_ffn_fc2_w, L0_ffn_fc2_b, L0_ffn_alpha, L1_attn_Wq, L1_attn_bq, L1_attn_Wk, L1_attn_bk, L1_attn_Wv, L1_attn_bv, L1_attn_Wo, L1_attn_bo, L1_attn_key_weights, L1_xattn_Wq, L1_xattn_bq, L1_xattn_Wkv, L1_xattn_bkv, L1_xattn_Wp, L1_xattn_bp, L1_ffn_router_w, L1_ffn_gate_up_proj, L1_ffn_down_proj, L1_ffn_shared_gate_w, L1_ffn_shared_up_w, L1_ffn_shared_down_w):
    import jax
    import jax.numpy as jnp

    def _L0_attn_ref(x, W_to_kv, W_compress, ln_gamma, ln_beta, W_q_comp, W_kv_comp, W_comp2lat, W_out_res, b_out_res):
        import jax, jax.numpy as jnp
        import numpy as np
        B, T, D_MODEL = (4, 512, 256)
        D_LATENT = 64
        D_COMP = 32
        THETA = 10000.0
        LN_EPS = 1e-05

        def _rope_tables(seq_len: int, dim: int):
            inv_freq = 1.0 / THETA ** (jnp.arange(0, dim, 2, dtype=jnp.float32) / dim)
            freqs = jnp.arange(seq_len, dtype=jnp.float32)[:, None] * inv_freq[None, :]
            cos = jnp.concatenate([jnp.cos(freqs), jnp.cos(freqs)], axis=-1)
            sin = jnp.concatenate([jnp.sin(freqs), jnp.sin(freqs)], axis=-1)
            return (cos, sin)

        def _rotate_half(x):
            x1, x2 = jnp.split(x, 2, axis=-1)
            return jnp.concatenate([-x2, x1], axis=-1)
        Bx, Tx, _ = x.shape
        dc = W_compress.shape[0]
        kv_latent = x @ W_to_kv.T
        c = kv_latent @ W_compress.T
        mu = jnp.mean(c, axis=-1, keepdims=True)
        var = jnp.mean((c - mu) ** 2, axis=-1, keepdims=True)
        ch = (c - mu) * jax.lax.rsqrt(var + LN_EPS) * ln_gamma + ln_beta
        q = ch @ W_q_comp.T
        kv = ch @ W_kv_comp.T
        k, v = jnp.split(kv, 2, axis=-1)
        cos, sin = _rope_tables(Tx, dc)
        q = q * cos + _rotate_half(q) * sin
        k = k * cos + _rotate_half(k) * sin
        scale = 1.0 / jnp.sqrt(jnp.float32(dc))
        scores = jnp.einsum('btd,bsd->bts', q, k) * scale
        causal = jnp.tril(jnp.ones((Tx, Tx), dtype=bool))
        scores = jnp.where(causal[None], scores, jnp.float32(-1e+30))
        attn = jax.nn.softmax(scores, axis=-1)
        o = jnp.einsum('bts,bsd->btd', attn, v)
        z = o @ W_comp2lat.T
        out = z @ W_to_kv + z @ W_out_res.T + b_out_res
        return out

    def _L0_xattn_ref(query, key, value, attention_mask, Wq, bq, Wk, bk, Wv, bv, Wqf, Wkf, Wo, bo):
        import jax, jax.numpy as jnp
        import numpy as np
        H = 256
        NH = 16
        HD = H // NH
        FD = 64
        B, Sq, _ = query.shape
        Sk = key.shape[1]

        def heads(x, W, b, S):
            return (x @ W.T + b).reshape(B, S, NH, HD).transpose(0, 2, 1, 3)
        q = heads(query, Wq, bq, Sq)
        k = heads(key, Wk, bk, Sk)
        v = heads(value, Wv, bv, Sk)
        q_prime = jax.nn.relu(jnp.einsum('bhnd,fd->bhnf', q, Wqf))
        k_prime = jax.nn.relu(jnp.einsum('bhnd,fd->bhnf', k, Wkf))
        k_prime = k_prime * attention_mask[:, None, :, None]
        kv = jnp.einsum('bhnf,bhne->bhfe', k_prime, v)
        qkv = jnp.einsum('bhmf,bhfe->bhme', q_prime, kv)
        k_sum = jnp.sum(k_prime, axis=2)
        qk_sum = jnp.einsum('bhmf,bhf->bhm', q_prime, k_sum)[..., None]
        out = qkv / (qk_sum + 1e-08)
        out = out.transpose(0, 2, 1, 3).reshape(B, Sq, H)
        return out @ Wo.T + bo

    def _L0_ffn_ref(hidden_states, gate_w, fc1_w, fc1_b, fc2_w, fc2_b, alpha):
        import jax, jax.numpy as jnp
        import numpy as np
        NUM_EXPERTS = 8
        HIDDEN = 256
        INTER = 256
        TOP_K = 2
        B, S, H = hidden_states.shape
        x = hidden_states.reshape(-1, H)
        probs = jax.nn.softmax(x @ gate_w, axis=-1)
        gate_score, gate_idx = jax.lax.top_k(probs, TOP_K)
        gate_score = gate_score / jnp.sum(gate_score, axis=-1, keepdims=True)
        onehot = jax.nn.one_hot(gate_idx, NUM_EXPERTS, dtype=x.dtype)
        combine = jnp.einsum('tk,tke->te', gate_score, onehot) * alpha[None, :]
        h = jnp.einsum('th,ehi->eti', x, fc1_w) + fc1_b[:, None, :]
        h = jax.nn.gelu(h, approximate=False)
        y = jnp.einsum('eti,eih->eth', h, fc2_w) + fc2_b[:, None, :]
        out = jnp.einsum('eth,te->th', y, combine)
        return out.reshape(B, S, H)

    def _L1_attn_ref(x, Wq, bq, Wk, bk, Wv, bv, Wo, bo, key_weights):
        import jax, jax.numpy as jnp
        import numpy as np
        HIDDEN = 256
        NUM_HEADS = 32
        HEAD_DIM = 64
        NUM_KV = 8
        GROUP = NUM_HEADS // NUM_KV
        SCALE = HEAD_DIM ** (-0.5)
        ROPE_BASE = 10000.0

        def apply_rope(t):
            S, D = (t.shape[-2], t.shape[-1])
            inv_freq = 1.0 / ROPE_BASE ** (jnp.arange(0, D, 2, dtype=jnp.float32) / D)
            ang = jnp.arange(S, dtype=jnp.float32)[:, None] * inv_freq[None, :]
            cos, sin = (jnp.cos(ang), jnp.sin(ang))
            x1, x2 = (t[..., :D // 2], t[..., D // 2:])
            return jnp.concatenate([x1 * cos - x2 * sin, x2 * cos + x1 * sin], axis=-1)
        B, S, _ = x.shape
        q = (x @ Wq.T + bq).reshape(B, S, NUM_HEADS, HEAD_DIM).transpose(0, 2, 1, 3)
        k = (x @ Wk.T + bk).reshape(B, S, NUM_KV, HEAD_DIM).transpose(0, 2, 1, 3)
        v = (x @ Wv.T + bv).reshape(B, S, NUM_KV, HEAD_DIM).transpose(0, 2, 1, 3)
        q = apply_rope(q)
        k = apply_rope(k)
        qg = q.reshape(B, NUM_KV, GROUP, S, HEAD_DIM)
        scores = jnp.einsum('bkgsd,bktd->bkgst', qg, k) * SCALE
        scores = scores * key_weights.reshape(1, NUM_KV, GROUP, 1, 1)
        causal = jnp.tril(jnp.ones((S, S), bool))
        scores = jnp.where(causal, scores, -jnp.inf)
        a = jax.nn.softmax(scores, axis=-1)
        o = jnp.einsum('bkgst,bktd->bkgsd', a, v)
        o = o.reshape(B, NUM_HEADS, S, HEAD_DIM).transpose(0, 2, 1, 3).reshape(B, S, NUM_HEADS * HEAD_DIM)
        return o @ Wo.T + bo

    def _L1_xattn_ref(x, cond, Wq, bq, Wkv, bkv, Wp, bp):
        import jax, jax.numpy as jnp
        import numpy as np
        D_MODEL = 256
        NUM_HEADS = 16
        HEAD_DIM = D_MODEL // NUM_HEADS

        def _fq_sym(x, axis):
            s = jnp.max(jnp.abs(x), axis=axis, keepdims=True) / 127.0
            s = jnp.maximum(s, 1e-08)
            q = jnp.clip(jnp.round(x / s), -127.0, 127.0) * s
            return x + jax.lax.stop_gradient(q - x)

        def _fq_unsigned(x, axis):
            s = jnp.max(x, axis=axis, keepdims=True) / 255.0
            s = jnp.maximum(s, 1e-08)
            q = jnp.clip(jnp.round(x / s), 0.0, 255.0) * s
            return x + jax.lax.stop_gradient(q - x)
        B, N, C = x.shape
        H, hd = (NUM_HEADS, HEAD_DIM)
        q = (x @ Wq + bq).reshape(1, B * N, H, hd)
        kv = (cond @ Wkv + bkv).reshape(1, -1, 2, H, hd)
        k, v = (kv[:, :, 0], kv[:, :, 1])
        scale = 1.0 / np.sqrt(hd).astype(np.float32)
        q = jnp.transpose(q * scale, (0, 2, 1, 3))
        k = jnp.transpose(k, (0, 2, 1, 3))
        v = jnp.transpose(v, (0, 2, 1, 3))
        q = _fq_sym(q, axis=-1)
        k = _fq_sym(k, axis=-1)
        v = _fq_sym(v, axis=2)
        attn = jnp.einsum('bhqd,bhkd->bhqk', q, k)
        attn = jax.nn.softmax(attn.astype(jnp.float32), axis=-1)
        attn = _fq_unsigned(attn, axis=-1)
        out = jnp.einsum('bhqk,bhkd->bhqd', attn, v)
        out = jnp.transpose(out, (0, 2, 1, 3)).reshape(B, N, C)
        return out @ Wp + bp

    def _L1_ffn_ref(hidden_states, router_w, gate_up_proj, down_proj, shared_gate_w, shared_up_w, shared_down_w):
        import jax, jax.numpy as jnp
        import numpy as np
        E, H, I = (8, 256, 512)
        TOP_K = 1
        B, S = (1, 256)
        orig_shape = hidden_states.shape
        x = hidden_states.reshape(-1, H)
        T = x.shape[0]
        logits = x @ router_w.T
        top_vals, top_idx = jax.lax.top_k(logits, TOP_K)
        scores = jnp.full_like(logits, -jnp.inf)
        scores = scores.at[jnp.arange(T)[:, None], top_idx].set(top_vals)
        scores = jax.nn.sigmoid(scores.astype(jnp.float32)).astype(logits.dtype)
        xr = x[None, :, :] * scores.T[:, :, None]
        gate_up = jnp.einsum('eth,ehf->etf', xr, gate_up_proj)
        gate, up = jnp.split(gate_up, 2, axis=-1)
        routed = jnp.einsum('etf,efh->eth', up * jax.nn.silu(gate), down_proj)
        routed_sum = routed.sum(axis=0)
        shared = jax.nn.silu(x @ shared_gate_w) * (x @ shared_up_w) @ shared_down_w
        return (shared + routed_sum).reshape(orig_shape)
    x = _layernorm(x + _L0_attn_ref(x, L0_attn_W_to_kv, L0_attn_W_compress, L0_attn_ln_gamma, L0_attn_ln_beta, L0_attn_W_q_comp, L0_attn_W_kv_comp, L0_attn_W_comp2lat, L0_attn_W_out_res, L0_attn_b_out_res), axis=-1)
    x = _layernorm(x + _L0_xattn_ref(x, ctx_2048, ctx_2048, mask_BxS2_ff1, L0_xattn_Wq, L0_xattn_bq, L0_xattn_Wk, L0_xattn_bk, L0_xattn_Wv, L0_xattn_bv, L0_xattn_Wqf, L0_xattn_Wkf, L0_xattn_Wo, L0_xattn_bo), axis=-1)
    x = _layernorm(x + _L0_ffn_ref(x, L0_ffn_gate_w, L0_ffn_fc1_w, L0_ffn_fc1_b, L0_ffn_fc2_w, L0_ffn_fc2_b, L0_ffn_alpha), axis=-1)
    x = _layernorm(x + _L1_attn_ref(x, L1_attn_Wq, L1_attn_bq, L1_attn_Wk, L1_attn_bk, L1_attn_Wv, L1_attn_bv, L1_attn_Wo, L1_attn_bo, L1_attn_key_weights), axis=-1)
    x = _layernorm(x + _L1_xattn_ref(x, ctx_2048, L1_xattn_Wq, L1_xattn_bq, L1_xattn_Wkv, L1_xattn_bkv, L1_xattn_Wp, L1_xattn_bp), axis=-1)
    x = _layernorm(x + _L1_ffn_ref(x, L1_ffn_router_w, L1_ffn_gate_up_proj, L1_ffn_down_proj, L1_ffn_shared_gate_w, L1_ffn_shared_up_w, L1_ffn_shared_down_w), axis=-1)
    return x

_drawn_inputs = setup_inputs


def setup_inputs(seed=0):
    import zlib

    import numpy as np

    out = dict(_drawn_inputs(seed))
    spreads = {'L0_attn_ln_gamma': (1.0, 0.6),
     'L0_attn_ln_beta': (0.0, 0.8),
     'L0_attn_W_out_res': (0.0, 0.8),
     'L0_attn_b_out_res': (0.0, 0.1),
     'L0_xattn_bq': (0.0, 0.8),
     'L0_xattn_bk': (0.0, 0.8),
     'L0_xattn_bv': (0.0, 0.1),
     'L0_xattn_bo': (0.0, 0.1),
     'L0_ffn_fc1_b': (0.0, 0.546),
     'L0_ffn_fc2_b': (0.0, 0.1),
     'L1_attn_bq': (0.0, 0.435),
     'L1_attn_bk': (0.0, 0.719),
     'L1_attn_bv': (0.0, 0.1),
     'L1_attn_bo': (0.0, 0.1),
     'L1_xattn_bq': (0.0, 0.8),
     'L1_xattn_bkv': (0.0, 0.275),
     'L1_xattn_bp': (0.0, 0.1)}
    factors = {'L0_attn_W_to_kv': 8.0,
     'L0_attn_W_compress': 8.0,
     'L0_attn_W_q_comp': 8.0,
     'L0_attn_W_kv_comp': 8.0,
     'L0_attn_W_comp2lat': 8.0,
     'L1_xattn_Wq': 8.0,
     'L1_xattn_Wkv': 3.589,
     'L1_ffn_router_w': 6.657,
     'L1_ffn_gate_up_proj': 6.01,
     'L1_ffn_down_proj': 5.975,
     'L1_ffn_shared_gate_w': 8.0,
     'L1_ffn_shared_up_w': 8.0,
     'L1_ffn_shared_down_w': 8.0}
    for name, (base, spread) in spreads.items():
        noise = np.random.default_rng([zlib.crc32(name.encode()), seed]).standard_normal(out[name].shape)
        drawn = base * np.exp(spread * noise) if base else spread * noise
        out[name] = jnp.asarray(drawn.astype(out[name].dtype))
    for name, factor in factors.items():
        out[name] = (out[name] * factor).astype(out[name].dtype)
    return out
```

```python
from contextlib import ExitStack

import concourse.bass as bass
from concourse import mybir

P = 128
F32 = mybir.dt.float32
BF16 = mybir.dt.bfloat16
I32 = mybir.dt.int32
ALU = mybir.AluOpType
ACT = mybir.ActivationFunctionType
AX = mybir.AxisListType.X
LN_EPS = 1e-5


class Banks:

    def __init__(self, psum, full, free):
        self.psum, self.full, self.free = psum, full, free
        self.n = [0] * len(full)
        self.next = 0
        self.uses = {}
        self.per = {}

    def take(self, key, count=1, bank=None, trip=0, per=0):
        nb = len(self.full)
        if bank is None:
            if self.next + count > nb:
                self.next = 0
            bank = self.next
            self.next = (bank + count) % nb
        waits = [(self.free[k], self.n[k] + trip * per) for k in range(bank, bank + count) if self.n[k]]
        for k in range(bank, bank + count):
            self.n[k] += 1
        self.uses[key] = [(k, self.n[k], per) for k in range(bank, bank + count)]
        return waits

    def looped(self, trips, per, banks=None):
        for k in banks or range(len(self.n)):
            self.n[k] += (trips - 1) * per

    def at(self, key, j=0):
        return self.psum[:, self.uses[key][j][0], :]

    def span(self, key):
        first, count = self.uses[key][0][0], len(self.uses[key])
        return self.psum[:, first:first + count, :].rearrange("p k n -> p (k n)")

    def filled(self, key, j=0, trip=0):
        k, n, per = self.uses[key][j]
        return self.full[k], n + trip * per

    def read(self, key, j=0, trip=0):
        k, n, per = self.uses[key][j]
        return self.free[k], n + trip * per

    def full_of(self, key, j=0):
        return self.full[self.uses[key][j][0]]

    def free_of(self, key, j=0):
        return self.free[self.uses[key][j][0]]


def build(nc, T, W, out):
    NB, D = T["NB"], T["D"]
    N = NB * P
    KD = D // P
    G = N // 512
    ctx = ExitStack()
    with ctx:
        def sb(name, shape, dt=F32):
            return ctx.enter_context(nc.sbuf_tensor(name, shape, dt))

        def sem(name):
            return ctx.enter_context(nc.semaphore(name))

        psum = ctx.enter_context(nc.psum_tensor("psum", [P, 8, 512], F32))
        banks = Banks(psum, [sem(f"bank_full{k}") for k in range(8)], [sem(f"bank_free{k}") for k in range(8)])
        take, at, span, filled, read, full_of, free_of = (banks.take, banks.at, banks.span, banks.filled, banks.read,
                                                          banks.full_of, banks.free_of)

        X = sb("X", [P, NB, D])
        H = sb("H", [P, NB, D])
        XB = sb("XB", [P, NB, D])
        XT_flat = sb("XT", [P, KD * N + P])
        XT = XT_flat[:, 0:KD * N].rearrange("p (k n) -> p k n", k=KD)
        XT_next = XT_flat[:, P:KD * N + P].rearrange("p (k n) -> p k n", k=KD)
        ctxT = sb("ctxT", [P, KD, N])
        ident = sb("ident", [P, P])
        neghalf = sb("neghalf", [P, NB])
        st = sb("st", [P, NB, 6])
        mv = sb("mv", [P, NB, 2])
        ve = sb("ve", [P, NB])
        rstd = sb("rstd", [P, NB])
        biases = sb("biases", [P, 4, D])

        HC = 32
        early = sb("early", [P, T["la_cols"] + T["lx_cols"] + 4 * KD * D])
        w_la = early[:, 0:T["la_cols"]]
        la = T["la"]

        def pack(t, table, name, rows=P):
            a, b = table[name]
            return t[0:rows, a:b]

        WkvT = pack(w_la, la, "WkvT").rearrange("p (k n) -> p k n", k=KD)
        WcT = pack(w_la, la, "WcT", 64)
        Wqkv = pack(w_la, la, "Wqkv", HC)
        Wc2lT = pack(w_la, la, "Wc2lT", HC)
        W_kv = pack(w_la, la, "W_kv", 64)
        W_res = pack(w_la, la, "W_res", 64)
        gamma = pack(w_la, la, "gamma", HC)
        beta = pack(w_la, la, "beta", HC)
        cosq = pack(w_la, la, "cos")
        sinq = pack(w_la, la, "sin")
        causal = pack(w_la, la, "causal")
        bv_lx = pack(w_la, la, "bv_lx")
        mask = pack(w_la, la, "mask")
        bq_lx = pack(w_la, la, "bq_lx")
        bk_lx = pack(w_la, la, "bk_lx")
        bdmask = pack(w_la, la, "bdmask")
        gate_w = pack(w_la, la, "gate_w").rearrange("p (k e) -> p k e", k=KD)
        alpha = pack(w_la, la, "alpha")
        tri = pack(w_la, la, "tri").rearrange("p (e j) -> p e j", e=8)
        fc2_b = pack(w_la, la, "fc2_b", 8)
        region = sb("region", [P, 24576])
        cursor = [0]

        def carve(rows, *shape, start=None):
            if start is not None:
                cursor[0] = start
            size = 1
            for s in shape:
                size *= s
            a = cursor[0]
            cursor[0] += size
            assert cursor[0] <= 24576
            v = region[0:rows, a:a + size]
            if len(shape) == 2:
                v = v.rearrange("p (a b) -> p a b", a=shape[0])
            if len(shape) == 3:
                v = v.rearrange("p (a b c) -> p a b c", a=shape[0], b=shape[1])
            return v

        Wsum = carve(64, D)
        kvlatT = carve(64, N)
        s1 = carve(P, NB)
        xc = carve(P, NB, HC)
        sq = carve(P, NB, HC)
        vl = carve(P, NB)
        rl = carve(P, NB)
        chT = carve(HC, N)
        t1 = carve(P, NB, 64)
        t2 = carve(P, NB, 64)
        v_la = carve(P, NB, HC)
        qT = carve(HC, N)
        kT = carve(HC, N)
        S = carve(P, NB, P)
        r1 = carve(P, NB)
        r2 = carve(P, NB)
        PT = carve(P, NB, P)
        oT = chT
        zT = kvlatT

        NH, FD, HD = 16, 64, 16
        CH = NH * FD // P
        AUG = 2 * (HD + 1)
        lx = T["lx"]
        w_lx = early[:, T["la_cols"]:T["la_cols"] + T["lx_cols"]]
        WqT = pack(w_lx, lx, "WqT").rearrange("p (k n) -> p k n", k=KD)
        WkT = pack(w_lx, lx, "WkT").rearrange("p (k n) -> p k n", k=KD)
        WvT = pack(w_lx, lx, "WvT").rearrange("p (k n) -> p k n", k=KD)
        WoT = pack(w_lx, lx, "WoT").rearrange("p (k n) -> p k n", k=KD)
        BDk = pack(w_lx, lx, "BDk")
        BDq = pack(w_lx, lx, "BDq")
        kx = carve(P, KD, N)
        qx = kx
        kp = carve(P, NB, NH * FD)
        qp = kp.rearrange("p b n -> p (b n)").rearrange("p (c n) -> p c n", c=CH)
        v_aug = carve(P, NB, NH * (HD + 1))
        v_aug_h = v_aug.rearrange("p b (h e) -> p b h e", e=HD + 1)
        kvm = carve(P, NB, NH * (HD + 1))
        a_x = H
        den = carve(P, NB, NH)
        rden = carve(P, NB, NH)
        aT = kx

        E = 8
        fc = early[:, T["la_cols"] + T["lx_cols"]:].rearrange("p (f w k n) -> p f w k n", f=2, w=2, k=KD)
        f1, f2 = fc[:, 0], fc[:, 1]
        f1b = sb("f1b", [P, 2, KD])
        lg = carve(P, NB, E, start=0)
        gm = carve(P, NB)
        pr = carve(P, NB, E)
        gs = carve(P, NB)
        gr = carve(P, NB)
        GT = carve(P, NB * E, E)
        GE = carve(P, NB * E, E)
        rank = carve(P, NB, E)
        comb = carve(P, NB, E)
        combT = carve(E, N)
        hT = carve(P, 2 * KD, N)

        KV, GRP, DH = 8, 4, 64
        QKV = (GRP + 2) * DH
        w_qkv = carve(P, KV, KD * QKV, start=cursor[0]).rearrange("p h (k n) -> p h k n", k=KD)
        b_qkv = carve(P, KV, QKV)
        WoT1 = carve(P, KV * 2, D)
        xT_t = carve(P, KD, P)
        raw = carve(P, QKV)
        straight = carve(P, 2, (GRP + 1) * DH)
        crossed = carve(P, 2, (GRP + 1) * DH)
        qk = carve(P, 2, (GRP + 2) * DH)
        v_t = carve(P, 4, DH)
        qkT1 = carve(P, 2, 3 * P)
        m_t = carve(P, 2, GRP)
        d_t = carve(P, 2, GRP)
        rd_t = carve(P, 2, GRP)
        oT1 = carve(P, 2, 2 * P)
        late = sb("late", [P, T["late_cols"]])
        lt = T["lt"]
        cos1 = pack(late, lt, "cos").rearrange("p (a c) -> p a c", a=2)
        sin1 = pack(late, lt, "sin").rearrange("p (a c) -> p a c", a=2)
        causal1 = pack(late, lt, "causal")
        kw = pack(late, lt, "kw")
        carrier = sem("carrier")
        kws = sb("kws", [P, KV * GRP])
        probs_zone = sb("probs_zone", [P, 4 * GRP * P])
        S1 = probs_zone[:, 0:2 * GRP * P].rearrange("p (r n) -> p r n", r=2)
        PT1 = probs_zone[:, 2 * GRP * P:].rearrange("p (r n) -> p r n", r=2)

        HX, DX = 16, 16
        PAIRS, SPL = HX // 2, 64
        kspT = sb("kspT", [P, PAIRS, N], BF16)
        v_int = sb("v_int", [P, NB, D], BF16)
        ident_b = sb("ident_b", [P, P], BF16)
        w_xx = sb("w_xx", [P, T["xx_cols"]])
        xx = T["xx"]
        Wq2 = pack(w_xx, xx, "Wq").rearrange("p (k n) -> p k n", k=KD)
        w_xk, xk = probs_zone[:, 0:T["xk_cols"]], T["xk"]
        Wk2 = pack(w_xk, xk, "Wk").rearrange("p (k n) -> p k n", k=KD)
        Wv2 = pack(w_xk, xk, "Wv").rearrange("p (k n) -> p k n", k=KD)
        Wp2 = pack(w_xx, xx, "Wp").rearrange("p (k n) -> p k n", k=KD)
        bq2, bk2, bv2 = pack(w_xx, xx, "bq"), pack(w_xk, xk, "bk"), pack(w_xk, xk, "bv")
        as_bf16 = lambda v: v.bitcast(BF16)
        qspT = as_bf16(early[:, 0:PAIRS * N // 2]).rearrange("p (j n) -> p j n", j=PAIRS)
        vT2 = early[:, 0:KD * N].rearrange("p (k n) -> p k n", k=KD)
        vq = as_bf16(early[:, KD * N:KD * N * 3 // 2]).rearrange("p (k n) -> p k n", k=KD)
        o = PAIRS * N // 2
        full_t = early[:, o:o + 512]
        rest_t = early[:, o + 512:o + 1024]
        parts_t = as_bf16(early[:, o + 1024:o + 2048]).rearrange("p (i h c) -> p i h c", i=2, h=HX)
        am = sb("am", [P, 2 * HX])
        scl = sb("scl", [P, 2 * HX])
        inv = sb("inv", [P, 2 * HX])
        sq_all = sb("sq_all", [P, NB, HX])
        nsq_all = sb("nsq_all", [P, NB, HX])
        mx_t = sb("mx_t", [P, 2])
        nb_t = sb("nb_t", [P, 2])
        sums_t = sb("sums_t", [P, HX])
        rs_t = sb("rs_t", [P, HX])
        sv = sb("sv", [P, KD])
        rv = sb("rv", [P, KD])
        e_t = probs_zone[:].rearrange("p (r n) -> p r n", r=2)
        r_t = as_bf16(ctxT[:].rearrange("p k n -> p (k n)")).rearrange("p (r n) -> p r n", r=4)
        rT_t = as_bf16(early[:, o:o + N]).rearrange("p (r n) -> p r n", r=2)
        qT_t = as_bf16(early[:, o + N + 2 * D:o + 2 * N]).rearrange("p (j t) -> p j t", j=PAIRS)

        I2 = 512
        SLOT_TILES = (N + E * (P - 1)) // P
        W_gu = region[:, 0:E * KD * 2 * I2].rearrange("p (k e n) -> p k e n", k=KD, e=E)
        W_dn = region[:, E * KD * 2 * I2:E * (KD * 2 + I2 // P // 2) * I2].rearrange("p (k e n) -> p k e n", k=I2 // P, e=E)
        shared_zone = kspT[:].rearrange("p j n -> p (j n)").bitcast(F32)
        W_sh = shared_zone[:, 0:KD * 2 * I2].rearrange("p (k n) -> p k n", k=KD)
        W_sd = shared_zone[:, KD * 2 * I2:KD * 2 * I2 + I2 // P * D].rearrange("p (k n) -> p k n", k=I2 // P)
        shT = early[:, 0:I2 // P * N].rearrange("p (m n) -> p m n", m=I2 // P)
        slots_in = early[:, o:o + D]
        slots_T = early[:, o + D:o + 2 * D]
        gated = early[:, o + 2 * D:o + 4 * D]
        hid = early[:, o + 4 * D:o + 6 * D]
        hid_T = early[:, o + 6 * D:o + 8 * D]
        slots_out = early[:, o + 8 * D:o + 9 * D]
        at_ = o + 9 * D
        lg2, sel = (early[:, a:a + NB * E].rearrange("p (b e) -> p b e", b=NB) for a in (at_, at_ + NB * E))
        owner_c = early[:, at_ + 2 * NB * E:at_ + 2 * NB * E + SLOT_TILES * E].rearrange("p (t e) -> p t e", t=SLOT_TILES)
        silu_t = probs_zone[:, 0:I2]
        more2 = probs_zone[:, I2:2 * I2].rearrange("p (b j) -> p b j", j=E)
        same2 = probs_zone[:, 2 * I2:3 * I2].rearrange("p (b j) -> p b j", j=E)
        rank2 = probs_zone[:, 3 * I2:3 * I2 + NB * E].rearrange("p (b e) -> p b e", b=NB)
        xr = XB
        yg = ctxT[:].rearrange("p k (b n) -> p (k b) n", n=D)
        top2 = sb("top2", [P, NB])
        score2 = sb("score2", [P, NB])
        scan_a = sb("scan_a", [P, NB, E])
        scan_b = sb("scan_b", [P, NB, E])
        tiles_e = sb("tiles_e", [P, 3, E])
        pos = sb("pos", [P, NB, E])
        slot_f = sb("slot_f", [P, NB])
        slot_i = sb("slot_i", [P, NB], I32)
        owner_f = sb("owner_f", [P, SLOT_TILES])
        owner_i = sb("owner_i", [P, SLOT_TILES], I32)
        router = pack(late, lt, "router").rearrange("p (k e) -> p k e", k=KD)
        tri2 = pack(late, lt, "tri").rearrange("p (e j) -> p e j", e=E)
        earlier = pack(late, lt, "earlier")
        ones = pack(late, lt, "ones")
        tile_no = pack(late, lt, "tile_no")
        x_slots = nc.dram_tensor("x_slots", [SLOT_TILES * P, D], F32, kind="Internal").ap()
        y_slots = nc.dram_tensor("y_slots", [SLOT_TILES * P, D], F32, kind="Internal").ap()

        s_w = {n: sem("s_" + n) for n in ("w_la", "w_lx", "xT", "x", "ctxT", "ident", "bias0", "late", "w_qkv", "WoT1", "w_xx", "w_gu", "w_dn", "w_sh")}
        s_out = sem("s_out")
        s_dve = sem("dve_step")
        s_act = sem("act_step")
        s_pool = sem("pool_step")
        x_ready = sem("x_ready")
        xb_ready = sem("xb_ready")
        var_ready = sem("var_ready")
        rstd_ready = sem("rstd_ready")
        wsum_ready = sem("wsum_ready")
        fc_loaded = [sem(f"fc_loaded{w}") for w in range(2)]
        s_sig = {}

        def signal(name):
            if name not in s_sig:
                s_sig[name] = sem(name)
            return s_sig[name]

        NCH = NB // 2
        rope1, neg_max1, exps1 = sem("rope1"), sem("neg_max1"), sem("exps1")
        probs1, turned1, tile_features = sem("probs1"), sem("turned1"), sem("tile_features")
        cmp_ready = sem("cmp_ready")

        def rank_experts(dve, then, score, more, same, before_, rank_, nth):
            for b in range(NB):
                of_j = score[:, b, :].unsqueeze(1).to_broadcast([P, E, E])
                of_e = score[:, b, :].unsqueeze(2).to_broadcast([P, E, E])
                dve.tensor_tensor(more[:, b * E:b * E + E, :], of_j, of_e, ALU.is_gt).then_inc(cmp_ready, 1)
                dve.tensor_tensor(same[:, b * E:b * E + E, :], of_j, of_e, ALU.is_equal).then_inc(cmp_ready, 1)
            dve.wait_ge(cmp_ready, 2 * NB * (nth + 1))
            same4 = same.rearrange("p (b e) j -> p b e j", b=NB)
            then(dve.tensor_tensor(same4, same4, before_.unsqueeze(1).to_broadcast([P, NB, E, E]), ALU.mult))
            then(dve.tensor_tensor(more, more, same, ALU.add))
            then(dve.tensor_reduce(rank_.rearrange("p b e -> p (b e)"), more, AX, ALU.add))

        w_scaled, raw_ready, recip_ready = sem("w_scaled"), sem("raw_ready"), sem("recip_ready")
        B_QKV, B_TR, B_S, B_PT, B_O, B_Y = 0, 1, 2, 4, 5, 6
        base = {}

        def head_steps(eng, step, tail):
            for h in range(KV):
                step(0, h, lambda back, h=h: h >= back, True)
            with eng.Fori(1, NB) as trip:
                for h in range(KV):
                    step(trip, h, lambda back: True, True)
            for h in range(tail):
                step(NB, h, lambda back, h=h: h < back, False)

        def grouped_attention_pe(pe):
            for k in range(8):
                base[k] = banks.n[k]
            pe.wait_ge(s_w["WoT1"], 16)
            pe.wait_ge(w_scaled, KV + 1)

            def step(trip, h, has, fresh):
                s = KV * trip + h
                if fresh:
                    if h == 0:
                        pe.wait_ge(tile_features, trip + 1)
                    pe.wait_ge(banks.free[B_QKV], base[B_QKV] + s)
                    for k in range(KD):
                        ins = pe.matmul(psum[:, B_QKV, 0:QKV], xT_t[:, k, :], w_qkv[:, h, k, :], start=(k == 0), stop=(k == KD - 1))
                    ins.then_inc(banks.full[B_QKV], 1)
                if has(1):
                    pe.wait_ge(rope1, 2 * s)
                    pe.wait_ge(banks.free[B_TR], base[B_TR] + s - 1)
                    for j in range(3):
                        ins = pe.transpose(psum[:, B_TR, j * P:j * P + P], qk[:, (h - 1) % 2, j * P:j * P + P], ident[:])
                    ins.then_inc(banks.full[B_TR], 1)
                if has(3):
                    pe.wait_ge(probs1, s - 2)
                    pe.wait_ge(banks.free[B_PT], base[B_PT] + s - 3)
                    for g in range(GRP):
                        ins = pe.transpose(psum[:, B_PT, g * P:g * P + P], S1[:, (h - 3) % 2, g * P:g * P + P], ident[:])
                    ins.then_inc(banks.full[B_PT], 1)
                if has(4):
                    hh = (h - 4) % KV
                    if hh == 0:
                        pe.wait_ge(banks.free[B_Y], base[B_Y] + trip)
                    pe.wait_ge(banks.free[B_O], base[B_O] + s - 3)
                    for j in range(2):
                        ins = pe.matmul(psum[:, B_Y, 0:D], oT1[:, (h - 4) % 2, j * P:j * P + P], WoT1[:, 2 * hh + j, :],
                                        start=(hh == 0 and j == 0), stop=(hh == KV - 1 and j == 1))
                    if hh == KV - 1:
                        ins.then_inc(banks.full[B_Y], 1)
                if has(1):
                    pe.wait_ge(banks.free[B_TR], base[B_TR] + s)
                    for par in range(2):
                        pe.wait_ge(banks.free[B_S + par], base[B_S + par] + s - 1)
                        r = slice(par * DH, par * DH + DH)
                        for j in range(2):
                            ins = pe.matmul(psum[:, B_S + par, j * P:j * P + P], qkT1[r, (h - 1) % 2, j * P:j * P + P],
                                            qkT1[r, (h - 1) % 2, 2 * P:3 * P], start=True, stop=True)
                        ins.then_inc(banks.full[B_S + par], 1)
                if has(3):
                    pe.wait_ge(banks.free[B_PT], base[B_PT] + s - 2)
                    pe.wait_ge(banks.free[B_O], base[B_O] + s - 3)
                    for par in range(2):
                        ins = pe.matmul(psum[par * DH:par * DH + DH, B_O, 0:2 * P], v_t[:, (h - 3) % 4, :],
                                        PT1[:, (h - 3) % 2, :].rearrange("p (j r t) -> p r j t", j=2, r=2)[:, par],
                                        start=True, stop=True)
                    ins.then_inc(banks.full[B_O], 1)

            head_steps(pe, step, 4)
            for k in range(6):
                banks.n[k] += NB * KV
            banks.n[B_Y] += NB
            banks.next = 0

        def grouped_attention_act(act):
            def step(trip, h, has, fresh):
                s = KV * trip + h
                if has(1):
                    act.wait_ge(banks.full[B_TR], base[B_TR] + s)
                    act.activation(qkT1[:, (h - 1) % 2, :], psum[:, B_TR, 0:3 * P], ACT.Copy).then_inc(banks.free[B_TR], 1)
                if has(3):
                    act.wait_ge(banks.full[B_PT], base[B_PT] + s - 2)
                    act.activation(PT1[:, (h - 3) % 2, :], psum[:, B_PT, :], ACT.Copy).then_inc(banks.free[B_PT], 1)
                    act.wait_ge(banks.full[B_O], base[B_O] + s - 2)
                    act.activation(oT1[:, (h - 3) % 2, :], psum[:, B_O, 0:2 * P], ACT.Copy).then_inc(banks.free[B_O], 1)
                if has(1):
                    act.wait_ge(neg_max1, s)
                    for g in range(GRP):
                        sl = S1[:, (h - 1) % 2, g * P:g * P + P]
                        ins = act.activation(sl, sl, ACT.Exp, bias=m_t[:, (h - 1) % 2, g:g + 1],
                                             accum_out=d_t[:, (h - 1) % 2, g:g + 1])
                    ins.then_inc(exps1, 1)

            head_steps(act, step, 3)

        def grouped_attention_dve(dve, then):
            def output(trip, b):
                dve.wait_ge(banks.full[B_Y], base[B_Y] + trip)
                dve.tensor_tensor(H[:, b, :].rearrange("p b n -> p (b n)"), psum[:, B_Y, 0:D],
                                  XB[:, b, :].rearrange("p b n -> p (b n)"), ALU.add).then_inc(banks.free[B_Y], 1)

            def step(trip, h, has, fresh):
                s = KV * trip + h
                if isinstance(trip, int) and trip == 0 and h == 0:
                    dve.tensor_scalar(xT_t, XT[:, :, 0:P], 1.0, None, ALU.mult).then_inc(tile_features, 1)
                if fresh:
                    dve.wait_ge(banks.full[B_QKV], base[B_QKV] + s + 1)
                    if has(1):
                        dve.wait_ge(turned1, 2 * s)
                    n = (GRP + 1) * DH
                    then(dve.tensor_tensor(raw[:, 0:n], psum[:, B_QKV, 0:n], b_qkv[:, h, 0:n], ALU.add), h, 1, trip)
                    dve.tensor_tensor(v_t[:, h % 4, :], psum[:, B_QKV, n:n + DH], b_qkv[:, h, n:n + DH], ALU.add)\
                       .then_inc(banks.free[B_QKV], 1)
                    rawv = raw[:, 0:n].rearrange("p (g a c) -> p g a c", g=GRP + 1, a=2)
                    if has(2):
                        dve.wait_ge(rope1, 2 * s - 2)
                    straight_v = straight[:, h % 2, :].rearrange("p (g a c) -> p g a c", g=GRP + 1, a=2)
                    crossed_v = crossed[:, h % 2, :].rearrange("p (g a c) -> p g a c", g=GRP + 1, a=2)
                    dve.tensor_tensor(straight_v, rawv, cos1.unsqueeze(1).to_broadcast([P, GRP + 1, 2, DH // 2]), ALU.mult)\
                       .then_inc(turned1, 1)
                    dve.tensor_tensor(crossed_v, rawv[:, :, ::-1, :], sin1.unsqueeze(1).to_broadcast([P, GRP + 1, 2, DH // 2]),
                                      ALU.mult).then_inc(turned1, 1)
                if has(1):
                    if has(3):
                        dve.wait_ge(banks.full[B_PT], base[B_PT] + s - 2)
                    for par in range(2):
                        dve.wait_ge(banks.full[B_S + par], base[B_S + par] + s)
                        dve.sem_inc(carrier, 1)
                        for j in range(2):
                            g = 2 * j + par
                            ins = dve.tensor_tensor_reduce(S1[:, (h - 1) % 2, g * P:g * P + P], psum[:, B_S + par, j * P:j * P + P],
                                                           causal1, 1.0, -3e38, ALU.add, ALU.max, m_t[:, (h - 1) % 2, g:g + 1])
                        ins.then_inc(banks.free[B_S + par], 1)
                    for par in range(2):
                        dve.wait_ge(banks.free[B_S + par], base[B_S + par] + s)
                    dve.tensor_scalar(m_t[:, (h - 1) % 2, :], m_t[:, (h - 1) % 2, :], -1.0, None, ALU.mult).then_inc(neg_max1, 1)
                if has(2):
                    dve.wait_ge(exps1, s - 1)
                    then(dve.reciprocal(rd_t[:, (h - 2) % 2, :], d_t[:, (h - 2) % 2, :]), h, 0, trip)
                    for g in range(GRP):
                        sl = S1[:, (h - 2) % 2, g * P:g * P + P]
                        ins = dve.tensor_scalar(sl, sl, rd_t[:, (h - 2) % 2, g:g + 1], None, ALU.mult)
                    ins.then_inc(probs1, 1)
                if fresh and h == KV - 1:
                    src = XT_next[:, :, 0:P] if isinstance(trip, int) else XT_next[:, :, bass.ds(trip * P, P)]
                    dve.tensor_scalar(xT_t, src, 1.0, None, ALU.mult).then_inc(tile_features, 1)
                if h == 3 and not isinstance(trip, int):
                    output(trip, bass.ds(trip - 1, 1))

            dve.wait_ge(xb_ready, 3 * NCH)
            dve.wait_ge(signal("spare_ready"), 1)
            head_steps(dve, step, 3)
            output(NB, slice(NB - 1, NB))
            dve.wait_ge(banks.free[B_Y], base[B_Y] + NB)

        def grouped_attention_pool(pool):
            def step(trip, h, has, fresh):
                s = KV * trip + h
                if fresh:
                    pool.wait_ge(turned1, 2 * s + 2)
                    if has(2):
                        pool.wait_ge(banks.full[B_TR], base[B_TR] + s - 1)
                    n = (GRP + 1) * DH
                    pool.tensor_tensor(qk[:, h % 2, 0:n], straight[:, h % 2, :], crossed[:, h % 2, :], ALU.add)\
                        .then_inc(rope1, 1)
                    pool.tensor_tensor(qk[:, h % 2, n:n + DH], straight[:, h % 2, n - DH:n], crossed[:, h % 2, n - DH:n],
                                       ALU.add).then_inc(rope1, 1)

            head_steps(pool, step, 0)

        MAGIC = 1.5 * 2.0 ** 23
        LN255 = 5.541263545158426
        stats_ready = sem("quant_step")
        parts_ready = sem("parts_ready")
        vq_ready, wp_ready, qs_ready = sem("vq_ready"), sem("wp_ready"), sem("qs_ready")
        v_done = sem("vT_ready")

        def quantise_rows(dve, count, key, bias, c, query):
            n = count[0]

            def then(ins):
                count[0] += 1
                ins.then_inc(stats_ready, 1)
                dve.wait_ge(stats_ready, count[0])

            hv = lambda v: v.rearrange("p (i h c) -> p i h c", i=2, h=HX)
            per_head = lambda v: v.rearrange("p (i h) -> p i h", i=2).unsqueeze(3).to_broadcast([P, 2, HX, DX])
            dve.wait_ge(*filled(key))
            dve.tensor_tensor(full_t.rearrange("p (i n) -> p i n", i=2), at(key).rearrange("p (i n) -> p i n", i=2),
                              bias.unsqueeze(1).to_broadcast([P, 2, D]), ALU.add).then_inc(free_of(key), 1)
            dve.wait_ge(*read(key))
            then(dve.tensor_reduce(am[:].rearrange("p (i h) -> p i h", i=2), hv(full_t), AX, ALU.max, apply_absolute_value=True))
            factor = DX ** -0.5 if query else 1.0
            then(dve.tensor_scalar(scl[:], am[:], 1.0 / 127.0, 1e-8 / factor, ALU.mult, ALU.max))
            then(dve.reciprocal(inv[:], scl[:]))
            then(dve.tensor_tensor(hv(full_t), hv(full_t), per_head(inv[:]), ALU.mult))
            then(dve.tensor_scalar(full_t, full_t, MAGIC, MAGIC, ALU.add, ALU.subtract))
            if query:
                sl = slice(2 * c, 2 * c + 2)
                then(dve.tensor_scalar(sq_all[:, sl, :].rearrange("p i h -> p (i h)"), scl[:], factor, None, ALU.mult))
                then(dve.tensor_scalar(nsq_all[:, sl, :].rearrange("p i h -> p (i h)"), scl[:], -factor, None, ALU.mult))
                if c:
                    dve.wait_ge(*filled(("qspT", 2 * c - 1)))
                for i in range(2):
                    dve.tensor_scalar(parts_t[:, i, :, 0:3 * DX].rearrange("p h (r c) -> p h r c", r=3),
                                      hv(full_t)[:, i].unsqueeze(2).to_broadcast([P, HX, 3, DX]), -127.0, 127.0,
                                      ALU.max, ALU.min).then_inc(parts_ready, 1)
                dve.wait_ge(parts_ready, 2 * (NCH + c + 1))
                return
            then(dve.tensor_scalar(full_t, full_t, -127.0, 127.0, ALU.max, ALU.min))
            then(dve.tensor_tensor(hv(full_t), hv(full_t), per_head(scl[:]), ALU.mult))
            if c:
                dve.wait_ge(*filled(("kspT", 2 * c - 1)))
            hi, mid, lo = (parts_t[:, :, :, r * DX:(r + 1) * DX] for r in range(3))
            then(dve.tensor_copy(hi, hv(full_t)))
            then(dve.tensor_tensor(hv(rest_t), hv(full_t), hi, ALU.subtract))
            then(dve.tensor_copy(mid, hv(rest_t)))
            then(dve.tensor_tensor(hv(full_t), hv(rest_t), mid, ALU.subtract))
            dve.tensor_copy(lo, hv(full_t)).then_inc(parts_ready, 2)
            dve.wait_ge(parts_ready, 2 * (c + 1))

        def turn_parts(pe, name, nth):
            for b in range(NB):
                claim_(pe, (name, b))
                pe.wait_ge(parts_ready, (2 * (b // 2) + (2 if name == "kspT" else b % 2 + 1)) + nth)
                for j in range(PAIRS):
                    ins = pe.transpose(at((name, b)).bitcast(BF16)[:, j * P:j * P + P],
                                       parts_t[:, b % 2, 2 * j:2 * j + 2, :].rearrange("p h c -> p (h c)"), ident_b[:])
                ins.then_inc(full_of((name, b)), 1)
                yield b

        def claim_(pe, key, count=1):
            for se, v in take(key, count):
                pe.wait_ge(se, v)

        def rows_of(pe, key, src, w):
            claim_(pe, key)
            c = key[1]
            for i in range(2):
                for k in range(KD):
                    ins = pe.matmul(at(key)[:, i * D:i * D + D], src[:, k, (2 * c + i) * P:(2 * c + i + 1) * P], w[:, k, :],
                                    start=(k == 0), stop=(k == KD - 1))
            ins.then_inc(full_of(key), 1)

        def context_pe(pe):
            pe.wait_ge(s_w["w_xx"], 32)
            pe.wait_ge(signal("ident_b_ready"), 1)
            for c in range(NCH):
                rows_of(pe, ("k2", c), ctxT, Wk2)
            turned = turn_parts(pe, "kspT", 0)
            for _ in turned:
                pass
            for m in range(KD):
                for n in range(G):
                    claim_(pe, ("v2", m, n))
                    for k in range(KD):
                        ins = pe.matmul(at(("v2", m, n)), Wv2[:, k, m * P:m * P + P], ctxT[:, k, n * 512:n * 512 + 512],
                                        start=(k == 0), stop=(k == KD - 1))
                    ins.then_inc(full_of(("v2", m, n)), 1)
            pe.wait_ge(vq_ready, KD)
            for q in range(2):
                claim_(pe, ("v_int", q))
                for i in range(4):
                    for k in range(KD):
                        ins = pe.transpose(at(("v_int", q)).bitcast(BF16)[:, (i * KD + k) * P:(i * KD + k + 1) * P],
                                           vq[:, k, (4 * q + i) * P:(4 * q + i + 1) * P], ident_b[:])
                ins.then_inc(full_of(("v_int", q)), 1)

        def context_act(act):
            for b in range(NB):
                act.wait_ge(*filled(("kspT", b)))
                act.activation(kspT[:, :, b * P:b * P + P], at(("kspT", b)).bitcast(BF16).rearrange("p (j t) -> p j t", j=PAIRS),
                               ACT.Copy).then_inc(free_of(("kspT", b)), 1)
            for m in range(KD):
                for n in range(G):
                    act.wait_ge(*filled(("v2", m, n)))
                    act.activation(vT2[:, m, n * 512:n * 512 + 512], at(("v2", m, n)), ACT.Identity, bias=bv2[:, m:m + 1])\
                       .then_inc(free_of(("v2", m, n)), 1)
            for q in range(2):
                act.wait_ge(*filled(("v_int", q)))
                act.activation(v_int[:, 4 * q:4 * q + 4, :].rearrange("p b n -> p (b n)"), at(("v_int", q)).bitcast(BF16),
                               ACT.Copy).then_inc(free_of(("v_int", q)), 1)

        def context_dve(dve, count):
            def then(ins):
                count[0] += 1
                ins.then_inc(stats_ready, 1)
                dve.wait_ge(stats_ready, count[0])

            dve.wait_ge(s_w["w_xx"], 32)
            then(dve.memset(parts_t, 0.0))
            dve.tensor_copy(ident_b[:], ident[:]).then_inc(signal("ident_b_ready"), 1)
            for c in range(NCH):
                quantise_rows(dve, count, ("k2", c), bk2, c, False)
            for m in range(KD):
                for n in range(G):
                    dve.wait_ge(*read(("v2", m, n)))
            then(dve.tensor_reduce(sv[:], vT2, AX, ALU.max, apply_absolute_value=True))
            then(dve.tensor_scalar(sv[:], sv[:], 1.0 / 127.0, 1e-8, ALU.mult, ALU.max))
            then(dve.reciprocal(rv[:], sv[:]))
            for k in range(KD):
                then(dve.tensor_scalar(vT2[:, k, :], vT2[:, k, :], rv[:, k:k + 1], MAGIC, ALU.mult, ALU.add))
                then(dve.tensor_scalar(vT2[:, k, :], vT2[:, k, :], MAGIC, -127.0, ALU.subtract, ALU.max))
                dve.tensor_scalar(vq[:, k, :], vT2[:, k, :], 127.0, None, ALU.min).then_inc(vq_ready, 1)
                dve.tensor_scalar(Wp2[:, k, :], Wp2[:, k, :], sv[:, k:k + 1], None, ALU.mult).then_inc(wp_ready, 1)

        def queries_pe(pe):
            for c in range(NCH):
                pe.wait_ge(*read(("xt", 3, c)))
                rows_of(pe, ("q2", c), XT, Wq2)
            for _ in turn_parts(pe, "qspT", 2 * NCH):
                pass

        def queries_act(act):
            for q in range(2):
                act.wait_ge(*read(("v_int", q)))
            for b in range(NB):
                act.wait_ge(*filled(("qspT", b)))
                act.activation(qspT[:, :, b * P:b * P + P], at(("qspT", b)).bitcast(BF16).rearrange("p (j t) -> p j t", j=PAIRS),
                               ACT.Copy).then_inc(free_of(("qspT", b)), 1)

        LT, LP = 3, 4
        OUT_STEPS = LP + 1, HX // 2 + LP + 1
        XS, XO = 0, 6
        exps2, rounded2, bias2, tile_queries, a_ready = (sem("exps2"), sem("rounded2"), sem("bias2"),
                                                         sem("tile_queries"), sem("a_ready"))
        base2 = {}

        def turn_use(trip, h):
            return HX // 2 * trip + h // 2 + 1

        def scale_of(scales, trip, h):
            return scales[:, slice(0, 1) if isinstance(trip, int) else bass.ds(trip, 1), h]

        def before(trip, h, back):
            h -= back
            return (trip, h) if h >= 0 else (trip - 1, h + HX)

        def tile_steps(eng, step, last):
            for h in range(HX):
                step(0, h, lambda back, h=h: h >= back, True)
            with eng.Fori(1, NB) as trip:
                for h in range(HX):
                    step(trip, h, lambda back: True, True)
            for h in range(last):
                step(NB, h, lambda back, h=h: h < back, False)

        def cross_pe(pe):
            for k in range(8):
                base2[k] = banks.n[k]
            pe.wait_ge(wp_ready, KD)

            def step(trip, h, has, fresh):
                s = HX * trip + h
                if fresh:
                    if h % (HX // 2) == 0:
                        pe.wait_ge(tile_queries, 2 * trip + 1 + h // (HX // 2))
                    k = XS + 2 * (h % 2)
                    pe.wait_ge(banks.free[k], base2[k] + HX // 2 * trip + h // 2)
                    r = slice(h % 2 * SPL, h % 2 * SPL + SPL)
                    for n in range(G):
                        ins = pe.matmul(psum[:, k + n, :], qT_t[r, h // 2, :], kspT[r, h // 2, n * 512:n * 512 + 512],
                                        start=True, stop=True)
                    ins.then_inc(banks.full[k], 1)
                if has(LP):
                    t, hh = before(trip, h, LP)
                    k = 4 + hh % 2
                    ko = XO + hh // (HX // 2)
                    pe.wait_ge(banks.free[k], base2[k] + turn_use(t, hh))
                    if hh % (HX // 2) == 0:
                        pe.wait_ge(banks.free[ko], base2[ko] + t)
                    for c in range(NB):
                        ins = pe.matmul(psum[:, ko, hh * DX:hh * DX + DX], rT_t[:, hh % 2, c * P:c * P + P],
                                        v_int[:, c, hh * DX:hh * DX + DX], start=(c == 0), stop=(c == NB - 1))
                    if hh % (HX // 2) == HX // 2 - 1:
                        ins.then_inc(banks.full[ko], 1)
                if has(LT):
                    t, hh = before(trip, h, LT)
                    k = 4 + hh % 2
                    pe.wait_ge(rounded2, s - LT + 1)
                    pe.wait_ge(banks.free[k], base2[k] + turn_use(t, hh) - 1)
                    for c in range(NB):
                        ins = pe.transpose(psum[:, k, :].bitcast(BF16)[:, c * P:c * P + P], r_t[:, hh % 4, c * P:c * P + P], ident_b[:])
                    ins.then_inc(banks.full[k], 1)

            tile_steps(pe, step, LP)
            for k in (0, 2, 4, 5):
                banks.n[k] += NB * HX // 2
            for k in (6, 7):
                banks.n[k] += NB
            banks.next = 0
            for c in range(NCH + 1):
                if c < NCH:
                    claim_(pe, ("a2T", c))
                    pe.wait_ge(a_ready, 2 * (2 * c + 2))
                    for k in range(KD):
                        for i in range(2):
                            ins = pe.transpose(at(("a2T", c))[:, (2 * k + i) * P:(2 * k + i + 1) * P],
                                               H[:, 2 * c + i, k * P:k * P + P], ident[:])
                    ins.then_inc(full_of(("a2T", c)), 1)
                if c:
                    pe.wait_ge(*read(("a2T", c - 1)))
                    rows_of(pe, ("y_cross", c - 1), XT, Wp2)

        def cross_act(act):
            def step(trip, h, has, fresh):
                s = HX * trip + h
                if has(LT) and h % 4 != 0:
                    turned_copy(act, trip, h)
                if fresh:
                    act.wait_ge(bias2, s + 1)
                    if has(2):
                        act.wait_ge(rounded2, s - 1)
                    k = XS + 2 * (h % 2)
                    act.sem_inc(carrier, 1)
                    act.activation(e_t[:, h % 2, :], psum[:, k:k + 2, :].rearrange("p k n -> p (k n)"), ACT.Exp,
                                   bias=nb_t[:, h % 2:h % 2 + 1], scale=scale_of(sq_all, trip, h),
                                   accum_out=sums_t[:, h:h + 1]).then_inc(banks.free[k], 1)

            tile_steps(act, step, LT)
            for c in range(NCH):
                act.wait_ge(*filled(("a2T", c)))
                act.activation(XT[:, :, 2 * c * P:2 * c * P + 2 * P], at(("a2T", c)).rearrange("p (k n) -> p k n", k=KD),
                               ACT.Copy).then_inc(free_of(("a2T", c)), 1)

        def turned_copy(eng, trip, h):
            t, hh = before(trip, h, LT)
            k = 4 + hh % 2
            eng.wait_ge(banks.full[k], base2[k] + turn_use(t, hh))
            src, dst = psum[:, k, :].bitcast(BF16), rT_t[:, hh % 2, :]
            if eng is nc.scalar or eng.engine == nc.scalar.engine:
                eng.activation(dst, src, ACT.Copy).then_inc(banks.free[k], 1)
            else:
                eng.tensor_scalar(dst, src, 1.0, None, ALU.mult).then_inc(banks.free[k], 1)

        def cross_dve(dve):
            next_qspT = qspT.rearrange("p j n -> p (j n)")[:, P:P + (PAIRS - 1) * N].rearrange("p (j n) -> p j n", n=N)

            def copy_queries(half, src):
                js = slice(half * PAIRS // 2, (half + 1) * PAIRS // 2)
                dve.tensor_scalar(qT_t[:, js], src[:, js], 1.0, None, ALU.mult).then_inc(tile_queries, 1)

            def output_half(t, half):
                ko = XO + half
                hs = slice(half * HX // 2, (half + 1) * HX // 2)
                dve.wait_ge(banks.full[ko], base2[ko] + t + 1)
                dve.reciprocal(rs_t[:, hs], sums_t[:, hs]).then_inc(qs_ready, 1)
                dve.wait_ge(qs_ready, 2 * t + half + 1)
                b = slice(t, t + 1) if isinstance(t, int) else bass.ds(t, 1)
                dve.tensor_tensor(H[:, b, half * P:half * P + P].rearrange("p b (h c) -> p (b h) c", c=DX),
                                  psum[:, ko, half * P:half * P + P].rearrange("p (h c) -> p h c", c=DX),
                                  rs_t[:, hs].unsqueeze(2).to_broadcast([P, HX // 2, DX]), ALU.mult).then_inc(banks.free[ko], 1)
                dve.wait_ge(banks.free[ko], base2[ko] + t + 1)
                dve.sem_inc(a_ready, 1)

            def step(trip, h, has, fresh):
                s = HX * trip + h
                first_tile = isinstance(trip, int) and trip == 0
                if first_tile and h == 0:
                    copy_queries(0, qspT[:, :, 0:P])
                    copy_queries(1, qspT[:, :, 0:P])
                if fresh and h == 2 and not first_tile:
                    copy_queries(1, qspT[:, :, bass.ds(trip * P, P)])
                if fresh and h == 10:
                    copy_queries(0, next_qspT[:, :, 0:P] if first_tile else next_qspT[:, :, bass.ds(trip * P, P)])
                if fresh:
                    k = XS + 2 * (h % 2)
                    dve.wait_ge(banks.full[k], base2[k] + HX // 2 * trip + h // 2 + 1)
                    dve.tensor_reduce(mx_t[:, h % 2:h % 2 + 1], psum[:, k:k + 2, :].rearrange("p k n -> p (k n)"), AX, ALU.max)\
                       .then_inc(maxed2, 1)
                    dve.wait_ge(maxed2, s + 1)
                    dve.tensor_scalar(nb_t[:, h % 2:h % 2 + 1], mx_t[:, h % 2:h % 2 + 1], scale_of(nsq_all, trip, h), LN255,
                                      ALU.mult, ALU.add).then_inc(bias2, 1)
                if has(1):
                    t, hh = before(trip, h, 1)
                    if has(5) if fresh else True:
                        t5, h5 = before(trip, h, 5)
                        dve.wait_ge(banks.full[4 + h5 % 2], base2[4 + h5 % 2] + turn_use(t5, h5))
                    k = XS + 2 * (hh % 2)
                    dve.wait_ge(banks.free[k], base2[k] + HX // 2 * t + hh // 2 + 1)
                    dve.tensor_scalar(r_t[:, hh % 4, :], e_t[:, hh % 2, :], MAGIC, MAGIC, ALU.add, ALU.subtract)\
                       .then_inc(rounded2, 1)
                if has(LT) and h % 4 == 0:
                    turned_copy(dve, trip, h)
                if h == OUT_STEPS[1]:
                    output_half(trip, 0)
                if h == OUT_STEPS[0] and not first_tile:
                    output_half(trip - 1, 1)

            tile_steps(dve, step, OUT_STEPS[0] + 1)
            dve.wait_ge(xb_ready, 4 * NCH)
            for c in range(NCH):
                dve.wait_ge(*filled(("y_cross", c)))
                dve.tensor_tensor(H[:, 2 * c:2 * c + 2, :].rearrange("p b n -> p (b n)"), at(("y_cross", c)),
                                  XB[:, 2 * c:2 * c + 2, :].rearrange("p b n -> p (b n)"), ALU.add)\
                   .then_inc(free_of(("y_cross", c)), 1)
            for c in range(NCH):
                dve.wait_ge(*read(("y_cross", c)))

        maxed2 = sem("maxed2")

        Z_X, Z_G, Z_U, Z_H, Z_Y = range(5)
        base3 = {}
        M2 = I2 // P
        scattered, gathered, slots_loaded, slots_stored = (sem("scattered"), sem("gathered"), sem("slots_loaded"),
                                                           sem("slots_stored"))
        sel_ready, score_ready, xr_ready, gated_ready, sh_ready, silu_ready = (
            sem("sel_ready"), sem("score_ready"), sem("xr_ready"), sem("gated_ready"), sem("sh_ready"), sem("silu_ready"))
        slot_ready, owner_ready, hid_ready = sem("slot_ready"), sem("owner_ready"), sem("hid_ready")

        def slot_steps(eng, step):
            step(0, True, False)
            with eng.Fori(1, SLOT_TILES) as t:
                step(t, True, True)
            step(SLOT_TILES, False, True)

        def experts_pe(pe):
            pe.wait_ge(s_w["late"], 16)
            claim_(pe, "router")
            for b in range(NB):
                pe.wait_ge(*read(("xt", 4, b // 2)))
                for k in range(KD):
                    ins = pe.matmul(at("router")[:, b * E:b * E + E], XT[:, k, b * P:b * P + P], router[:, k, :],
                                    start=(k == 0), stop=(k == KD - 1))
            ins.then_inc(full_of("router"), 1)
            pe.wait_ge(s_w["w_sh"], 32)
            for n in range(G):
                for m in range(M2):
                    for part in range(2):
                        key = ("sh", part, m, n)
                        claim_(pe, key)
                        for k in range(KD):
                            ins = pe.matmul(at(key), W_sh[:, k, part * I2 + m * P:part * I2 + m * P + P],
                                            XT[:, k, n * 512:n * 512 + 512], start=(k == 0), stop=(k == KD - 1))
                        ins.then_inc(full_of(key), 1)
                if n == 0:
                    claim_(pe, "pos")
                    pe.wait_ge(sel_ready, 1)
                    flat = lambda v: v.rearrange("p b e -> p (b e)")
                    pe.matmul(at("pos")[:, 0:NB * E], earlier, flat(sel[:]), start=True, stop=False)
                    pe.matmul(at("pos")[:, 0:NB * E], ones, flat(scan_a[:]), start=False, stop=True)
                    pe.matmul(at("pos")[:, NB * E:(NB + 1) * E], ones, scan_b[:, NB - 1, :], start=True, stop=True)\
                      .then_inc(full_of("pos"), 1)
            for c in range(NCH):
                claim_(pe, ("ysh", c))
                if c % 2 == 0:
                    pe.wait_ge(sh_ready, M2 * (c // 2 + 1))
                for i in range(2):
                    b = 2 * c + i
                    for m in range(M2):
                        ins = pe.matmul(at(("ysh", c))[:, i * D:i * D + D], shT[:, m, b * P:b * P + P], W_sd[:, m, :],
                                        start=(m == 0), stop=(m == M2 - 1))
                ins.then_inc(full_of(("ysh", c)), 1)
            for k in range(8):
                base3[k] = banks.n[k]
            pe.wait_ge(s_w["w_gu"], 16)
            pe.wait_ge(s_w["w_dn"], 16)
            pe.wait_ge(owner_ready, 1)

            def turn_slots(t):
                pe.wait_ge(banks.free[Z_X], base3[Z_X] + t)
                pe.wait_ge(slots_loaded, 16 * t + 16)
                for k in range(KD):
                    ins = pe.transpose(psum[:, Z_X, k * P:k * P + P], slots_in[:, k * P:k * P + P], ident[:])
                ins.then_inc(banks.full[Z_X], 1)

            turn_slots(0)

            def owner_of(t):
                at_ = slice(t, t + 1) if isinstance(t, int) else bass.ds(t, 1)
                return pe.value_load(owner_i[0:1, at_], min_val=0, max_val=E - 1)

            def step(t, now, prev):
                if prev:
                    pe.wait_ge(hid_ready, t)
                    pe.wait_ge(banks.free[Z_H], base3[Z_H] + t - 1)
                    for m in range(M2):
                        ins = pe.transpose(psum[:, Z_H, m * P:m * P + P], hid[:, m * P:m * P + P], ident[:])
                    ins.then_inc(banks.full[Z_H], 1)
                if now:
                    e = owner_of(t)
                    pe.wait_ge(banks.free[Z_X], base3[Z_X] + t + 1)
                    for part, k_ in ((0, Z_G), (1, Z_U)):
                        pe.wait_ge(banks.free[k_], base3[k_] + t)
                        for k in range(KD):
                            ins = pe.matmul(psum[:, k_, :], slots_T[:, k * P:k * P + P],
                                            W_gu[:, k, bass.ds(e, 1), part * I2:part * I2 + I2].rearrange("p e n -> p (e n)"),
                                            start=(k == 0), stop=(k == KD - 1))
                        ins.then_inc(banks.full[k_], 1)
                    if not isinstance(t, int) or t + 1 < SLOT_TILES:
                        turn_next(t)
                if prev:
                    e = owner_of(t - 1)
                    pe.wait_ge(banks.free[Z_H], base3[Z_H] + t)
                    pe.wait_ge(banks.free[Z_Y], base3[Z_Y] + t - 1)
                    for m in range(M2):
                        ins = pe.matmul(psum[:, Z_Y, 0:D], hid_T[:, m * P:m * P + P],
                                        W_dn[:, m, bass.ds(e, 1), :].rearrange("p e n -> p (e n)"),
                                        start=(m == 0), stop=(m == M2 - 1))
                    ins.then_inc(banks.full[Z_Y], 1)

            def turn_next(t):
                turn_slots(t + 1)

            slot_steps(pe, step)
            for k in (Z_G, Z_U, Z_H, Z_Y):
                banks.n[k] += SLOT_TILES
            banks.n[Z_X] += SLOT_TILES + 1

        def experts_act(act):
            act.wait_ge(score_ready, 1)
            act.activation(score2[:], top2[:], ACT.Sigmoid).then_inc(score_ready, 1)
            for n in range(G):
                for m in range(M2):
                    act.wait_ge(*filled(("sh", 0, m, n)))
                    if m or n:
                        act.wait_ge(sh_ready, n * M2 + m)
                    act.activation(silu_t, at(("sh", 0, m, n)), ACT.Silu).then_inc(free_of(("sh", 0, m, n)), 1)

            def step(t, now, prev):
                if now:
                    act.wait_ge(banks.full[Z_X], base3[Z_X] + t + 1)
                    act.activation(slots_T, psum[:, Z_X, 0:D], ACT.Copy).then_inc(banks.free[Z_X], 1)
                    act.wait_ge(banks.full[Z_G], base3[Z_G] + t + 1)
                    act.activation(gated, psum[:, Z_G, :], ACT.Silu).then_inc(banks.free[Z_G], 1)
                if prev:
                    act.wait_ge(banks.full[Z_Y], base3[Z_Y] + t)
                    act.wait_ge(slots_stored, 16 * t)
                    act.activation(slots_out, psum[:, Z_Y, 0:D], ACT.Copy).then_inc(banks.free[Z_Y], 1)

            step(0, True, False)
            with act.Fori(1, SLOT_TILES) as t:
                step(t, True, True)
            step(SLOT_TILES, False, True)

        def experts_dve(dve, then):
            dve.wait_ge(*filled("router"))
            flat = lambda v: v.rearrange("p b e -> p (b e)")
            dve.tensor_copy(flat(lg2[:]), at("router")[:, 0:NB * E]).then_inc(free_of("router"), 1)
            dve.wait_ge(*read("router"))
            dve.tensor_reduce(top2[:], lg2[:], AX, ALU.max).then_inc(score_ready, 1)
            rank_experts(dve, then, lg2[:], more2, same2, tri2, rank2, 1)
            then(dve.tensor_scalar(sel[:], rank2, 0.5, None, ALU.is_lt))
            then(dve.tensor_copy(scan_a[:, 0:1, :], sel[:, 0:1, :]))
            then(dve.tensor_tensor(scan_a[:, 1:NB, :], sel[:, 1:NB, :], sel[:, 0:NB - 1, :], ALU.add))
            then(dve.tensor_copy(scan_b[:, 0:2, :], scan_a[:, 0:2, :]))
            then(dve.tensor_tensor(scan_b[:, 2:NB, :], scan_a[:, 2:NB, :], scan_a[:, 0:NB - 2, :], ALU.add))
            then(dve.tensor_copy(scan_a[:, 0:4, :], scan_b[:, 0:4, :]))
            then(dve.tensor_tensor(scan_a[:, 4:NB, :], scan_b[:, 4:NB, :], scan_b[:, 0:NB - 4, :], ALU.add))
            then(dve.tensor_copy(scan_b[:], scan_a[:]))
            dve.tensor_tensor(scan_a[:], scan_b[:], sel[:], ALU.subtract).then_inc(sel_ready, 1)
            dve.wait_ge(*filled("pos"))
            then(dve.tensor_copy(flat(pos[:]), at("pos")[:, 0:NB * E]))
            dve.tensor_scalar(tiles_e[:, 0, :], at("pos")[:, NB * E:(NB + 1) * E], 1.0 / P, (P - 1.0) / P - 0.5 + 0.5 / P,
                              ALU.mult, ALU.add).then_inc(free_of("pos"), 1)
            dve.wait_ge(*read("pos"))
            then(dve.tensor_scalar(tiles_e[:, 0, :], tiles_e[:, 0, :], MAGIC, MAGIC, ALU.add, ALU.subtract))
            src, dst = 0, 1
            for d in (1, 2, 4):
                then(dve.tensor_copy(tiles_e[:, dst, 0:d], tiles_e[:, src, 0:d]))
                then(dve.tensor_tensor(tiles_e[:, dst, d:E], tiles_e[:, src, d:E], tiles_e[:, src, 0:E - d], ALU.add))
                src, dst = dst, (2 if dst == 1 else 1)
            upto, start = src, dst
            then(dve.tensor_tensor(tiles_e[:, start, :], tiles_e[:, upto, :], tiles_e[:, 0, :], ALU.subtract))
            then(dve.scalar_tensor_tensor(pos[:], tiles_e[:, start, :].unsqueeze(1).to_broadcast([P, NB, E]), float(P), pos[:],
                                          ALU.mult, ALU.add))
            then(dve.tensor_tensor(pos[:], pos[:], sel[:], ALU.mult))
            then(dve.tensor_reduce(slot_f[:], pos[:], AX, ALU.add))
            dve.tensor_copy(slot_i[:], slot_f[:]).then_inc(slot_ready, 1)
            then(dve.tensor_tensor(owner_c[:], tiles_e[:, upto, :].unsqueeze(1).to_broadcast([P, SLOT_TILES, E]),
                                   tile_no.unsqueeze(2).to_broadcast([P, SLOT_TILES, E]), ALU.is_le))
            then(dve.tensor_reduce(owner_f[:], owner_c[:], AX, ALU.add))
            dve.tensor_scalar(owner_i[:], owner_f[:], E - 1.0, None, ALU.min).then_inc(owner_ready, 1)
            dve.wait_ge(score_ready, 2)
            for b in range(NB):
                dve.tensor_scalar(xr[:, b, :], X[:, b, :], score2[:, b:b + 1], None, ALU.mult).then_inc(xr_ready, 1)
            for n in range(G):
                for m in range(M2):
                    dve.wait_ge(*read(("sh", 0, m, n)))
                    dve.wait_ge(*filled(("sh", 1, m, n)))
                    dve.tensor_tensor(shT[:, m, n * 512:n * 512 + 512], silu_t, at(("sh", 1, m, n)), ALU.mult)\
                       .then_inc(free_of(("sh", 1, m, n)), 1)
                    dve.wait_ge(*read(("sh", 1, m, n)))
                    dve.sem_inc(sh_ready, 1)
            for c in range(NCH):
                dve.wait_ge(*filled(("ysh", c)))
                dve.tensor_tensor(H[:, 2 * c:2 * c + 2, :].rearrange("p b n -> p (b n)"), at(("ysh", c)),
                                  X[:, 2 * c:2 * c + 2, :].rearrange("p b n -> p (b n)"), ALU.add)\
                   .then_inc(free_of(("ysh", c)), 1)

            def step(t, now, prev):
                if prev:
                    dve.wait_ge(banks.full[Z_H], base3[Z_H] + t)
                    dve.tensor_scalar(hid_T, psum[:, Z_H, :], 1.0, None, ALU.mult).then_inc(banks.free[Z_H], 1)
                if now:
                    dve.wait_ge(banks.free[Z_G], base3[Z_G] + t + 1)
                    dve.wait_ge(banks.full[Z_U], base3[Z_U] + t + 1)
                    dve.tensor_tensor(hid, gated, psum[:, Z_U, :], ALU.mult).then_inc(banks.free[Z_U], 1)
                    dve.wait_ge(banks.free[Z_U], base3[Z_U] + t + 1)
                    dve.sem_inc(hid_ready, 1)

            slot_steps(dve, step)
            dve.wait_ge(gathered, 16 * NB)
            for b in range(NB):
                dve.tensor_tensor(H[:, b, :], H[:, b, :], yg[:, b, :], ALU.add).then_inc(signal("summed"), 1)
            dve.wait_ge(signal("summed"), NB)

        def experts_pool(pool):
            pool.wait_ge(slot_ready, 1)
            pool.wait_ge(slots_stored, 16)
            for b in range(NB):
                pool.wait_ge(xr_ready, b + 1)
                pool.indirect_dma_start(x_slots, bass.IndirectOffsetOnAxis(ap=slot_i[:, b:b + 1], axis=0), xr[:, b, :], None)\
                    .then_inc(scattered, 16)
            pool.wait_ge(slots_stored, 16 + 16 * SLOT_TILES)
            for b in range(NB):
                pool.indirect_dma_start(yg[:, b, :], None, y_slots, bass.IndirectOffsetOnAxis(ap=slot_i[:, b:b + 1], axis=0))\
                    .then_inc(gathered, 16)

        def experts_sp(sp):
            sp.wait_ge(scattered, 16 * NB)
            for t in range(SLOT_TILES + 1):
                if t:
                    sp.wait_ge(banks.full[Z_X], base3[Z_X] + t)
                row = min(t, SLOT_TILES - 1) * P
                sp.dma_start(slots_in, x_slots[row:row + P, :]).then_inc(slots_loaded, 16)
                if t >= 2:
                    store_slots(sp, t - 2)
            store_slots(sp, SLOT_TILES - 1)

        def store_slots(sp, t):
            sp.wait_ge(banks.free[Z_Y], base3[Z_Y] + t + 1)
            sp.dma_start(y_slots[t * P:t * P + P, :], slots_out).then_inc(slots_stored, 16)

        block = ctx.enter_context(nc.Block())

        @block.tensor
        def _(pe):
            def mm(key, j, cols, pairs, last=False, rows=P, start=True):
                for i, (l, r) in enumerate(pairs):
                    ins = pe.matmul(at(key, j)[0:rows, cols], l, r, start=(i == 0), stop=(i == len(pairs) - 1))
                if last:
                    ins.then_inc(full_of(key, j), 1)

            def claim(key, count=1):
                for s, v in take(key, count):
                    pe.wait_ge(s, v)

            pe.wait_ge(s_w["w_la"], 16)
            pe.wait_ge(s_w["xT"], 16)
            for n in range(G):
                claim(("lat", n))
                mm(("lat", n), 0, slice(0, 512), [(WkvT[:, k, :], XT[:, k, n * 512:n * 512 + 512]) for k in range(KD)], True, 64)
            claim("c")
            for n in range(G):
                pe.wait_ge(*read(("lat", n)))
            for b in range(NB):
                mm("c", 0, slice(b * HC, b * HC + HC), [(kvlatT[:, b * P:b * P + P], WcT)], b == NB - 1)

            pe.wait_ge(s_w["w_lx"], 16)
            pe.wait_ge(s_w["ctxT"], 16)
            for m in range(KD):
                for n in range(G):
                    claim(("kx", m, n))
                    mm(("kx", m, n), 0, slice(0, 512),
                       [(WkT[:, k, m * P:m * P + P], ctxT[:, k, n * 512:n * 512 + 512]) for k in range(KD)], True)
            pe.wait_ge(s_w["ident"], 16)
            claim("cT", G)
            pe.wait_ge(signal("cn_ready"), 1)
            for b in range(NB):
                ins = pe.transpose(span("cT")[0:HC, b * P:b * P + P], xc[:, b, :], ident[:])
                if b % 4 == 3:
                    ins.then_inc(full_of("cT", b // 4), 1)
            for b in range(NB // 2):
                claim(("v", b))
                for i in range(2):
                    mm(("v", b), 0, slice(i * D, i * D + D),
                       [(ctxT[:, k, (2 * b + i) * P:(2 * b + i + 1) * P], WvT[:, k, :]) for k in range(KD)], i == 1)
            for j in range(2):
                pe.wait_ge(*read("cT", j))
            for j in range(3):
                claim(("qkv", j))
                bs = range(3 * j, min(NB, 3 * j + 3))
                for b in bs:
                    mm(("qkv", j), 0, slice((b - 3 * j) * 160, (b - 3 * j) * 160 + 160),
                       [(chT[:, b * P:b * P + P], Wqkv)], b == bs[-1])
            for m in range(KD):
                for n in range(G):
                    pe.wait_ge(*read(("kx", m, n)))
            for b in range(NB):
                for h in range(2):
                    claim(("kp", b, h))
                    mm(("kp", b, h), 0, slice(0, 512), [(kx[:, h, b * P:b * P + P], BDk)], True)
                if b == 3:
                    pe.wait_ge(signal("rope_ready"), 1)
                    for which in range(2):
                        claim(("qkT", which), 2)
                        for c in range(NB):
                            ins = pe.transpose(span(("qkT", which))[0:HC, c * P:c * P + P],
                                               t1[:, c, which * HC:which * HC + HC], ident[:])
                            if c % 4 == 3:
                                ins.then_inc(full_of(("qkT", which), c // 4), 1)
            for which in range(2):
                for j in range(2):
                    pe.wait_ge(*read(("qkT", which), j))
            claim("S", 2)
            for b in range(NB):
                mm("S", b // 4, slice(b % 4 * P, b % 4 * P + P), [(qT[:, b * P:b * P + P], kT[:, b * P:b * P + P])], b % 4 == 3)
            pe.wait_ge(signal("ones_ready"), 1)
            for b in range(NB):
                claim(("kv", b))
                pe.wait_ge(*read(("v", b // 2)))
                for h in range(2):
                    pe.wait_ge(*read(("kp", b, h)))
                for c in range(CH):
                    mm(("kv", b), 0, slice(c * AUG, c * AUG + AUG),
                       [(kp[:, b, c * P:c * P + P], v_aug[:, b, c * AUG:c * AUG + AUG])], c == CH - 1)
            claim("PT", 2)
            pe.wait_ge(signal("P_ready"), 1)
            for b in range(NB):
                ins = pe.transpose(span("PT")[:, b * P:b * P + P], S[:, b, :], ident[:])
                if b % 4 == 3:
                    ins.then_inc(full_of("PT", b // 4), 1)
            claim("oT", 2)
            for j in range(3):
                pe.wait_ge(*read(("qkv", j)))
            for j in range(2):
                pe.wait_ge(*read("PT", j))
            for b in range(NB):
                mm("oT", b // 4, slice(b % 4 * P, b % 4 * P + P), [(v_la[:, b, :], PT[:, b, :])], b % 4 == 3, HC)
            for n in range(G):
                claim(("zT", n))
                pe.wait_ge(*read("oT", n))
                mm(("zT", n), 0, slice(0, 512), [(Wc2lT, oT[:, n * 512:n * 512 + 512])], True, 64)
            for n in range(G):
                pe.wait_ge(*read(("zT", n)))
            pe.wait_ge(wsum_ready, 1)
            for c in range(NCH):
                claim(("y", 0, c))
                for i in range(2):
                    b = 2 * c + i
                    mm(("y", 0, c), 0, slice(i * D, i * D + D), [(zT[:, b * P:b * P + P], Wsum)], i == 1)

            def to_features(layer):
                for c in range(NCH):
                    claim(("xt", layer, c))
                    pe.wait_ge(x_ready, layer * NB + 2 * c + 2)
                    for i in range(2):
                        for k in range(KD):
                            ins = pe.transpose(at(("xt", layer, c))[:, (2 * i + k) * P:(2 * i + k + 1) * P],
                                               X[:, 2 * c + i, k * P:k * P + P], ident[:])
                    ins.then_inc(full_of(("xt", layer, c)), 1)

            to_features(0)
            for c in range(NCH):
                pe.wait_ge(*read(("xt", 0, c)))
            for m in range(KD):
                for n in range(G):
                    claim(("qx", m, n))
                    mm(("qx", m, n), 0, slice(0, 512),
                       [(WqT[:, k, m * P:m * P + P], XT[:, k, n * 512:n * 512 + 512]) for k in range(KD)], True)
            for n in range(G):
                for m in range(KD):
                    pe.wait_ge(*read(("qx", m, n)))
                for c in range(CH):
                    r = c % 4 * 32
                    claim(("qp", c, n))
                    mm(("qp", c, n), 0, slice(0, 512), [(BDq[r:r + 32, :], qx[r:r + 32, c // 4, n * 512:n * 512 + 512])], True)
            for b in range(NB):
                claim(("ox", b))
                pe.wait_ge(*read(("kv", b)))
                for c in range(CH):
                    pe.wait_ge(*read(("qp", c, b // 4)))
                for c in range(CH):
                    mm(("ox", b), 0, slice(c * AUG, c * AUG + AUG),
                       [(qp[:, c, b * P:b * P + P], kvm[:, b, c * AUG:c * AUG + AUG])], c == CH - 1)
            for c in range(NCH):
                claim(("aT", c))
                for i in range(2):
                    pe.wait_ge(*read(("ox", 2 * c + i)))
                for i in range(2):
                    for k in range(KD):
                        ins = pe.transpose(at(("aT", c))[:, (2 * i + k) * P:(2 * i + k + 1) * P],
                                           a_x[:, 2 * c + i, k * P:k * P + P], ident[:])
                ins.then_inc(full_of(("aT", c)), 1)
            for c in range(NCH):
                claim(("y", 1, c))
                pe.wait_ge(*read(("aT", c)))
                for i in range(2):
                    b = 2 * c + i
                    mm(("y", 1, c), 0, slice(i * D, i * D + D),
                       [(aT[:, k, b * P:b * P + P], WoT[:, k, :]) for k in range(KD)], i == 1)
            to_features(1)
            for c in range(NCH):
                pe.wait_ge(*read(("xt", 1, c)))
            claim("gate")
            for b in range(NB):
                mm("gate", 0, slice(b * E, b * E + E), [(XT[:, k, b * P:b * P + P], gate_w[:, k, :]) for k in range(KD)], b == NB - 1)
            claim("combT", 2)
            pe.wait_ge(signal("comb_ready"), 1)
            for b in range(NB):
                ins = pe.transpose(span("combT")[0:E, b * P:b * P + P], comb[:, b, :], ident[:])
                if b % 4 == 3:
                    ins.then_inc(full_of("combT", b // 4), 1)
            for j in range(2):
                pe.wait_ge(*read("combT", j))
            for c in range(NCH):
                claim(("yb", c))
                for i in range(2):
                    b = 2 * c + i
                    mm(("yb", c), 0, slice(i * D, i * D + D), [(combT[:, b * P:b * P + P], fc2_b)], i == 1)
            banks.next = 0
            with pe.Fori(0, E // 2) as trip:
                for w in range(2):
                    pe.wait_ge(fc_loaded[w], 48 * trip + 48)
                    for m in range(KD):
                        for n in range(G):
                            key = ("h1", w, m, n)
                            for se, v in take(key, trip=trip, per=2):
                                pe.wait_ge(se, v)
                            mm(key, 0, slice(0, 512),
                               [(f1[:, w, k, m * P:m * P + P], XT[:, k, n * 512:n * 512 + 512]) for k in range(KD)], True)
                for w in range(2):
                    for c in range(NCH):
                        key = ("y2", w, c)
                        for se, v in take(key, trip=trip, per=2):
                            pe.wait_ge(se, v)
                        if c == 0:
                            for m in range(KD):
                                for n in range(G):
                                    pe.wait_ge(*read(("h1", w, m, n), trip=trip))
                        for i in range(2):
                            b = 2 * c + i
                            mm(key, 0, slice(i * D, i * D + D),
                               [(hT[:, w * KD + k, b * P:b * P + P], f2[:, w, k, :]) for k in range(KD)], i == 1)
            banks.looped(E // 2, 2)
            to_features(2)
            context_pe(pe)
            grouped_attention_pe(pe)
            to_features(3)
            queries_pe(pe)
            cross_pe(pe)
            to_features(4)
            experts_pe(pe)

        @block.scalar
        def _(act):
            act.dma_start(ctxT[:], W["ctxT"]).then_inc(s_w["ctxT"], 16)
            act.dma_start(ident[:], W["ident"]).then_inc(s_w["ident"], 16)
            act.dma_start(biases[:], W["biases"]).then_inc(s_w["bias0"], 16)

            def from_features(layer):
                for c in range(NCH):
                    act.wait_ge(*filled(("xt", layer, c)))
                    act.activation(XT[:, :, 2 * c * P:(2 * c + 2) * P].rearrange("p k (i t) -> p i k t", i=2),
                                   at(("xt", layer, c)).rearrange("p (i k t) -> p i k t", i=2, k=KD),
                                   ACT.Copy).then_inc(free_of(("xt", layer, c)), 1)

            for n in range(G):
                act.wait_ge(*filled(("lat", n)))
                act.activation(kvlatT[:, n * 512:n * 512 + 512], at(("lat", n))[0:64, :], ACT.Copy)\
                   .then_inc(free_of(("lat", n)), 1)
            for m in range(KD):
                for n in range(G):
                    act.wait_ge(*filled(("kx", m, n)))
                    act.activation(kx[:, m, n * 512:n * 512 + 512], at(("kx", m, n)), ACT.Identity, bias=bk_lx[:, m:m + 1])\
                       .then_inc(free_of(("kx", m, n)), 1)
            for j in range(2):
                act.wait_ge(*filled("cT", j))
                act.activation(chT[:, j * 512:j * 512 + 512], at("cT", j)[0:HC, :], ACT.Identity,
                               bias=beta, scale=gamma).then_inc(free_of("cT", j), 1)
            for which, dst in enumerate((qT, kT)):
                for j in range(2):
                    act.wait_ge(*filled(("qkT", which), j))
                    act.activation(dst[:, j * 512:j * 512 + 512], at(("qkT", which), j)[0:HC, :], ACT.Copy)\
                       .then_inc(free_of(("qkT", which), j), 1)
            act.wait_ge(signal("S_less_max"), 1)
            act.activation(S, S, ACT.Exp).then_inc(signal("S_exp"), 1)
            for j in range(2):
                act.wait_ge(*filled("PT", j))
                act.activation(PT[:, 4 * j:4 * j + 4, :].rearrange("p b t -> p (b t)"), at("PT", j), ACT.Copy)\
                   .then_inc(free_of("PT", j), 1)
            for j in range(2):
                act.wait_ge(*filled("oT", j))
                act.activation(oT[:, j * 512:j * 512 + 512], at("oT", j)[0:HC, :], ACT.Copy).then_inc(free_of("oT", j), 1)
            for n in range(G):
                act.wait_ge(*filled(("zT", n)))
                act.activation(zT[:, n * 512:n * 512 + 512], at(("zT", n))[0:64, :], ACT.Copy).then_inc(free_of(("zT", n)), 1)
            from_features(0)
            for m in range(KD):
                for n in range(G):
                    act.wait_ge(*filled(("qx", m, n)))
                    act.activation(qx[:, m, n * 512:n * 512 + 512], at(("qx", m, n)), ACT.Identity, bias=bq_lx[:, m:m + 1])\
                       .then_inc(free_of(("qx", m, n)), 1)
            for n in range(G):
                for c in range(0, CH, 2):
                    act.wait_ge(*filled(("qp", c, n)))
                    act.activation(qp[:, c, n * 512:n * 512 + 512], at(("qp", c, n)), ACT.Relu)\
                       .then_inc(free_of(("qp", c, n)), 1)
            for c in range(NCH):
                act.wait_ge(*filled(("aT", c)))
                act.activation(aT[:, :, 2 * c * P:(2 * c + 2) * P].rearrange("p k (i t) -> p i k t", i=2),
                               at(("aT", c)).rearrange("p (i k t) -> p i k t", i=2, k=KD),
                               ACT.Copy).then_inc(free_of(("aT", c)), 1)
            from_features(1)
            act.wait_ge(*read("gate"))
            act.activation(pr, lg, ACT.Exp).then_inc(signal("gate_exp"), 1)
            for j in range(2):
                act.wait_ge(*filled("combT", j))
                act.activation(combT[:, j * 512:j * 512 + 512], at("combT", j)[0:E, :], ACT.Copy)\
                   .then_inc(free_of("combT", j), 1)
            with act.Fori(0, E // 2) as trip:
                for w in range(2):
                    act.wait_ge(*filled(("y2", w, NCH - 1), trip=trip - 1))
                    for m in range(KD):
                        for n in range(G):
                            act.wait_ge(*filled(("h1", w, m, n), trip=trip))
                            act.activation(hT[:, w * KD + m, n * 512:n * 512 + 512], at(("h1", w, m, n)), ACT.Gelu,
                                           bias=f1b[:, w, m:m + 1]).then_inc(free_of(("h1", w, m, n)), 1)
            from_features(2)
            context_act(act)
            grouped_attention_act(act)
            from_features(3)
            queries_act(act)
            cross_act(act)
            from_features(4)
            experts_act(act)

        @block.vector
        def _(dve):
            steps = [0]

            def then(ins):
                steps[0] += 1
                ins.then_inc(s_dve, 1)
                dve.wait_ge(s_dve, steps[0])

            def stats(c):
                for b in (2 * c, 2 * c + 1):
                    then(dve.bn_stats(st[:, b, :], H[:, b, :]))
                    then(dve.bn_aggr(mv[:, b, :], st[:, b, :]))
                dve.tensor_scalar(ve[:, 2 * c:2 * c + 2], mv[:, 2 * c:2 * c + 2, 1], LN_EPS, None, ALU.add)\
                   .then_inc(var_ready, 1)

            def normalise(layer, c):
                dve.wait_ge(rstd_ready, layer * NCH + c + 1)
                for b in (2 * c, 2 * c + 1):
                    dve.tensor_scalar(X[:, b, :], H[:, b, :], mv[:, b, 0:1], rstd[:, b:b + 1], ALU.subtract, ALU.mult)\
                       .then_inc(x_ready, 1)

            def norm_layer(layer, nth, add=True):
                for c in range(NCH):
                    if add:
                        dve.wait_ge(*filled(("y", layer, c)))
                        dve.wait_ge(xb_ready, nth * NCH + c + 1)
                        dve.tensor_tensor(H[:, 2 * c:2 * c + 2, :].rearrange("p b n -> p (b n)"), at(("y", layer, c)),
                                          XB[:, 2 * c:2 * c + 2, :].rearrange("p b n -> p (b n)"), ALU.add)\
                           .then_inc(free_of(("y", layer, c)), 1)
                        dve.wait_ge(*read(("y", layer, c)))
                    stats(c)
                    if c:
                        normalise(layer, c - 1)
                normalise(layer, NCH - 1)

            dve.wait_ge(s_w["w_la"], 16)
            dve.wait_ge(*filled("c"))
            cp = at("c")[:, 0:NB * HC].rearrange("p (b n) -> p b n", b=NB)
            then(dve.tensor_reduce(s1, cp, AX, ALU.add))
            dve.scalar_tensor_tensor(xc, s1.unsqueeze(2).to_broadcast([P, NB, HC]), -1.0 / HC, cp, ALU.mult, ALU.add)\
               .then_inc(free_of("c"), 1)
            dve.wait_ge(*read("c"))
            then(dve.tensor_tensor(sq, xc, xc, ALU.mult))
            then(dve.tensor_reduce(vl, sq, AX, ALU.add))
            dve.tensor_scalar(vl, vl, 1.0 / HC, LN_EPS, ALU.mult, ALU.add).then_inc(signal("latent_var"), 1)
            dve.wait_ge(signal("latent_rstd"), 1)
            dve.tensor_tensor(xc, xc, rl.unsqueeze(2).to_broadcast([P, NB, HC]), ALU.mult).then_inc(signal("cn_ready"), 1)
            for b in range(NB // 2):
                dve.wait_ge(*filled(("v", b)))
                dve.tensor_tensor(v_aug_h[:, 2 * b:2 * b + 2, :, 0:HD],
                                  at(("v", b)).rearrange("p (i h e) -> p i h e", i=2, h=NH),
                                  bv_lx.rearrange("p (h e) -> p h e", h=NH).unsqueeze(1).to_broadcast([P, 2, NH, HD]),
                                  ALU.add).then_inc(free_of(("v", b)), 1)
            for j in range(3):
                dve.wait_ge(*filled(("qkv", j)))
                nb = min(NB, 3 * j + 3) - 3 * j
                pq = at(("qkv", j))[:, 0:nb * 160].rearrange("p (b n) -> p b n", b=nb)
                bs = slice(3 * j, 3 * j + nb)
                then(dve.tensor_tensor(t1[:, bs, :], pq[:, :, 0:64], cosq.unsqueeze(1).to_broadcast([P, nb, 64]), ALU.mult))
                then(dve.tensor_tensor(t2[:, bs, :], pq[:, :, 64:128], sinq.unsqueeze(1).to_broadcast([P, nb, 64]), ALU.mult))
                dve.tensor_copy(v_la[:, bs, :], pq[:, :, 128:160]).then_inc(free_of(("qkv", j)), 1)
            dve.tensor_tensor(t1, t1, t2, ALU.add).then_inc(signal("rope_ready"), 1)
            for b in range(NB):
                for h in range(2):
                    dve.wait_ge(*filled(("kp", b, h)))
                    dve.tensor_scalar(kp[:, b, h * 512:h * 512 + 512], at(("kp", b, h)), 0.0, mask[:, b:b + 1],
                                      ALU.max, ALU.mult).then_inc(free_of(("kp", b, h)), 1)
            for j in range(2):
                dve.wait_ge(*filled("S", j))
                dve.scalar_tensor_tensor(S[:, 4 * j:4 * j + 4, :], at("S", j).rearrange("p (b t) -> p b t", b=4),
                                         float(HC) ** -0.5, causal.unsqueeze(1).to_broadcast([P, 4, P]),
                                         ALU.mult, ALU.add).then_inc(free_of("S", j), 1)
            for j in range(2):
                dve.wait_ge(*read("S", j))
            then(dve.tensor_reduce(r1, S, AX, ALU.max))
            dve.tensor_tensor(S, S, r1.unsqueeze(2).to_broadcast([P, NB, P]), ALU.subtract)\
               .then_inc(signal("S_less_max"), 1)
            for b in range(NB):
                dve.wait_ge(*filled(("kv", b)))
                dve.tensor_tensor(kvm[:, b, :], at(("kv", b))[:, 0:CH * AUG], bdmask, ALU.mult)\
                   .then_inc(free_of(("kv", b)), 1)
            dve.wait_ge(signal("S_exp"), 1)
            then(dve.tensor_reduce(r2, S, AX, ALU.add))
            then(dve.reciprocal(r2, r2))
            dve.tensor_tensor(S, S, r2.unsqueeze(2).to_broadcast([P, NB, P]), ALU.mult).then_inc(signal("P_ready"), 1)
            dve.wait_ge(slots_stored, 16)
            norm_layer(0, 0)
            for n in range(G):
                for c in range(1, CH, 2):
                    dve.wait_ge(*filled(("qp", c, n)))
                    dve.tensor_scalar(qp[:, c, n * 512:n * 512 + 512], at(("qp", c, n)), 0.0, None, ALU.max)\
                       .then_inc(free_of(("qp", c, n)), 1)
            for b in range(NB):
                dve.wait_ge(*filled(("ox", b)))
                po = at(("ox", b))[:, 0:CH * AUG].rearrange("p (h e) -> p h e", e=HD + 1)
                then(dve.tensor_scalar(den[:, b, :], po[:, :, HD], 1e-8, None, ALU.add))
                then(dve.reciprocal(rden[:, b, :], den[:, b, :]))
                dve.tensor_tensor(a_x[:, b, :].rearrange("p (h e) -> p h e", h=NH), po[:, :, 0:HD],
                                  rden[:, b, :].unsqueeze(2).to_broadcast([P, NH, HD]), ALU.mult)\
                   .then_inc(free_of(("ox", b)), 1)
            norm_layer(1, 1)
            dve.wait_ge(*filled("gate"))
            pg = at("gate")[:, 0:NB * E].rearrange("p (b e) -> p b e", b=NB)
            then(dve.tensor_reduce(gm, pg, AX, ALU.max))
            dve.tensor_tensor(lg, pg, gm.unsqueeze(2).to_broadcast([P, NB, E]), ALU.subtract).then_inc(free_of("gate"), 1)
            dve.wait_ge(*read("gate"))
            dve.wait_ge(signal("gate_exp"), 1)
            then(dve.tensor_reduce(gs, pr, AX, ALU.add))
            then(dve.reciprocal(gs, gs))
            then(dve.tensor_tensor(pr, pr, gs.unsqueeze(2).to_broadcast([P, NB, E]), ALU.mult))
            rank_experts(dve, then, pr, GT, GE, tri, rank, 0)
            then(dve.scalar_tensor_tensor(comb, rank, 1.5, pr, ALU.is_lt, ALU.mult))
            then(dve.tensor_reduce(gr, comb, AX, ALU.add))
            then(dve.reciprocal(gr, gr))
            then(dve.tensor_tensor(comb, comb, gr.unsqueeze(2).to_broadcast([P, NB, E]), ALU.mult))
            dve.tensor_tensor(comb, comb, alpha.unsqueeze(1).to_broadcast([P, NB, E]), ALU.mult)\
               .then_inc(signal("comb_ready"), 1)
            dve.wait_ge(signal("comb_ready"), 1)
            for c in range(NCH):
                dve.wait_ge(*filled(("yb", c)))
                dve.tensor_tensor(H[:, 2 * c:2 * c + 2, :].rearrange("p b n -> p (b n)"), at(("yb", c)),
                                  X[:, 2 * c:2 * c + 2, :].rearrange("p b n -> p (b n)"), ALU.add)\
                   .then_inc(free_of(("yb", c)), 1)
            for c in range(NCH):
                dve.wait_ge(*read(("yb", c)))
            with dve.Fori(0, E // 2) as trip:
                for w in range(2):
                    for c in range(NCH):
                        dve.wait_ge(*filled(("y2", w, c), trip=trip))
                        dve.wait_ge(*read(("y2", 1 - w, c), trip=trip - 1 + w))
                        for i in range(2):
                            b = 2 * c + i
                            ins = dve.scalar_tensor_tensor(H[:, b, :], at(("y2", w, c))[:, i * D:i * D + D],
                                                           comb[:, b, bass.ds(2 * trip + w, 1)],
                                                           H[:, b, :], ALU.mult, ALU.add)
                        ins.then_inc(free_of(("y2", w, c)), 1)
            for c in range(NCH):
                dve.wait_ge(*read(("y2", 1, c), trip=E // 2 - 1))
            norm_layer(2, None, add=False)

            def then_in_loop(ins, h, which, trip):
                sems = (raw_ready, recip_ready)
                ins.then_inc(sems[1 - which], 1)
                dve.wait_ge(sems[1 - which], KV * trip + h + 1 - (0 if which else 2))

            count = [0]
            context_dve(dve, count)
            for c in range(NCH):
                dve.wait_ge(*read(("xt", 2, c)))
            grouped_attention_dve(dve, then_in_loop)
            norm_layer(3, None, add=False)
            for c in range(NCH):
                quantise_rows(dve, count, ("q2", c), bq2, c, True)
            for b in range(NB):
                dve.wait_ge(*read(("qspT", b)))
            cross_dve(dve)
            norm_layer(4, None, add=False)
            experts_dve(dve, then)
            norm_layer(5, None, add=False)

        @block.gpsimd
        def _(pool):
            pool.memset(H[:, 0, :], 0.0).then_inc(signal("zeros_ready"), 1)
            pool.memset(XT_flat[:, KD * N:], 0.0).then_inc(signal("spare_ready"), 1)
            pool.memset(neghalf[:], -0.5).then_inc(signal("neghalf_ready"), 1)
            pool.memset(v_aug_h[:, :, :, HD:HD + 1], 1.0).then_inc(signal("ones_ready"), 1)
            pool.wait_ge(s_w["w_la"], 16)
            pool.tensor_tensor(Wsum, W_kv, W_res, ALU.add).then_inc(wsum_ready, 1)
            pool.wait_ge(s_w["x"], 16)
            pool.wait_ge(s_w["bias0"], 16)
            pool.wait_ge(signal("neghalf_ready"), 1)

            def plus_bias(nth, c):
                pool.tensor_tensor(XB[:, 2 * c:2 * c + 2, :], X[:, 2 * c:2 * c + 2, :],
                                   biases[:, nth, :].unsqueeze(1).to_broadcast([P, 2, D]), ALU.add).then_inc(xb_ready, 1)

            def norm_layer(layer, nth=None):
                for c in range(NCH + 1):
                    if c < NCH:
                        pool.wait_ge(var_ready, layer * NCH + c + 1)
                        pool.tensor_tensor(rstd[:, 2 * c:2 * c + 2], ve[:, 2 * c:2 * c + 2], neghalf[:, 0:2], ALU.pow)\
                            .then_inc(rstd_ready, 1)
                    if c and nth is not None:
                        pool.wait_ge(x_ready, layer * NB + 2 * c)
                        plus_bias(nth, c - 1)

            for c in range(NCH):
                plus_bias(0, c)
            pool.wait_ge(signal("latent_var"), 1)
            pool.tensor_tensor(rl, vl, neghalf[:], ALU.pow).then_inc(signal("latent_rstd"), 1)
            norm_layer(0, 1)
            norm_layer(1)
            pool.wait_ge(s_w["late"], 16)
            pool.tensor_scalar(kws[:], kw, DH ** -0.5, None, ALU.mult).then_inc(signal("kws_ready"), 1)
            pool.wait_ge(signal("kws_ready"), 1)
            pool.wait_ge(s_w["w_qkv"], 32)
            for h in range(KV):
                wq = w_qkv[:, h, :, 0:GRP * DH].rearrange("p k (g c) -> p k g c", g=GRP)
                for k in range(KD):
                    ins = pool.tensor_tensor(wq[:, k], wq[:, k], kws[:, h * GRP:h * GRP + GRP].unsqueeze(2).to_broadcast([P, GRP, DH]),
                                       ALU.mult)
                ins.then_inc(w_scaled, 1)
            bq = b_qkv[:, :, 0:GRP * DH].rearrange("p h (g c) -> p h g c", g=GRP)
            pool.tensor_tensor(bq, bq, kws[:].rearrange("p (h g) -> p h g", h=KV).unsqueeze(3).to_broadcast([P, KV, GRP, DH]),
                               ALU.mult).then_inc(w_scaled, 1)
            norm_layer(2, 2)
            grouped_attention_pool(pool)
            norm_layer(3, 3)
            norm_layer(4)
            experts_pool(pool)
            norm_layer(5)

        @block.sync
        def _(sp):
            sp.dma_start(w_la, W["w_la"]).then_inc(s_w["w_la"], 16)
            sp.dma_start(XT[:], W["xT"]).then_inc(s_w["xT"], 16)
            sp.dma_start(w_lx, W["w_lx"]).then_inc(s_w["w_lx"], 16)
            sp.dma_start(X[:], W["x"]).then_inc(s_w["x"], 16)
            sp.wait_ge(signal("zeros_ready"), 1)
            sp.dma_start(x_slots.rearrange("(t p) n -> p t n", p=P), H[:, 0:1, :].to_broadcast([P, SLOT_TILES, D]))\
              .then_inc(slots_stored, 16)
            for e in range(E):
                w = e % 2
                if e >= 2:
                    sp.wait_ge(*filled(("y2", w, NCH - 1), trip=e // 2 - 1))
                    sp.wait_ge(*read(("h1", w, KD - 1, G - 1), trip=e // 2 - 1))
                sp.dma_start(f1[:, w], W["fc1"][:, e]).then_inc(fc_loaded[w], 16)
                sp.dma_start(f2[:, w], W["fc2"][:, e]).then_inc(fc_loaded[w], 16)
                sp.dma_start(f1b[:, w], W["fc1_b"][:, e]).then_inc(fc_loaded[w], 16)
            sp.dma_start(late[:], W["late"]).then_inc(s_w["late"], 16)
            sp.dma_start(w_xk, W["w_xk"]).then_inc(s_w["w_xx"], 16)
            sp.dma_start(w_xx[:], W["w_xx"]).then_inc(s_w["w_xx"], 16)
            sp.wait_ge(*filled(("y", 1, NCH - 1)))
            sp.dma_start(w_qkv, W["w_qkv"]).then_inc(s_w["w_qkv"], 16)
            sp.dma_start(b_qkv, W["b_qkv"]).then_inc(s_w["w_qkv"], 16)
            sp.dma_start(WoT1, W["WoT1"]).then_inc(s_w["WoT1"], 16)
            sp.wait_ge(banks.full[B_Y], base[B_Y] + NB)
            sp.dma_start(W_gu, W["w_gu"]).then_inc(s_w["w_gu"], 16)
            sp.dma_start(W_dn, W["w_dn"]).then_inc(s_w["w_dn"], 16)
            sp.wait_ge(banks.full[XS + 2], base2[XS + 2] + NB * HX // 2)
            sp.dma_start(W_sh, W["w_sh"]).then_inc(s_w["w_sh"], 16)
            sp.dma_start(W_sd, W["w_sd"]).then_inc(s_w["w_sh"], 16)
            experts_sp(sp)
            for b in range(NB):
                sp.wait_ge(x_ready, 5 * NB + b + 1)
                sp.dma_start(out[b], X[:, b, :]).then_inc(s_out, 16)
            sp.wait_ge(s_out, 16 * NB)


def column_table(parts):
    table, at = {}, 0
    for name, a in parts:
        table[name] = (at, at + a.shape[1])
        at += a.shape[1]
    return table, at


def side_by_side(np, parts):
    table, width = column_table(parts)
    whole = np.zeros((P, width), np.float32)
    for name, a in parts:
        whole[:a.shape[0], table[name][0]:table[name][1]] = a
    return whole, table, width


def lay_out(np, i):
    NB, _, D = i["x"].shape
    KD = D // P
    rows = lambda w: np.concatenate([w[k * P:(k + 1) * P] for k in range(w.shape[0] // P)], axis=1)
    over = lambda v: np.broadcast_to(v[None, :], (P, v.shape[0]))
    cols = lambda v: v.reshape(-1, P).T
    T = {"NB": NB, "D": D}
    A = {}
    A["xT"] = rows(i["x"].reshape(NB * P, D).T).reshape(P, KD, NB * P)
    A["ctxT"] = rows(i["ctx_2048"].reshape(NB * P, D).T).reshape(P, KD, NB * P)
    A["x"] = i["x"].transpose(1, 0, 2)
    A["ident"] = np.eye(P, dtype=np.float32)
    A["biases"] = np.stack([over(i[n]) for n in ("L0_attn_b_out_res", "L0_xattn_bo", "L1_attn_bo", "L1_xattn_bp")], axis=1)
    HC = i["L0_attn_W_compress"].shape[0]
    half = np.r_[HC // 2:HC, 0:HC // 2]
    Wq, Wk, Wv = i["L0_attn_W_q_comp"], i["L0_attn_W_kv_comp"][:HC], i["L0_attn_W_kv_comp"][HC:]
    t = np.arange(P, dtype=np.float32)[:, None]
    f = t * (1.0 / 10000.0 ** (np.arange(0, HC, 2, dtype=np.float32) / HC))[None, :].astype(np.float32)
    cos, sin = np.cos(f).astype(np.float32), np.sin(f).astype(np.float32)
    cos, sin = np.concatenate([cos, cos], 1), np.concatenate([-sin, sin], 1)
    E = i["L0_ffn_gate_w"].shape[1]
    heads = np.zeros((P, 8 * 34), np.float32)
    heads.reshape(2, P // 2, 8, 2, 17)[0, :, :, 0] = 1
    heads.reshape(2, P // 2, 8, 2, 17)[1, :, :, 1] = 1
    la = [("WkvT", rows(i["L0_attn_W_to_kv"].T)), ("WcT", i["L0_attn_W_compress"].T),
          ("Wqkv", np.concatenate([Wq.T, Wk.T, Wq[half].T, Wk[half].T, Wv.T], axis=1)),
          ("Wc2lT", i["L0_attn_W_comp2lat"].T), ("W_kv", i["L0_attn_W_to_kv"]), ("W_res", i["L0_attn_W_out_res"].T),
          ("gamma", i["L0_attn_ln_gamma"][:, None]), ("beta", i["L0_attn_ln_beta"][:, None]),
          ("cos", np.concatenate([cos, cos], 1)), ("sin", np.concatenate([sin, sin], 1)),
          ("causal", np.where(np.tril(np.ones((P, P), bool)), 0.0, -1e30).astype(np.float32)),
          ("bv_lx", over(i["L0_xattn_bv"])), ("mask", i["mask_BxS2_ff1"].T),
          ("bq_lx", cols(i["L0_xattn_bq"])), ("bk_lx", cols(i["L0_xattn_bk"])), ("bdmask", heads),
          ("gate_w", rows(i["L0_ffn_gate_w"])), ("alpha", over(i["L0_ffn_alpha"])),
          ("tri", np.broadcast_to(np.tril(np.ones((E, E), np.float32), -1).reshape(1, -1), (P, E * E))),
          ("fc2_b", i["L0_ffn_fc2_b"])]
    A["w_la"], T["la"], T["la_cols"] = side_by_side(np, la)
    BDk, BDq = np.zeros((P, 8 * 64), np.float32), np.zeros((P, P), np.float32)
    for h in range(8):
        BDk[h * 16:h * 16 + 16, h * 64:h * 64 + 64] = i["L0_xattn_Wkf"].T
        BDq[h * 16:h * 16 + 16, h % 2 * 64:h % 2 * 64 + 64] = i["L0_xattn_Wqf"].T
    lx = [("WqT", rows(i["L0_xattn_Wq"].T)), ("WkT", rows(i["L0_xattn_Wk"].T)), ("WvT", rows(i["L0_xattn_Wv"].T)),
          ("WoT", rows(i["L0_xattn_Wo"].T)), ("BDk", BDk), ("BDq", BDq)]
    A["w_lx"], T["lx"], T["lx_cols"] = side_by_side(np, lx)
    KV, GRP, DH = 8, 4, 64
    head = lambda n: i[n].reshape(KV, -1, DH, D)
    whole = np.concatenate([head("L1_attn_Wq"), head("L1_attn_Wk"), head("L1_attn_Wv")], axis=1)
    A["w_qkv"] = whole.reshape(KV, (GRP + 2) * DH, KD, P).transpose(3, 0, 2, 1)
    bias = np.concatenate([i[n].reshape(KV, -1) for n in ("L1_attn_bq", "L1_attn_bk", "L1_attn_bv")], axis=1)
    A["b_qkv"] = np.broadcast_to(bias[None], (P,) + bias.shape)
    A["WoT1"] = i["L1_attn_Wo"].T.reshape(KV * 2, P, D).transpose(1, 0, 2)
    f = t * (1.0 / 10000.0 ** (np.arange(0, DH, 2, dtype=np.float32) / DH))[None, :].astype(np.float32)
    cos, sin = np.cos(f).astype(np.float32), np.sin(f).astype(np.float32)
    late = [("cos", np.concatenate([cos, cos], 1)), ("sin", np.concatenate([-sin, sin], 1)),
            ("causal", dict(la)["causal"]), ("kw", over(i["L1_attn_key_weights"])),
            ("router", rows(i["L1_ffn_router_w"].T)), ("tri", dict(la)["tri"]),
            ("earlier", np.triu(np.ones((P, P), np.float32), 1)), ("ones", np.ones((P, P), np.float32)),
            ("tile_no", over(np.arange((NB * P + E * (P - 1)) // P, dtype=np.float32)))]
    A["late"], T["lt"], T["late_cols"] = side_by_side(np, late)
    bkv = i["L1_xattn_bkv"]
    xk = [("Wk", rows(i["L1_xattn_Wkv"][:, :D])), ("Wv", rows(i["L1_xattn_Wkv"][:, D:])), ("bk", over(bkv[:D])),
          ("bv", cols(bkv[D:]))]
    A["w_xk"], T["xk"], T["xk_cols"] = side_by_side(np, xk)
    xx = [("Wq", rows(i["L1_xattn_Wq"])), ("Wp", rows(i["L1_xattn_Wp"])), ("bq", over(i["L1_xattn_bq"]))]
    A["w_xx"], T["xx"], T["xx_cols"] = side_by_side(np, xx)
    by_rows = lambda w: w.reshape(w.shape[0], -1, P, w.shape[2]).transpose(2, 0, 1, 3)
    by_depth = lambda w: w.reshape(w.shape[0], -1, P, w.shape[2]).transpose(2, 1, 0, 3)
    A["w_gu"], A["w_dn"] = by_depth(i["L1_ffn_gate_up_proj"]), by_depth(i["L1_ffn_down_proj"])
    A["w_sh"] = np.concatenate([i["L1_ffn_shared_gate_w"], i["L1_ffn_shared_up_w"]], axis=1).reshape(KD, P, -1).transpose(1, 0, 2)
    A["w_sd"] = i["L1_ffn_shared_down_w"].reshape(-1, P, D).transpose(1, 0, 2)
    A["fc1"], A["fc2"] = by_rows(i["L0_ffn_fc1_w"]), by_rows(i["L0_ffn_fc2_w"])
    A["fc1_b"] = i["L0_ffn_fc1_b"].reshape(E, KD, P).transpose(2, 0, 1)
    return T, {n: np.ascontiguousarray(a) for n, a in A.items()}


def kernel(**inputs):
    import numpy as np
    import concourse.bacc as bacc
    from concourse.bass_utils import run_bass_kernel_spmd as run

    inputs = {n: np.asarray(a) for n, a in inputs.items()}
    T, arrays = lay_out(np, inputs)
    nc = bacc.Bacc("TRN2", target_bir_lowering=False, num_devices=1)
    W = {n: nc.dram_tensor("in_" + n, a.shape, mybir.dt.from_np(a.dtype), kind="ExternalInput").ap() for n, a in arrays.items()}
    out = nc.dram_tensor("out", inputs["x"].shape, F32, kind="ExternalOutput").ap()
    build(nc, T, W, out)
    return run(nc, [{"in_" + n: a for n, a in arrays.items()}], core_ids=[0]).results[0]["out"]
```

```python
from contextlib import ExitStack

import concourse.bass as bass
from concourse import mybir

P = 128
F32 = mybir.dt.float32
BF16 = mybir.dt.bfloat16
I32 = mybir.dt.int32
ALU = mybir.AluOpType
ACT = mybir.ActivationFunctionType
AX = mybir.AxisListType.X
LN_EPS = 1e-5


class Banks:

    def __init__(self, psum, full, free):
        self.psum, self.full, self.free = psum, full, free
        self.n = [0] * len(full)
        self.next = 0
        self.uses = {}

    def take(self, key, count=1, bank=None, trip=0, per=0):
        nb = len(self.full)
        if bank is None:
            if self.next + count > nb:
                self.next = 0
            bank = self.next
            self.next = (bank + count) % nb
        waits = [(self.free[k], self.n[k] + trip * per) for k in range(bank, bank + count) if self.n[k]]
        for k in range(bank, bank + count):
            self.n[k] += 1
        self.uses[key] = [(k, self.n[k], per) for k in range(bank, bank + count)]
        return waits

    def looped(self, trips, per, banks=None):
        for k in banks or range(len(self.n)):
            self.n[k] += (trips - 1) * per

    def at(self, key, j=0):
        return self.psum[:, self.uses[key][j][0], :]

    def span(self, key):
        first, count = self.uses[key][0][0], len(self.uses[key])
        return self.psum[:, first:first + count, :].rearrange("p k n -> p (k n)")

    def filled(self, key, j=0, trip=0):
        k, n, per = self.uses[key][j]
        return self.full[k], n + trip * per

    def read(self, key, j=0, trip=0):
        k, n, per = self.uses[key][j]
        return self.free[k], n + trip * per

    def full_of(self, key, j=0):
        return self.full[self.uses[key][j][0]]

    def free_of(self, key, j=0):
        return self.free[self.uses[key][j][0]]


def build(nc, T, W, out):
    NB, D = T["NB"], T["D"]
    N = NB * P
    KD = D // P
    G = N // 512
    ctx = ExitStack()
    with ctx:
        def sb(name, shape, dt=F32):
            return ctx.enter_context(nc.sbuf_tensor(name, shape, dt))

        def sem(name):
            return ctx.enter_context(nc.semaphore(name))

        psum = ctx.enter_context(nc.psum_tensor("psum", [P, 8, 512], F32))
        banks = Banks(psum, [sem(f"bank_full{k}") for k in range(8)], [sem(f"bank_free{k}") for k in range(8)])
        take, at, span, filled, read, full_of, free_of = (banks.take, banks.at, banks.span, banks.filled, banks.read,
                                                          banks.full_of, banks.free_of)

        X = sb("X", [P, NB, D])
        H = sb("H", [P, NB, D])
        XB = sb("XB", [P, NB, D])
        XT_flat = sb("XT", [P, KD * N + P])
        XT = XT_flat[:, 0:KD * N].rearrange("p (k n) -> p k n", k=KD)
        XT_next = XT_flat[:, P:KD * N + P].rearrange("p (k n) -> p k n", k=KD)
        ctxT = sb("ctxT", [P, KD, N])
        ident = sb("ident", [P, P])
        neghalf = sb("neghalf", [P, NB])
        st = sb("st", [P, NB, 6])
        mv = sb("mv", [P, NB, 2])
        ve = sb("ve", [P, NB])
        rstd = sb("rstd", [P, NB])
        biases = sb("biases", [P, 4, D])

        HC = 32
        early = sb("early", [P, T["la_cols"] + T["lx_cols"] + 4 * KD * D])
        w_la = early[:, 0:T["la_cols"]]
        la = T["la"]

        def pack(t, table, name, rows=P):
            a, b = table[name]
            return t[0:rows, a:b]

        WkvT = pack(w_la, la, "WkvT").rearrange("p (k n) -> p k n", k=KD)
        WcT = pack(w_la, la, "WcT", 64)
        Wqkv = pack(w_la, la, "Wqkv", HC)
        Wc2lT = pack(w_la, la, "Wc2lT", HC)
        W_kv = pack(w_la, la, "W_kv", 64)
        W_res = pack(w_la, la, "W_res", 64)
        gamma = pack(w_la, la, "gamma", HC)
        beta = pack(w_la, la, "beta", HC)
        cosq = pack(w_la, la, "cos")
        sinq = pack(w_la, la, "sin")
        causal = pack(w_la, la, "causal")
        bv_lx = pack(w_la, la, "bv_lx")
        mask = pack(w_la, la, "mask")
        bq_lx = pack(w_la, la, "bq_lx")
        bk_lx = pack(w_la, la, "bk_lx")
        bdmask = pack(w_la, la, "bdmask")
        gate_w = pack(w_la, la, "gate_w").rearrange("p (k e) -> p k e", k=KD)
        alpha = pack(w_la, la, "alpha")
        tri = pack(w_la, la, "tri").rearrange("p (e j) -> p e j", e=8)
        fc2_b = pack(w_la, la, "fc2_b", 8)
        region = sb("region", [P, 24576])
        cursor = [0]

        def carve(rows, *shape, start=None):
            if start is not None:
                cursor[0] = start
            size = 1
            for s in shape:
                size *= s
            a = cursor[0]
            cursor[0] += size
            assert cursor[0] <= 24576
            v = region[0:rows, a:a + size]
            if len(shape) == 2:
                v = v.rearrange("p (a b) -> p a b", a=shape[0])
            if len(shape) == 3:
                v = v.rearrange("p (a b c) -> p a b c", a=shape[0], b=shape[1])
            return v

        Wsum = carve(64, D)
        kvlatT = carve(64, N)
        s1 = carve(P, NB)
        xc = carve(P, NB, HC)
        sq = carve(P, NB, HC)
        vl = carve(P, NB)
        rl = carve(P, NB)
        chT = carve(HC, N)
        t1 = carve(P, NB, 64)
        t2 = carve(P, NB, 64)
        v_la = carve(P, NB, HC)
        qT = carve(HC, N)
        kT = carve(HC, N)
        S = carve(P, NB, P)
        r1 = carve(P, NB)
        r2 = carve(P, NB)
        PT = carve(P, NB, P)
        oT = chT
        zT = kvlatT

        NH, FD, HD = 16, 64, 16
        CH = NH * FD // P
        AUG = 2 * (HD + 1)
        lx = T["lx"]
        w_lx = early[:, T["la_cols"]:T["la_cols"] + T["lx_cols"]]
        WqT = pack(w_lx, lx, "WqT").rearrange("p (k n) -> p k n", k=KD)
        WkT = pack(w_lx, lx, "WkT").rearrange("p (k n) -> p k n", k=KD)
        WvT = pack(w_lx, lx, "WvT").rearrange("p (k n) -> p k n", k=KD)
        WoT = pack(w_lx, lx, "WoT").rearrange("p (k n) -> p k n", k=KD)
        BDk = pack(w_lx, lx, "BDk")
        BDq = pack(w_lx, lx, "BDq")
        kx = carve(P, KD, N)
        qx = kx
        kp = carve(P, NB, NH * FD)
        qp = kp.rearrange("p b n -> p (b n)").rearrange("p (c n) -> p c n", c=CH)
        v_aug = carve(P, NB, NH * (HD + 1))
        v_aug_h = v_aug.rearrange("p b (h e) -> p b h e", e=HD + 1)
        kvm = carve(P, NB, NH * (HD + 1))
        KV_LATE = range(5, NB)
        a_x = H
        den = carve(P, NB, NH)
        rden = carve(P, NB, NH)
        aT = kx

        E = 8
        fc = early[:, T["la_cols"] + T["lx_cols"]:].rearrange("p (f w k n) -> p f w k n", f=2, w=2, k=KD)
        f1, f2 = fc[:, 0], fc[:, 1]
        f1b = sb("f1b", [P, 2, KD])
        lg = carve(P, NB, E, start=0)
        gm = carve(P, NB)
        pr = carve(P, NB, E)
        gs = carve(P, NB)
        gr = carve(P, NB)
        GT = carve(P, NB * E, E)
        GE = carve(P, NB * E, E)
        rank = carve(P, NB, E)
        comb = carve(P, NB, E)
        combT = carve(E, N)
        hT = carve(P, 2 * KD, N)

        KV, GRP, DH = 8, 4, 64
        QKV = (GRP + 2) * DH
        w_qkv = carve(P, KV, KD * QKV, start=cursor[0]).rearrange("p h (k n) -> p h k n", k=KD)
        b_qkv = carve(P, KV, QKV)
        WoT1 = carve(P, KV * 2, D)
        xT_t = carve(P, KD, P)
        raw = carve(P, QKV)
        straight = carve(P, 2, (GRP + 1) * DH)
        crossed = carve(P, 2, (GRP + 1) * DH)
        qk = carve(P, 2, (GRP + 2) * DH)
        v_t = carve(P, 4, DH)
        qkT1 = carve(P, 2, 3 * P)
        m_t = carve(P, 2, GRP)
        d_t = carve(P, 2, GRP)
        rd_t = carve(P, 2, GRP)
        oT1 = carve(P, 2, 2 * P)
        late = sb("late", [P, T["late_cols"]])
        lt = T["lt"]
        cos1 = pack(late, lt, "cos").rearrange("p (a c) -> p a c", a=2)
        sin1 = pack(late, lt, "sin").rearrange("p (a c) -> p a c", a=2)
        causal1 = pack(late, lt, "causal")
        kw = pack(late, lt, "kw")
        carrier = sem("carrier")
        kws = sb("kws", [P, KV * GRP])
        probs_zone = sb("probs_zone", [P, 4 * GRP * P])
        S1 = probs_zone[:, 0:2 * GRP * P].rearrange("p (r n) -> p r n", r=2)
        PT1 = probs_zone[:, 2 * GRP * P:].rearrange("p (r n) -> p r n", r=2)

        HX, DX = 16, 16
        PAIRS, SPL = HX // 2, 64
        kspT = sb("kspT", [P, NB, HX * SPL], BF16)
        k_parts = kspT[:].rearrange("p b (h c) -> p b h c", h=HX)
        kspT_j = kspT[:].rearrange("p b (j t) -> p j b t", j=PAIRS)
        v_int = sb("v_int", [P, NB, D], BF16)
        ident_b = sb("ident_b", [P, P], BF16)
        w_xx = sb("w_xx", [P, T["xx_cols"]])
        xx = T["xx"]
        Wq2 = pack(w_xx, xx, "Wq").rearrange("p (k n) -> p k n", k=KD)
        w_xk, xk = probs_zone[:, 0:T["xk_cols"]], T["xk"]
        Wk2 = pack(w_xk, xk, "Wk").rearrange("p (k n) -> p k n", k=KD)
        Wv2 = pack(w_xk, xk, "Wv").rearrange("p (k n) -> p k n", k=KD)
        Wp2 = pack(w_xx, xx, "Wp").rearrange("p (k n) -> p k n", k=KD)
        bq2, bk2, bv2 = pack(w_xx, xx, "bq"), pack(w_xk, xk, "bk"), pack(w_xk, xk, "bv")
        as_bf16 = lambda v: v.bitcast(BF16)
        qspT = as_bf16(early[:, 0:PAIRS * N // 2]).rearrange("p (j n) -> p j n", j=PAIRS)
        o = T["la_cols"]
        assert KD * N + 512 <= T["lx_cols"]
        vT2 = early[:, o:o + KD * N].rearrange("p (k n) -> p k n", k=KD)
        rest_k = early[:, o + KD * N:o + KD * N + 512]
        vq = as_bf16(probs_zone[:, 0:KD * N // 2]).rearrange("p (k n) -> p k n", k=KD)
        o = PAIRS * N // 2
        DVE_TURNS = (NB - 3, NB - 1)
        QB = 4
        q_rows = early[:, o:o + QB * D].rearrange("p (i h c) -> p i h c", i=QB, h=HX)
        q_parts = as_bf16(ctxT[:].rearrange("p k n -> p (k n)")).rearrange("p (i h c) -> p i h c", i=QB, h=HX)
        am = sb("am", [P, QB * HX])
        scl = sb("scl", [P, QB * HX])
        inv = sb("inv", [P, QB * HX])
        sq_all = sb("sq_all", [P, NB, HX])
        nsq_all = sb("nsq_all", [P, NB, HX])
        mx_t = sb("mx_t", [P, 2])
        nb_t = sb("nb_t", [P, 2])
        sums_t = sb("sums_t", [P, HX])
        rs_t = sb("rs_t", [P, HX])
        sv = sb("sv", [P, KD])
        rv = sb("rv", [P, KD])
        e_t = probs_zone[:].rearrange("p (r n) -> p r n", r=2)
        r_t = as_bf16(ctxT[:].rearrange("p k n -> p (k n)")).rearrange("p (r n) -> p r n", r=4)
        rT_t = as_bf16(early[:, o:o + N]).rearrange("p (r n) -> p r n", r=2)
        qT_t = as_bf16(early[:, o + N + 2 * D:o + 2 * N]).rearrange("p (j t) -> p j t", j=PAIRS)

        I2 = 512
        SLOT_TILES = (N + E * (P - 1)) // P
        W_gu = region[:, 0:E * KD * 2 * I2].rearrange("p (k e n) -> p k e n", k=KD, e=E)
        W_dn = region[:, E * KD * 2 * I2:E * (KD * 2 + I2 // P // 2) * I2].rearrange("p (k e n) -> p k e n", k=I2 // P, e=E)
        shared_zone = kspT[:].rearrange("p b n -> p (b n)").bitcast(F32)
        W_sh = shared_zone[:, 0:KD * 2 * I2].rearrange("p (k n) -> p k n", k=KD)
        W_sd = shared_zone[:, KD * 2 * I2:KD * 2 * I2 + I2 // P * D].rearrange("p (k n) -> p k n", k=I2 // P)
        shT = early[:, 0:I2 // P * N].rearrange("p (m n) -> p m n", m=I2 // P)
        slots_in = early[:, o:o + D]
        slots_T = early[:, o + D:o + 2 * D]
        gated = early[:, o + 2 * D:o + 4 * D]
        hid = early[:, o + 4 * D:o + 6 * D]
        hid_T = early[:, o + 6 * D:o + 8 * D]
        slots_out = early[:, o + 8 * D:o + 9 * D]
        at_ = o + 9 * D
        lg2, sel = (early[:, a:a + NB * E].rearrange("p (b e) -> p b e", b=NB) for a in (at_, at_ + NB * E))
        owner_c = early[:, at_ + 2 * NB * E:at_ + 2 * NB * E + SLOT_TILES * E].rearrange("p (t e) -> p t e", t=SLOT_TILES)
        silu_t = probs_zone[:, 0:I2]
        more2 = probs_zone[:, I2:2 * I2].rearrange("p (b j) -> p b j", j=E)
        same2 = probs_zone[:, 2 * I2:3 * I2].rearrange("p (b j) -> p b j", j=E)
        rank2 = probs_zone[:, 3 * I2:3 * I2 + NB * E].rearrange("p (b e) -> p b e", b=NB)
        xr = XB
        yg = ctxT[:].rearrange("p k (b n) -> p (k b) n", n=D)
        top2 = sb("top2", [P, NB])
        score2 = sb("score2", [P, NB])
        scan_a = sb("scan_a", [P, NB, E])
        scan_b = sb("scan_b", [P, NB, E])
        tiles_e = sb("tiles_e", [P, 3, E])
        pos = sb("pos", [P, NB, E])
        slot_f = sb("slot_f", [P, NB])
        slot_i = sb("slot_i", [P, NB], I32)
        owner_f = sb("owner_f", [P, SLOT_TILES])
        owner_i = sb("owner_i", [P, SLOT_TILES], I32)
        router = pack(late, lt, "router").rearrange("p (k e) -> p k e", k=KD)
        tri2 = pack(late, lt, "tri").rearrange("p (e j) -> p e j", e=E)
        earlier = pack(late, lt, "earlier")
        ones = pack(late, lt, "ones")
        tile_no = pack(late, lt, "tile_no")
        x_slots = nc.dram_tensor("x_slots", [SLOT_TILES * P, D], F32, kind="Internal").ap()
        y_slots = nc.dram_tensor("y_slots", [SLOT_TILES * P, D], F32, kind="Internal").ap()

        s_w = {n: sem("s_" + n) for n in ("w_first", "w_la", "w_lx", "xT0", "xT1", "x", "ctxT", "ident", "bias0", "late", "w_qkv", "WoT1", "w_xx", "w_gu", "w_dn", "w_sh")}
        s_out = sem("s_out")
        s_dve = sem("dve_step")
        x_ready = sem("x_ready")
        xb_ready = sem("xb_ready")
        var_ready = sem("var_ready")
        rstd_ready = sem("rstd_ready")
        wsum_ready = sem("wsum_ready")
        fc_loaded = [sem(f"fc_loaded{w}") for w in range(2)]
        s_sig = {}

        def signal(name):
            if name not in s_sig:
                s_sig[name] = sem(name)
            return s_sig[name]

        NCH = NB // 2
        rope1, neg_max1, exps1 = sem("rope1"), sem("neg_max1"), sem("exps1")
        probs1, turned1, tile_features = sem("probs1"), sem("turned1"), sem("tile_features")
        cmp_ready = sem("cmp_ready")

        def rank_experts(dve, then, score, more, same, before_, rank_, nth):
            for b in range(NB):
                of_j = score[:, b, :].unsqueeze(1).to_broadcast([P, E, E])
                of_e = score[:, b, :].unsqueeze(2).to_broadcast([P, E, E])
                dve.tensor_tensor(more[:, b * E:b * E + E, :], of_j, of_e, ALU.is_gt).then_inc(cmp_ready, 1)
                dve.tensor_tensor(same[:, b * E:b * E + E, :], of_j, of_e, ALU.is_equal).then_inc(cmp_ready, 1)
            dve.wait_ge(cmp_ready, 2 * NB * (nth + 1))
            same4 = same.rearrange("p (b e) j -> p b e j", b=NB)
            then(dve.tensor_tensor(same4, same4, before_.unsqueeze(1).to_broadcast([P, NB, E, E]), ALU.mult))
            then(dve.tensor_tensor(more, more, same, ALU.add))
            then(dve.tensor_reduce(rank_.rearrange("p b e -> p (b e)"), more, AX, ALU.add))

        w_scaled, raw_ready, recip_ready = sem("w_scaled"), sem("raw_ready"), sem("recip_ready")
        B_QKV, B_TR, B_S, B_PT, B_O, B_Y = 0, 1, 2, 4, 5, 6
        base = {}

        def head_steps(eng, step, tail):
            for h in range(KV):
                step(0, h, lambda back, h=h: h >= back, True)
            with eng.Fori(1, NB) as trip:
                for h in range(KV):
                    step(trip, h, lambda back: True, True)
            for h in range(tail):
                step(NB, h, lambda back, h=h: h < back, False)

        def grouped_attention_pe(pe):
            for k in range(8):
                base[k] = banks.n[k]
            pe.wait_ge(s_w["WoT1"], 16)
            pe.wait_ge(w_scaled, KV + 1)

            def step(trip, h, has, fresh):
                s = KV * trip + h
                if fresh:
                    if h == 0:
                        pe.wait_ge(tile_features, trip + 1)
                    pe.wait_ge(banks.free[B_QKV], base[B_QKV] + s)
                    for k in range(KD):
                        ins = pe.matmul(psum[:, B_QKV, 0:QKV], xT_t[:, k, :], w_qkv[:, h, k, :], start=(k == 0), stop=(k == KD - 1))
                    ins.then_inc(banks.full[B_QKV], 1)
                if has(1):
                    pe.wait_ge(rope1, 2 * s)
                    pe.wait_ge(banks.free[B_TR], base[B_TR] + s - 1)
                    for j in range(3):
                        ins = pe.transpose(psum[:, B_TR, j * P:j * P + P], qk[:, (h - 1) % 2, j * P:j * P + P], ident[:])
                    ins.then_inc(banks.full[B_TR], 1)
                if has(3):
                    pe.wait_ge(probs1, s - 2)
                    pe.wait_ge(banks.free[B_PT], base[B_PT] + s - 3)
                    for g in range(GRP):
                        ins = pe.transpose(psum[:, B_PT, g * P:g * P + P], S1[:, (h - 3) % 2, g * P:g * P + P], ident[:])
                    ins.then_inc(banks.full[B_PT], 1)
                if has(4):
                    hh = (h - 4) % KV
                    if hh == 0:
                        pe.wait_ge(banks.free[B_Y], base[B_Y] + trip)
                    pe.wait_ge(banks.free[B_O], base[B_O] + s - 3)
                    for j in range(2):
                        ins = pe.matmul(psum[:, B_Y, 0:D], oT1[:, (h - 4) % 2, j * P:j * P + P], WoT1[:, 2 * hh + j, :],
                                        start=(hh == 0 and j == 0), stop=(hh == KV - 1 and j == 1))
                    if hh == KV - 1:
                        ins.then_inc(banks.full[B_Y], 1)
                if has(1):
                    pe.wait_ge(banks.free[B_TR], base[B_TR] + s)
                    for par in range(2):
                        pe.wait_ge(banks.free[B_S + par], base[B_S + par] + s - 1)
                        r = slice(par * DH, par * DH + DH)
                        for j in range(2):
                            ins = pe.matmul(psum[:, B_S + par, j * P:j * P + P], qkT1[r, (h - 1) % 2, j * P:j * P + P],
                                            qkT1[r, (h - 1) % 2, 2 * P:3 * P], start=True, stop=True)
                        ins.then_inc(banks.full[B_S + par], 1)
                if has(3):
                    pe.wait_ge(banks.free[B_PT], base[B_PT] + s - 2)
                    pe.wait_ge(banks.free[B_O], base[B_O] + s - 3)
                    for par in range(2):
                        ins = pe.matmul(psum[par * DH:par * DH + DH, B_O, 0:2 * P], v_t[:, (h - 3) % 4, :],
                                        PT1[:, (h - 3) % 2, :].rearrange("p (j r t) -> p r j t", j=2, r=2)[:, par],
                                        start=True, stop=True)
                    ins.then_inc(banks.full[B_O], 1)

            head_steps(pe, step, 4)
            for k in range(6):
                banks.n[k] += NB * KV
            banks.n[B_Y] += NB
            banks.next = 0

        def grouped_attention_act(act):
            def step(trip, h, has, fresh):
                s = KV * trip + h
                if has(1):
                    act.wait_ge(banks.full[B_TR], base[B_TR] + s)
                    act.activation(qkT1[:, (h - 1) % 2, :], psum[:, B_TR, 0:3 * P], ACT.Copy).then_inc(banks.free[B_TR], 1)
                if has(3):
                    act.wait_ge(banks.full[B_PT], base[B_PT] + s - 2)
                    act.activation(PT1[:, (h - 3) % 2, :], psum[:, B_PT, :], ACT.Copy).then_inc(banks.free[B_PT], 1)
                    act.wait_ge(banks.full[B_O], base[B_O] + s - 2)
                    act.activation(oT1[:, (h - 3) % 2, :], psum[:, B_O, 0:2 * P], ACT.Copy).then_inc(banks.free[B_O], 1)
                if has(1):
                    act.wait_ge(neg_max1, s)
                    for g in range(GRP):
                        sl = S1[:, (h - 1) % 2, g * P:g * P + P]
                        ins = act.activation(sl, sl, ACT.Exp, bias=m_t[:, (h - 1) % 2, g:g + 1],
                                             accum_out=d_t[:, (h - 1) % 2, g:g + 1])
                    ins.then_inc(exps1, 1)

            head_steps(act, step, 3)

        def grouped_attention_dve(dve, then):
            def output(trip, b):
                dve.wait_ge(banks.full[B_Y], base[B_Y] + trip)
                dve.tensor_tensor(H[:, b, :].rearrange("p b n -> p (b n)"), psum[:, B_Y, 0:D],
                                  XB[:, b, :].rearrange("p b n -> p (b n)"), ALU.add).then_inc(banks.free[B_Y], 1)

            def step(trip, h, has, fresh):
                s = KV * trip + h
                if isinstance(trip, int) and trip == 0 and h == 0:
                    dve.wait_ge(*read(("xt", 2, 0)))
                    dve.tensor_scalar(xT_t, XT[:, :, 0:P], 1.0, None, ALU.mult).then_inc(tile_features, 1)
                if fresh:
                    dve.wait_ge(banks.full[B_QKV], base[B_QKV] + s + 1)
                    if has(1):
                        dve.wait_ge(turned1, 2 * s)
                    n = (GRP + 1) * DH
                    then(dve.tensor_tensor(raw[:, 0:n], psum[:, B_QKV, 0:n], b_qkv[:, h, 0:n], ALU.add), h, 1, trip)
                    dve.tensor_tensor(v_t[:, h % 4, :], psum[:, B_QKV, n:n + DH], b_qkv[:, h, n:n + DH], ALU.add)\
                       .then_inc(banks.free[B_QKV], 1)
                    rawv = raw[:, 0:n].rearrange("p (g a c) -> p g a c", g=GRP + 1, a=2)
                    if has(2):
                        dve.wait_ge(rope1, 2 * s - 2)
                    straight_v = straight[:, h % 2, :].rearrange("p (g a c) -> p g a c", g=GRP + 1, a=2)
                    crossed_v = crossed[:, h % 2, :].rearrange("p (g a c) -> p g a c", g=GRP + 1, a=2)
                    dve.tensor_tensor(straight_v, rawv, cos1.unsqueeze(1).to_broadcast([P, GRP + 1, 2, DH // 2]), ALU.mult)\
                       .then_inc(turned1, 1)
                    dve.tensor_tensor(crossed_v, rawv[:, :, ::-1, :], sin1.unsqueeze(1).to_broadcast([P, GRP + 1, 2, DH // 2]),
                                      ALU.mult).then_inc(turned1, 1)
                if fresh and h == KV - 1 and isinstance(trip, int):
                    dve.wait_ge(xb_ready, 3 * NCH)
                    for c in range(NCH):
                        dve.wait_ge(*read(("xt", 2, c)))
                if fresh and h == KV - 1:
                    src = XT_next[:, :, 0:P] if isinstance(trip, int) else XT_next[:, :, bass.ds(trip * P, P)]
                    dve.tensor_scalar(xT_t, src, 1.0, None, ALU.mult).then_inc(tile_features, 1)
                if has(1):
                    if has(3):
                        dve.wait_ge(banks.full[B_PT], base[B_PT] + s - 2)
                    for par in range(2):
                        dve.wait_ge(banks.full[B_S + par], base[B_S + par] + s)
                        dve.sem_inc(carrier, 1)
                        for j in range(2):
                            g = 2 * j + par
                            ins = dve.tensor_tensor_reduce(S1[:, (h - 1) % 2, g * P:g * P + P], psum[:, B_S + par, j * P:j * P + P],
                                                           causal1, 1.0, -3e38, ALU.add, ALU.max, m_t[:, (h - 1) % 2, g:g + 1])
                        ins.then_inc(banks.free[B_S + par], 1)
                    for par in range(2):
                        dve.wait_ge(banks.free[B_S + par], base[B_S + par] + s)
                    dve.tensor_scalar(m_t[:, (h - 1) % 2, :], m_t[:, (h - 1) % 2, :], -1.0, None, ALU.mult).then_inc(neg_max1, 1)
                if has(2):
                    dve.wait_ge(exps1, s - 1)
                    then(dve.reciprocal(rd_t[:, (h - 2) % 2, :], d_t[:, (h - 2) % 2, :]), h, 0, trip)
                    for g in range(GRP):
                        sl = S1[:, (h - 2) % 2, g * P:g * P + P]
                        ins = dve.tensor_scalar(sl, sl, rd_t[:, (h - 2) % 2, g:g + 1], None, ALU.mult)
                    ins.then_inc(probs1, 1)
                if h == 3 and not isinstance(trip, int):
                    output(trip, bass.ds(trip - 1, 1))

            dve.wait_ge(signal("spare_ready"), 1)
            head_steps(dve, step, 3)

            def last_output(c):
                if c == 0:
                    dve.wait_ge(banks.free[B_Y], base[B_Y] + NB - 1)
                if c == NCH - 1:
                    output(NB, slice(NB - 1, NB))
                    dve.wait_ge(banks.free[B_Y], base[B_Y] + NB)

            return last_output

        def grouped_attention_pool(pool):
            def step(trip, h, has, fresh):
                s = KV * trip + h
                if fresh:
                    pool.wait_ge(turned1, 2 * s + 2)
                    if has(2):
                        pool.wait_ge(banks.full[B_TR], base[B_TR] + s - 1)
                    n = (GRP + 1) * DH
                    pool.tensor_tensor(qk[:, h % 2, 0:n], straight[:, h % 2, :], crossed[:, h % 2, :], ALU.add)\
                        .then_inc(rope1, 1)
                    pool.tensor_tensor(qk[:, h % 2, n:n + DH], straight[:, h % 2, n - DH:n], crossed[:, h % 2, n - DH:n],
                                       ALU.add).then_inc(rope1, 1)

            head_steps(pool, step, 0)

        MAGIC = 1.5 * 2.0 ** 23
        LN255 = 5.541263545158426
        stats_ready = sem("quant_step")
        parts_ready, keys_step = sem("parts_ready"), sem("keys_step")
        vq_ready, wp_ready, qs_ready = sem("vq_ready"), sem("wp_ready"), sem("qs_ready")

        hv = lambda v: v.rearrange("p (i h c) -> p i h c", i=2, h=HX)
        per_head = lambda v, i: v[:, 0:i * HX].rearrange("p (i h) -> p i h", i=i).unsqueeze(3).to_broadcast([P, i, HX, DX])

        def rounded_rows(dve, then, rows, tiles, factor):
            n = tiles * HX
            then(dve.tensor_reduce(am[:, 0:n].rearrange("p (i h) -> p i h", i=tiles), rows, AX, ALU.max,
                                   apply_absolute_value=True))
            then(dve.tensor_scalar(scl[:, 0:n], am[:, 0:n], 1.0 / 127.0, 1e-8 / factor, ALU.mult, ALU.max))
            then(dve.reciprocal(inv[:, 0:n], scl[:, 0:n]))
            then(dve.tensor_tensor(rows, rows, per_head(inv, tiles), ALU.mult))
            then(dve.tensor_scalar(rows, rows, MAGIC, MAGIC, ALU.add, ALU.subtract))

        def quantise_queries(dve, count, q):
            def then(ins):
                count[0] += 1
                ins.then_inc(stats_ready, 1)
                dve.wait_ge(stats_ready, count[0])

            chunks = range(q * QB // 2, (q + 1) * QB // 2)
            for c in chunks:
                i = 2 * (c % (QB // 2))
                dve.wait_ge(*filled(("q2", c)))
                dve.tensor_tensor(q_rows[:, i:i + 2].rearrange("p i h c -> p i (h c)"),
                                  at(("q2", c)).rearrange("p (i n) -> p i n", i=2),
                                  bq2.unsqueeze(1).to_broadcast([P, 2, D]), ALU.add).then_inc(free_of(("q2", c)), 1)
            for c in chunks:
                dve.wait_ge(*read(("q2", c)))
            factor = DX ** -0.5
            rounded_rows(dve, then, q_rows, QB, factor)
            sl = slice(q * QB, (q + 1) * QB)
            dve.tensor_scalar(sq_all[:, sl, :].rearrange("p i h -> p (i h)"), scl[:], factor, None, ALU.mult)
            if q:
                dve.wait_ge(*filled(("qspT", q * QB - 1)))
            for i in range(QB):
                dve.tensor_scalar(q_parts[:, i, :, 0:3 * DX].rearrange("p h (r c) -> p h r c", r=3),
                                  q_rows[:, i].unsqueeze(2).to_broadcast([P, HX, 3, DX]), -127.0, 127.0,
                                  ALU.max, ALU.min).then_inc(parts_ready, 1)
            then(dve.tensor_scalar(nsq_all[:, sl, :].rearrange("p i h -> p (i h)"), scl[:], -factor, None, ALU.mult))

        K_STEPS = 12

        def quantise_keys(dve, trip, half):
            at_step = [trip * K_STEPS + (0 if half == 0 else 6)]

            def then(ins):
                at_step[0] = at_step[0] + 1
                ins.then_inc(keys_step, 1)
                dve.wait_ge(keys_step, at_step[0])

            chunk = bass.ds(trip * 2, 2)
            rows = XB[:, chunk, :].rearrange("p i (h c) -> p i h c", h=HX)
            if half == 0:
                rounded_rows(dve, then, rows, 2, 1.0)
                then(dve.tensor_scalar(rows, rows, -127.0, 127.0, ALU.max, ALU.min))
                return
            hi, mid, lo = (k_parts[:, chunk, :, r * DX:(r + 1) * DX] for r in range(3))
            then(dve.tensor_tensor(rows, rows, per_head(scl, 2), ALU.mult))
            then(dve.tensor_copy(hi, rows))
            then(dve.tensor_tensor(hv(rest_k), rows, hi, ALU.subtract))
            then(dve.tensor_copy(mid, hv(rest_k)))
            then(dve.tensor_tensor(rows, hv(rest_k), mid, ALU.subtract))
            then(dve.tensor_copy(lo, rows))

        def turn_parts(pe):
            for b in range(NB):
                claim_(pe, ("qspT", b))
                pe.wait_ge(parts_ready, b + 1)
                for j in range(PAIRS):
                    ins = pe.transpose(at(("qspT", b)).bitcast(BF16)[:, j * P:j * P + P],
                                       q_parts[:, b % QB, 2 * j:2 * j + 2, :].rearrange("p h c -> p (h c)"), ident_b[:])
                ins.then_inc(full_of(("qspT", b)), 1)

        def claim_(pe, key, count=1):
            for se, v in take(key, count):
                pe.wait_ge(se, v)

        def rows_of(pe, key, src, w):
            claim_(pe, key)
            c = key[-1]
            for i in range(2):
                for k in range(KD):
                    ins = pe.matmul(at(key)[:, i * D:i * D + D], src[:, k, (2 * c + i) * P:(2 * c + i + 1) * P], w[:, k, :],
                                    start=(k == 0), stop=(k == KD - 1))
            ins.then_inc(full_of(key), 1)

        def context_pe(pe):
            pe.wait_ge(s_w["w_xx"], 32)
            for c in range(NCH):
                rows_of(pe, ("k2", c), ctxT, Wk2)
            for m in range(KD):
                for n in range(G):
                    claim_(pe, ("v2", m, n))
                    for k in range(KD):
                        ins = pe.matmul(at(("v2", m, n)), Wv2[:, k, m * P:m * P + P], ctxT[:, k, n * 512:n * 512 + 512],
                                        start=(k == 0), stop=(k == KD - 1))
                    ins.then_inc(full_of(("v2", m, n)), 1)

        KEYS_FIRST, KEYS_LATER = range(NB // 2), range(NB // 2, NB)

        def turned_keys_pe(pe, tiles):
            pe.wait_ge(keys_step, K_STEPS * NCH)
            pe.wait_ge(signal("ident_b_ready"), 1)
            for b in tiles:
                claim_(pe, ("kspT", b))
                for j in range(PAIRS):
                    ins = pe.transpose(at(("kspT", b)).bitcast(BF16)[:, j * P:j * P + P], kspT[:, b, j * P:j * P + P], ident_b[:])
                ins.then_inc(full_of(("kspT", b)), 1)

        def turned_values_pe(pe):
            pe.wait_ge(vq_ready, KD)
            for q in range(2):
                claim_(pe, ("v_int", q))
                for i in range(4):
                    for k in range(KD):
                        ins = pe.transpose(at(("v_int", q)).bitcast(BF16)[:, (i * KD + k) * P:(i * KD + k + 1) * P],
                                           vq[:, k, (4 * q + i) * P:(4 * q + i + 1) * P], ident_b[:])
                ins.then_inc(full_of(("v_int", q)), 1)

        def context_act(act):
            for m in range(KD):
                for n in range(G):
                    act.wait_ge(*filled(("v2", m, n)))
                    act.activation(vT2[:, m, n * 512:n * 512 + 512], at(("v2", m, n)), ACT.Identity, bias=bv2[:, m:m + 1])\
                       .then_inc(free_of(("v2", m, n)), 1)

        def turned_keys_act(act, tiles):
            for b in tiles:
                act.wait_ge(*filled(("kspT", b)))
                act.activation(kspT[:, b, :], at(("kspT", b)).bitcast(BF16), ACT.Copy).then_inc(free_of(("kspT", b)), 1)

        def turned_values_act(act):
            for q in range(2):
                act.wait_ge(*filled(("v_int", q)))
                act.activation(v_int[:, 4 * q:4 * q + 4, :].rearrange("p b n -> p (b n)"), at(("v_int", q)).bitcast(BF16),
                               ACT.Copy).then_inc(free_of(("v_int", q)), 1)

        def context_dve(dve, count):
            def then(ins):
                count[0] += 1
                ins.then_inc(stats_ready, 1)
                dve.wait_ge(stats_ready, count[0])

            dve.wait_ge(s_w["w_xx"], 32)
            dve.tensor_copy(ident_b[:], ident[:]).then_inc(signal("ident_b_ready"), 1)
            for c in range(NCH):
                dve.wait_ge(*filled(("k2", c)))
                dve.tensor_tensor(XB[:, 2 * c:2 * c + 2, :], at(("k2", c)).rearrange("p (i n) -> p i n", i=2),
                                  bk2.unsqueeze(1).to_broadcast([P, 2, D]), ALU.add).then_inc(free_of(("k2", c)), 1)

        def values_dve(dve, count):
            def then(ins):
                count[0] += 1
                ins.then_inc(stats_ready, 1)
                dve.wait_ge(stats_ready, count[0])

            for m in range(KD):
                for n in range(G):
                    dve.wait_ge(*read(("v2", m, n)))
            then(dve.tensor_reduce(sv[:], vT2, AX, ALU.max, apply_absolute_value=True))
            then(dve.tensor_scalar(sv[:], sv[:], 1.0 / 127.0, 1e-8, ALU.mult, ALU.max))
            then(dve.reciprocal(rv[:], sv[:]))
            for k in range(KD):
                then(dve.tensor_scalar(vT2[:, k, :], vT2[:, k, :], rv[:, k:k + 1], MAGIC, ALU.mult, ALU.add))
                then(dve.tensor_scalar(vT2[:, k, :], vT2[:, k, :], MAGIC, -127.0, ALU.subtract, ALU.max))
                dve.tensor_scalar(vq[:, k, :], vT2[:, k, :], 127.0, None, ALU.min).then_inc(vq_ready, 1)
                dve.tensor_scalar(Wp2[:, k, :], Wp2[:, k, :], sv[:, k:k + 1], None, ALU.mult).then_inc(wp_ready, 1)

        def queries_pe(pe, c):
            pe.wait_ge(*read(("xt", 3, c)))
            rows_of(pe, ("q2", c), XT, Wq2)

        def queries_act(act):
            for q in range(2):
                act.wait_ge(*read(("v_int", q)))
            for b in [b for b in range(NB) if b not in DVE_TURNS]:
                act.wait_ge(*filled(("qspT", b)))
                act.activation(qspT[:, :, b * P:b * P + P], at(("qspT", b)).bitcast(BF16).rearrange("p (j t) -> p j t", j=PAIRS),
                               ACT.Copy).then_inc(free_of(("qspT", b)), 1)

        LT, LP = 3, 4
        OUT_STEPS = LP + 1, HX // 2 + LP + 1
        ROUND_FIRST = 320
        XS, XO = 0, 6
        rounded2, bias2, tile_queries, a_ready = sem("rounded2"), sem("bias2"), sem("tile_queries"), sem("a_ready")
        base2 = {}

        def turn_use(trip, h):
            return HX // 2 * trip + h // 2 + 1

        def scale_of(scales, trip, h):
            return scales[:, slice(0, 1) if isinstance(trip, int) else bass.ds(trip, 1), h]

        def before(trip, h, back):
            h -= back
            return (trip, h) if h >= 0 else (trip - 1, h + HX)

        def tile_steps(eng, step, last):
            for h in range(HX):
                step(0, h, lambda back, h=h: h >= back, True)
            with eng.Fori(1, NB) as trip:
                for h in range(HX):
                    step(trip, h, lambda back: True, True)
            for h in range(last):
                step(NB, h, lambda back, h=h: h < back, False)

        def cross_pe(pe):
            for k in range(8):
                base2[k] = banks.n[k]
            pe.wait_ge(wp_ready, KD)

            def step(trip, h, has, fresh):
                s = HX * trip + h
                if fresh:
                    if h % (HX // 2) == 0:
                        pe.wait_ge(tile_queries, 2 * trip + 1 + h // (HX // 2))
                    k = XS + 2 * (h % 2)
                    pe.wait_ge(banks.free[k], base2[k] + HX // 2 * trip + h // 2)
                    r = slice(h % 2 * SPL, h % 2 * SPL + SPL)
                    for n in range(G):
                        ins = pe.matmul(psum[:, k + n, :], qT_t[r, h // 2, :], kspT_j[r, h // 2, 4 * n:4 * n + 4, :],
                                        start=True, stop=True)
                    ins.then_inc(banks.full[k], 1)
                if has(LT):
                    t, hh = before(trip, h, LT)
                    k = 4 + hh % 2
                    pe.wait_ge(rounded2, s - LT + 1)
                    pe.wait_ge(banks.free[k], base2[k] + turn_use(t, hh) - 1)
                    for c in range(NB):
                        ins = pe.transpose(psum[:, k, :].bitcast(BF16)[:, c * P:c * P + P], r_t[:, hh % 4, c * P:c * P + P], ident_b[:])
                    ins.then_inc(banks.full[k], 1)
                if has(LP):
                    t, hh = before(trip, h, LP)
                    k = 4 + hh % 2
                    ko = XO + hh // (HX // 2)
                    pe.wait_ge(banks.free[k], base2[k] + turn_use(t, hh))
                    if hh % (HX // 2) == 0:
                        pe.wait_ge(banks.free[ko], base2[ko] + t)
                    for c in range(NB):
                        ins = pe.matmul(psum[:, ko, hh * DX:hh * DX + DX], rT_t[:, hh % 2, c * P:c * P + P],
                                        v_int[:, c, hh * DX:hh * DX + DX], start=(c == 0), stop=(c == NB - 1))
                    if hh % (HX // 2) == HX // 2 - 1:
                        ins.then_inc(banks.full[ko], 1)

            tile_steps(pe, step, LP)
            for k in (0, 2, 4, 5):
                banks.n[k] += NB * HX // 2
            for k in (6, 7):
                banks.n[k] += NB
            banks.next = 0
            for c in range(NCH + 1):
                if c < NCH:
                    claim_(pe, ("a2T", c))
                    pe.wait_ge(a_ready, 2 * (2 * c + 2))
                    for k in range(KD):
                        for i in range(2):
                            ins = pe.transpose(at(("a2T", c))[:, (2 * k + i) * P:(2 * k + i + 1) * P],
                                               H[:, 2 * c + i, k * P:k * P + P], ident[:])
                    ins.then_inc(full_of(("a2T", c)), 1)
                if c:
                    pe.wait_ge(*read(("a2T", c - 1)))
                    rows_of(pe, ("y", 4, c - 1), XT, Wp2)

        def cross_act(act):
            def step(trip, h, has, fresh):
                s = HX * trip + h
                if has(LT):
                    turned_copy(act, trip, h)
                if fresh:
                    act.wait_ge(bias2, s + 1)
                    if has(2):
                        act.wait_ge(rounded2, s - 1)
                    k = XS + 2 * (h % 2)
                    act.sem_inc(carrier, 1)
                    act.activation(e_t[:, h % 2, :], psum[:, k:k + 2, :].rearrange("p k n -> p (k n)"), ACT.Exp,
                                   bias=nb_t[:, h % 2:h % 2 + 1], scale=scale_of(sq_all, trip, h),
                                   accum_out=sums_t[:, h:h + 1]).then_inc(banks.free[k], 1)

            tile_steps(act, step, LT)
            for c in range(NCH):
                act.wait_ge(*filled(("a2T", c)))
                act.activation(XT[:, :, 2 * c * P:2 * c * P + 2 * P], at(("a2T", c)).rearrange("p (k n) -> p k n", k=KD),
                               ACT.Copy).then_inc(free_of(("a2T", c)), 1)

        def turned_copy(act, trip, h):
            t, hh = before(trip, h, LT)
            k = 4 + hh % 2
            act.wait_ge(banks.full[k], base2[k] + turn_use(t, hh))
            act.activation(rT_t[:, hh % 2, :], psum[:, k, :].bitcast(BF16), ACT.Copy).then_inc(banks.free[k], 1)

        def cross_dve(dve):
            next_qspT = qspT.rearrange("p j n -> p (j n)")[:, P:P + (PAIRS - 1) * N].rearrange("p (j n) -> p j n", n=N)

            def copy_queries(half, src):
                js = slice(half * PAIRS // 2, (half + 1) * PAIRS // 2)
                dve.tensor_scalar(qT_t[:, js], src[:, js], 1.0, None, ALU.mult).then_inc(tile_queries, 1)

            def output_half(t, half):
                ko = XO + half
                hs = slice(half * HX // 2, (half + 1) * HX // 2)
                dve.wait_ge(banks.full[ko], base2[ko] + t + 1)
                dve.reciprocal(rs_t[:, hs], sums_t[:, hs]).then_inc(qs_ready, 1)
                dve.wait_ge(qs_ready, 2 * t + half + 1)
                b = slice(t, t + 1) if isinstance(t, int) else bass.ds(t, 1)
                dve.tensor_tensor(H[:, b, half * P:half * P + P].rearrange("p b (h c) -> p (b h) c", c=DX),
                                  psum[:, ko, half * P:half * P + P].rearrange("p (h c) -> p h c", c=DX),
                                  rs_t[:, hs].unsqueeze(2).to_broadcast([P, HX // 2, DX]), ALU.mult).then_inc(banks.free[ko], 1)
                dve.wait_ge(banks.free[ko], base2[ko] + t + 1)
                dve.sem_inc(a_ready, 1)

            def step(trip, h, has, fresh):
                s = HX * trip + h
                first_tile = isinstance(trip, int) and trip == 0
                if first_tile and h == 0:
                    copy_queries(0, qspT[:, :, 0:P])
                    copy_queries(1, qspT[:, :, 0:P])
                if fresh and h == 2 and not first_tile:
                    copy_queries(1, qspT[:, :, bass.ds(trip * P, P)])
                if fresh and h == 10:
                    copy_queries(0, next_qspT[:, :, 0:P] if first_tile else next_qspT[:, :, bass.ds(trip * P, P)])
                if fresh:
                    k = XS + 2 * (h % 2)
                    dve.wait_ge(banks.full[k], base2[k] + HX // 2 * trip + h // 2 + 1)
                    dve.tensor_reduce(mx_t[:, h % 2:h % 2 + 1], psum[:, k:k + 2, :].rearrange("p k n -> p (k n)"), AX, ALU.max)\
                       .then_inc(maxed2, 1)
                if has(1):
                    t, hh = before(trip, h, 1)
                    if has(5) if fresh else True:
                        t5, h5 = before(trip, h, 5)
                        dve.wait_ge(banks.full[4 + h5 % 2], base2[4 + h5 % 2] + turn_use(t5, h5))
                    k = XS + 2 * (hh % 2)
                    dve.wait_ge(banks.free[k], base2[k] + HX // 2 * t + hh // 2 + 1)
                    dve.tensor_scalar(r_t[:, hh % 4, 0:ROUND_FIRST], e_t[:, hh % 2, 0:ROUND_FIRST], MAGIC, MAGIC, ALU.add, ALU.subtract)
                if fresh:
                    dve.wait_ge(maxed2, s + 1)
                    dve.tensor_scalar(nb_t[:, h % 2:h % 2 + 1], mx_t[:, h % 2:h % 2 + 1], scale_of(nsq_all, trip, h), LN255,
                                      ALU.mult, ALU.add).then_inc(bias2, 1)
                if has(1):
                    dve.tensor_scalar(r_t[:, hh % 4, ROUND_FIRST:], e_t[:, hh % 2, ROUND_FIRST:], MAGIC, MAGIC, ALU.add, ALU.subtract)\
                       .then_inc(rounded2, 1)
                if h == OUT_STEPS[1]:
                    output_half(trip, 0)
                if h == OUT_STEPS[0] and not first_tile:
                    output_half(trip - 1, 1)

            tile_steps(dve, step, OUT_STEPS[0] + 1)

        maxed2 = sem("maxed2")

        Z_X, Z_G, Z_U, Z_H, Z_Y = range(5)
        base3 = {}
        M2 = I2 // P
        scattered, slots_loaded, slots_stored = sem("scattered"), sem("slots_loaded"), sem("slots_stored")
        gathered = [sem(f"gathered{b}") for b in range(NB)]
        sel_ready, score_ready, xr_ready, sh_ready = sem("sel_ready"), sem("score_ready"), sem("xr_ready"), sem("sh_ready")
        slot_ready, owner_ready, hid_ready = sem("slot_ready"), sem("owner_ready"), sem("hid_ready")

        def slot_steps(eng, step):
            step(0, True, False)
            with eng.Fori(1, SLOT_TILES) as t:
                step(t, True, True)
            step(SLOT_TILES, False, True)

        def experts_pe(pe):
            pe.wait_ge(s_w["late"], 16)
            claim_(pe, "router")
            for b in range(NB):
                pe.wait_ge(*read(("xt", 4, b // 2)))
                for k in range(KD):
                    ins = pe.matmul(at("router")[:, b * E:b * E + E], XT[:, k, b * P:b * P + P], router[:, k, :],
                                    start=(k == 0), stop=(k == KD - 1))
            ins.then_inc(full_of("router"), 1)
            pe.wait_ge(s_w["w_sh"], 32)
            for n in range(G):
                for m in range(M2):
                    for part in range(2):
                        key = ("sh", part, m, n)
                        claim_(pe, key)
                        for k in range(KD):
                            ins = pe.matmul(at(key), W_sh[:, k, part * I2 + m * P:part * I2 + m * P + P],
                                            XT[:, k, n * 512:n * 512 + 512], start=(k == 0), stop=(k == KD - 1))
                        ins.then_inc(full_of(key), 1)
                    if n == 0 and m == 1:
                        claim_(pe, "pos")
                        pe.wait_ge(sel_ready, 1)
                        flat = lambda v: v.rearrange("p b e -> p (b e)")
                        pe.matmul(at("pos")[:, 0:NB * E], earlier, flat(sel[:]), start=True, stop=False)
                        pe.matmul(at("pos")[:, 0:NB * E], ones, flat(scan_a[:]), start=False, stop=True)
                        pe.matmul(at("pos")[:, NB * E:(NB + 1) * E], ones, scan_b[:, NB - 1, :], start=True, stop=True)\
                          .then_inc(full_of("pos"), 1)
            for k in range(8):
                base3[k] = banks.n[k]
            pe.wait_ge(s_w["w_gu"], 16)
            pe.wait_ge(s_w["w_dn"], 16)
            pe.wait_ge(owner_ready, 1)

            def turn_slots(t):
                pe.wait_ge(banks.free[Z_X], base3[Z_X] + t)
                pe.wait_ge(slots_loaded, 16 * t + 16)
                for k in range(KD):
                    ins = pe.transpose(psum[:, Z_X, k * P:k * P + P], slots_in[:, k * P:k * P + P], ident[:])
                ins.then_inc(banks.full[Z_X], 1)

            turn_slots(0)

            def owner_of(t):
                at_ = slice(t, t + 1) if isinstance(t, int) else bass.ds(t, 1)
                return pe.value_load(owner_i[0:1, at_], min_val=0, max_val=E - 1)

            def step(t, now, prev):
                if prev:
                    e_before = owner_of(t - 1)
                    pe.wait_ge(hid_ready, t)
                    pe.wait_ge(banks.free[Z_H], base3[Z_H] + t - 1)
                    for m in range(M2):
                        ins = pe.transpose(psum[:, Z_H, m * P:m * P + P], hid[:, m * P:m * P + P], ident[:])
                    ins.then_inc(banks.full[Z_H], 1)
                if now:
                    e = owner_of(t)
                    pe.wait_ge(banks.free[Z_X], base3[Z_X] + t + 1)
                    for part, k_ in ((0, Z_G), (1, Z_U)):
                        pe.wait_ge(banks.free[k_], base3[k_] + t)
                        for k in range(KD):
                            ins = pe.matmul(psum[:, k_, :], slots_T[:, k * P:k * P + P],
                                            W_gu[:, k, bass.ds(e, 1), part * I2:part * I2 + I2].rearrange("p e n -> p (e n)"),
                                            start=(k == 0), stop=(k == KD - 1))
                        ins.then_inc(banks.full[k_], 1)
                    if not isinstance(t, int) or t + 1 < SLOT_TILES:
                        turn_next(t)
                if prev:
                    pe.wait_ge(banks.free[Z_H], base3[Z_H] + t)
                    pe.wait_ge(banks.free[Z_Y], base3[Z_Y] + t - 1)
                    for m in range(M2):
                        ins = pe.matmul(psum[:, Z_Y, 0:D], hid_T[:, m * P:m * P + P],
                                        W_dn[:, m, bass.ds(e_before, 1), :].rearrange("p e n -> p (e n)"),
                                        start=(m == 0), stop=(m == M2 - 1))
                    ins.then_inc(banks.full[Z_Y], 1)

            def turn_next(t):
                turn_slots(t + 1)

            slot_steps(pe, step)
            for k in (Z_G, Z_U, Z_H, Z_Y):
                banks.n[k] += SLOT_TILES
            banks.n[Z_X] += SLOT_TILES + 1
            for c in range(NCH):
                for se, v in take(("ysh", c), bank=(5, 6, 7, Z_G)[c]):
                    pe.wait_ge(se, v)
                if c % 2 == 0:
                    pe.wait_ge(sh_ready, M2 * (c // 2 + 1))
                for i in range(2):
                    b = 2 * c + i
                    for m in range(M2):
                        ins = pe.matmul(at(("ysh", c))[:, i * D:i * D + D], shT[:, m, b * P:b * P + P], W_sd[:, m, :],
                                        start=(m == 0), stop=(m == M2 - 1))
                ins.then_inc(full_of(("ysh", c)), 1)

        def experts_act(act):
            act.wait_ge(score_ready, 1)
            act.activation(score2[:], top2[:], ACT.Sigmoid).then_inc(score_ready, 1)
            for n in range(G):
                for m in range(M2):
                    act.wait_ge(*filled(("sh", 0, m, n)))
                    if m or n:
                        act.wait_ge(sh_ready, n * M2 + m)
                    act.activation(silu_t, at(("sh", 0, m, n)), ACT.Silu).then_inc(free_of(("sh", 0, m, n)), 1)

            def step(t, now, prev):
                if now:
                    act.wait_ge(banks.full[Z_G], base3[Z_G] + t + 1)
                    act.activation(gated, psum[:, Z_G, :], ACT.Silu).then_inc(banks.free[Z_G], 1)
                    act.wait_ge(banks.full[Z_U], base3[Z_U] + t + 1)
                    slots_turned(t + 1)
                if prev:
                    act.wait_ge(banks.full[Z_Y], base3[Z_Y] + t)
                    act.wait_ge(slots_stored, 16 * t)
                    act.activation(slots_out, psum[:, Z_Y, 0:D], ACT.Copy).then_inc(banks.free[Z_Y], 1)

            def slots_turned(t):
                act.wait_ge(banks.full[Z_X], base3[Z_X] + t + 1)
                act.activation(slots_T, psum[:, Z_X, 0:D], ACT.Copy).then_inc(banks.free[Z_X], 1)

            slots_turned(0)
            slot_steps(act, step)

        def experts_dve(dve, then):
            dve.wait_ge(*filled("router"))
            flat = lambda v: v.rearrange("p b e -> p (b e)")
            dve.tensor_copy(flat(lg2[:]), at("router")[:, 0:NB * E]).then_inc(free_of("router"), 1)
            dve.wait_ge(*read("router"))
            dve.tensor_reduce(top2[:], lg2[:], AX, ALU.max).then_inc(score_ready, 1)
            rank_experts(dve, then, lg2[:], more2, same2, tri2, rank2, 1)
            then(dve.tensor_scalar(sel[:], rank2, 0.5, None, ALU.is_lt))
            then(dve.tensor_copy(scan_a[:, 0:1, :], sel[:, 0:1, :]))
            then(dve.tensor_tensor(scan_a[:, 1:NB, :], sel[:, 1:NB, :], sel[:, 0:NB - 1, :], ALU.add))
            then(dve.tensor_copy(scan_b[:, 0:2, :], scan_a[:, 0:2, :]))
            then(dve.tensor_tensor(scan_b[:, 2:NB, :], scan_a[:, 2:NB, :], scan_a[:, 0:NB - 2, :], ALU.add))
            then(dve.tensor_copy(scan_a[:, 0:4, :], scan_b[:, 0:4, :]))
            then(dve.tensor_tensor(scan_a[:, 4:NB, :], scan_b[:, 4:NB, :], scan_b[:, 0:NB - 4, :], ALU.add))
            then(dve.tensor_copy(scan_b[:], scan_a[:]))
            dve.tensor_tensor(scan_a[:], scan_b[:], sel[:], ALU.subtract).then_inc(sel_ready, 1)
            dve.wait_ge(*filled("pos"))
            then(dve.tensor_copy(flat(pos[:]), at("pos")[:, 0:NB * E]))
            dve.tensor_scalar(tiles_e[:, 0, :], at("pos")[:, NB * E:(NB + 1) * E], 1.0 / P, (P - 1.0) / P - 0.5 + 0.5 / P,
                              ALU.mult, ALU.add).then_inc(free_of("pos"), 1)
            dve.wait_ge(*read("pos"))
            then(dve.tensor_scalar(tiles_e[:, 0, :], tiles_e[:, 0, :], MAGIC, MAGIC, ALU.add, ALU.subtract))
            src, dst = 0, 1
            for d in (1, 2, 4):
                then(dve.tensor_copy(tiles_e[:, dst, 0:d], tiles_e[:, src, 0:d]))
                then(dve.tensor_tensor(tiles_e[:, dst, d:E], tiles_e[:, src, d:E], tiles_e[:, src, 0:E - d], ALU.add))
                src, dst = dst, (2 if dst == 1 else 1)
            upto, start = src, dst
            then(dve.tensor_tensor(tiles_e[:, start, :], tiles_e[:, upto, :], tiles_e[:, 0, :], ALU.subtract))
            then(dve.scalar_tensor_tensor(pos[:], tiles_e[:, start, :].unsqueeze(1).to_broadcast([P, NB, E]), float(P), pos[:],
                                          ALU.mult, ALU.add))
            then(dve.tensor_tensor(pos[:], pos[:], sel[:], ALU.mult))
            then(dve.tensor_reduce(slot_f[:], pos[:], AX, ALU.add))
            dve.tensor_copy(slot_i[:], slot_f[:]).then_inc(slot_ready, 1)
            then(dve.tensor_tensor(owner_c[:], tiles_e[:, upto, :].unsqueeze(1).to_broadcast([P, SLOT_TILES, E]),
                                   tile_no.unsqueeze(2).to_broadcast([P, SLOT_TILES, E]), ALU.is_le))
            then(dve.tensor_reduce(owner_f[:], owner_c[:], AX, ALU.add))
            dve.tensor_scalar(owner_i[:], owner_f[:], E - 1.0, None, ALU.min).then_inc(owner_ready, 1)
            dve.wait_ge(score_ready, 2)
            for b in range(NB):
                dve.tensor_scalar(xr[:, b, :], X[:, b, :], score2[:, b:b + 1], None, ALU.mult).then_inc(xr_ready, 1)
            for n in range(G):
                for m in range(M2):
                    dve.wait_ge(*read(("sh", 0, m, n)))
                    dve.wait_ge(*filled(("sh", 1, m, n)))
                    dve.tensor_tensor(shT[:, m, n * 512:n * 512 + 512], silu_t, at(("sh", 1, m, n)), ALU.mult)\
                       .then_inc(free_of(("sh", 1, m, n)), 1)
                    dve.wait_ge(*read(("sh", 1, m, n)))
                    dve.sem_inc(sh_ready, 1)
            def step(t, now, prev):
                if prev:
                    dve.wait_ge(banks.full[Z_H], base3[Z_H] + t)
                    dve.tensor_scalar(hid_T, psum[:, Z_H, :], 1.0, None, ALU.mult).then_inc(banks.free[Z_H], 1)
                if now:
                    dve.wait_ge(banks.free[Z_G], base3[Z_G] + t + 1)
                    dve.wait_ge(banks.full[Z_U], base3[Z_U] + t + 1)
                    dve.tensor_tensor(hid, gated, psum[:, Z_U, :], ALU.mult).then_inc(banks.free[Z_U], 1)
                    dve.wait_ge(banks.free[Z_U], base3[Z_U] + t + 1)
                    dve.sem_inc(hid_ready, 1)

            slot_steps(dve, step)

            def add_experts(c):
                dve.wait_ge(*filled(("ysh", c)))
                dve.tensor_tensor(H[:, 2 * c:2 * c + 2, :].rearrange("p b n -> p (b n)"), at(("ysh", c)),
                                  X[:, 2 * c:2 * c + 2, :].rearrange("p b n -> p (b n)"), ALU.add)\
                   .then_inc(free_of(("ysh", c)), 1)
                dve.wait_ge(*read(("ysh", c)))
                for b in (2 * c, 2 * c + 1):
                    dve.wait_ge(gathered[b], 16)
                    dve.tensor_tensor(H[:, b, :], H[:, b, :], yg[:, b, :], ALU.add).then_inc(signal("summed"), 1)
                dve.wait_ge(signal("summed"), 2 * c + 2)

            return add_experts

        def experts_pool(pool):
            pool.wait_ge(slot_ready, 1)
            pool.wait_ge(slots_stored, 16)
            for b in range(NB):
                pool.wait_ge(xr_ready, b + 1)
                pool.indirect_dma_start(x_slots, bass.IndirectOffsetOnAxis(ap=slot_i[:, b:b + 1], axis=0), xr[:, b, :], None)\
                    .then_inc(scattered, 16)
            pool.wait_ge(slots_stored, 16 + 16 * SLOT_TILES)
            for b in range(NB):
                pool.indirect_dma_start(yg[:, b, :], None, y_slots, bass.IndirectOffsetOnAxis(ap=slot_i[:, b:b + 1], axis=0))\
                    .then_inc(gathered[b], 16)

        def experts_sp(sp):
            sp.wait_ge(scattered, 16 * NB)
            for t in range(SLOT_TILES + 1):
                if t:
                    sp.wait_ge(banks.full[Z_X], base3[Z_X] + t)
                row = min(t, SLOT_TILES - 1) * P
                sp.dma_start(slots_in, x_slots[row:row + P, :]).then_inc(slots_loaded, 16)
                if t >= 2:
                    store_slots(sp, t - 2)
            store_slots(sp, SLOT_TILES - 1)

        def store_slots(sp, t):
            sp.wait_ge(banks.free[Z_Y], base3[Z_Y] + t + 1)
            sp.dma_start(y_slots[t * P:t * P + P, :], slots_out).then_inc(slots_stored, 16)

        block = ctx.enter_context(nc.Block())

        @block.tensor
        def _(pe):
            def mm(key, j, cols, pairs, last=False, rows=P, start=True):
                for i, (l, r) in enumerate(pairs):
                    ins = pe.matmul(at(key, j)[0:rows, cols], l, r, start=(i == 0), stop=(i == len(pairs) - 1))
                if last:
                    ins.then_inc(full_of(key, j), 1)

            def claim(key, count=1):
                for s, v in take(key, count):
                    pe.wait_ge(s, v)

            pe.wait_ge(s_w["w_first"], 16)
            for n in range(G):
                pe.wait_ge(s_w[f"xT{n}"], 16)
                claim(("lat", n))
                mm(("lat", n), 0, slice(0, 512), [(WkvT[:, k, :], XT[:, k, n * 512:n * 512 + 512]) for k in range(KD)], True, 64)
            claim("c")
            for n in range(G):
                pe.wait_ge(*read(("lat", n)))
            for b in range(NB):
                mm("c", 0, slice(b * HC, b * HC + HC), [(kvlatT[:, b * P:b * P + P], WcT)], b == NB - 1)

            pe.wait_ge(s_w["w_la"], 16)
            pe.wait_ge(s_w["w_lx"], 16)
            pe.wait_ge(s_w["ctxT"], 16)
            for m in range(KD):
                for n in range(G):
                    claim(("kx", m, n))
                    mm(("kx", m, n), 0, slice(0, 512),
                       [(WkT[:, k, m * P:m * P + P], ctxT[:, k, n * 512:n * 512 + 512]) for k in range(KD)], True)
            pe.wait_ge(s_w["ident"], 16)
            claim("cT", G)
            pe.wait_ge(signal("cn_ready"), 1)
            for b in range(NB):
                ins = pe.transpose(span("cT")[0:HC, b * P:b * P + P], xc[:, b, :], ident[:])
                if b % 4 == 3:
                    ins.then_inc(full_of("cT", b // 4), 1)
            for b in range(NB // 2):
                claim(("v", b))
                for i in range(2):
                    mm(("v", b), 0, slice(i * D, i * D + D),
                       [(ctxT[:, k, (2 * b + i) * P:(2 * b + i + 1) * P], WvT[:, k, :]) for k in range(KD)], i == 1)
            for j in range(2):
                pe.wait_ge(*read("cT", j))
            for j in range(3):
                claim(("qkv", j))
                bs = range(3 * j, min(NB, 3 * j + 3))
                for b in bs:
                    mm(("qkv", j), 0, slice((b - 3 * j) * 160, (b - 3 * j) * 160 + 160),
                       [(chT[:, b * P:b * P + P], Wqkv)], b == bs[-1])
            for m in range(KD):
                for n in range(G):
                    pe.wait_ge(*read(("kx", m, n)))
            for b in range(NB):
                for h in range(2):
                    claim(("kp", b, h))
                    mm(("kp", b, h), 0, slice(0, 512), [(kx[:, h, b * P:b * P + P], BDk)], True)
                if b == 3:
                    pe.wait_ge(signal("rope_ready"), 1)
                    for which in range(2):
                        claim(("qkT", which), 2)
                        for c in range(NB):
                            ins = pe.transpose(span(("qkT", which))[0:HC, c * P:c * P + P],
                                               t1[:, c, which * HC:which * HC + HC], ident[:])
                            if c % 4 == 3:
                                ins.then_inc(full_of(("qkT", which), c // 4), 1)
            for which in range(2):
                for j in range(2):
                    pe.wait_ge(*read(("qkT", which), j))
            claim("S", 2)
            for b in range(NB):
                mm("S", b // 4, slice(b % 4 * P, b % 4 * P + P), [(qT[:, b * P:b * P + P], kT[:, b * P:b * P + P])], b % 4 == 3)
            pe.wait_ge(signal("values_masked"), 1)

            def keys_times_values(b):
                claim(("kv", b))
                for h in range(2):
                    pe.wait_ge(*read(("kp", b, h)))
                for c in range(CH):
                    mm(("kv", b), 0, slice(c * AUG, c * AUG + AUG),
                       [(kp[:, b, c * P:c * P + P], v_aug[:, b, c * AUG:c * AUG + AUG])], c == CH - 1)

            keys_times_values(0)
            keys_times_values(1)
            claim("PT", 2)
            pe.wait_ge(signal("P_ready"), 1)
            for b in range(NB):
                ins = pe.transpose(span("PT")[:, b * P:b * P + P], S[:, b, :], ident[:])
                if b % 4 == 3:
                    ins.then_inc(full_of("PT", b // 4), 1)
            keys_times_values(2)
            claim("oT", 2)
            for j in range(3):
                pe.wait_ge(*read(("qkv", j)))
            for j in range(2):
                pe.wait_ge(*read("PT", j))
            for b in range(NB):
                mm("oT", b // 4, slice(b % 4 * P, b % 4 * P + P), [(v_la[:, b, :], PT[:, b, :])], b % 4 == 3, HC)
            keys_times_values(3)
            for n in range(G):
                claim(("zT", n))
                pe.wait_ge(*read("oT", n))
                mm(("zT", n), 0, slice(0, 512), [(Wc2lT, oT[:, n * 512:n * 512 + 512])], True, 64)
            keys_times_values(4)
            for n in range(G):
                pe.wait_ge(*read(("zT", n)))
            pe.wait_ge(wsum_ready, 1)
            for c in range(NCH):
                claim(("y", 0, c))
                for i in range(2):
                    b = 2 * c + i
                    mm(("y", 0, c), 0, slice(i * D, i * D + D), [(zT[:, b * P:b * P + P], Wsum)], i == 1)
            for b in KV_LATE:
                keys_times_values(b)

            def to_features(layer, behind=None):
                for c in range(NCH):
                    claim(("xt", layer, c))
                    pe.wait_ge(x_ready, layer * NB + 2 * c + 2)
                    for i in range(2):
                        for k in range(KD):
                            ins = pe.transpose(at(("xt", layer, c))[:, (2 * i + k) * P:(2 * i + k + 1) * P],
                                               X[:, 2 * c + i, k * P:k * P + P], ident[:])
                    ins.then_inc(full_of(("xt", layer, c)), 1)
                    if behind and c:
                        behind(c - 1)
                if behind:
                    behind(NCH - 1)

            to_features(0)
            for c in range(NCH):
                pe.wait_ge(*read(("xt", 0, c)))
            for m in range(KD):
                for n in range(G):
                    claim(("qx", m, n))
                    mm(("qx", m, n), 0, slice(0, 512),
                       [(WqT[:, k, m * P:m * P + P], XT[:, k, n * 512:n * 512 + 512]) for k in range(KD)], True)
            for n in range(G):
                for m in range(KD):
                    pe.wait_ge(*read(("qx", m, n)))
                for c in range(CH):
                    r = c % 4 * 32
                    claim(("qp", c, n))
                    mm(("qp", c, n), 0, slice(0, 512), [(BDq[r:r + 32, :], qx[r:r + 32, c // 4, n * 512:n * 512 + 512])], True)
            for b in range(NB):
                claim(("ox", b))
                pe.wait_ge(*read(("kv", b)))
                for c in range(CH):
                    pe.wait_ge(*read(("qp", c, b // 4)))
                for c in range(CH):
                    mm(("ox", b), 0, slice(c * AUG, c * AUG + AUG),
                       [(qp[:, c, b * P:b * P + P], kvm[:, b, c * AUG:c * AUG + AUG])], c == CH - 1)
            for c in range(NCH):
                claim(("aT", c))
                for i in range(2):
                    pe.wait_ge(*read(("ox", 2 * c + i)))
                for i in range(2):
                    for k in range(KD):
                        ins = pe.transpose(at(("aT", c))[:, (2 * i + k) * P:(2 * i + k + 1) * P],
                                           a_x[:, 2 * c + i, k * P:k * P + P], ident[:])
                ins.then_inc(full_of(("aT", c)), 1)
            for c in range(NCH):
                claim(("y", 1, c))
                pe.wait_ge(*read(("aT", c)))
                for i in range(2):
                    b = 2 * c + i
                    mm(("y", 1, c), 0, slice(i * D, i * D + D),
                       [(aT[:, k, b * P:b * P + P], WoT[:, k, :]) for k in range(KD)], i == 1)
            to_features(1)
            for c in range(NCH):
                pe.wait_ge(*read(("xt", 1, c)))
            claim("gate")
            for b in range(NB):
                mm("gate", 0, slice(b * E, b * E + E), [(XT[:, k, b * P:b * P + P], gate_w[:, k, :]) for k in range(KD)], b == NB - 1)
            context_pe(pe)
            claim("combT", 2)
            pe.wait_ge(signal("comb_ready"), 1)
            for b in range(NB):
                ins = pe.transpose(span("combT")[0:E, b * P:b * P + P], comb[:, b, :], ident[:])
                if b % 4 == 3:
                    ins.then_inc(full_of("combT", b // 4), 1)
            for j in range(2):
                pe.wait_ge(*read("combT", j))
            for c in range(NCH):
                claim(("yb", c))
                for i in range(2):
                    b = 2 * c + i
                    mm(("yb", c), 0, slice(i * D, i * D + D), [(combT[:, b * P:b * P + P], fc2_b)], i == 1)
            banks.next = 0
            with pe.Fori(0, E // 2) as trip:
                for w in range(2):
                    pe.wait_ge(fc_loaded[w], 48 * trip + 48)
                    for m in range(KD):
                        for n in range(G):
                            key = ("h1", w, m, n)
                            for se, v in take(key, trip=trip, per=2):
                                pe.wait_ge(se, v)
                            mm(key, 0, slice(0, 512),
                               [(f1[:, w, k, m * P:m * P + P], XT[:, k, n * 512:n * 512 + 512]) for k in range(KD)], True)
                for w in range(2):
                    for c in range(NCH):
                        key = ("y2", w, c)
                        for se, v in take(key, trip=trip, per=2):
                            pe.wait_ge(se, v)
                        if c == 0:
                            for m in range(KD):
                                for n in range(G):
                                    pe.wait_ge(*read(("h1", w, m, n), trip=trip))
                        for i in range(2):
                            b = 2 * c + i
                            mm(key, 0, slice(i * D, i * D + D),
                               [(hT[:, w * KD + k, b * P:b * P + P], f2[:, w, k, :]) for k in range(KD)], i == 1)
            banks.looped(E // 2, 2)
            turned_keys_pe(pe, KEYS_FIRST)
            turned_values_pe(pe)
            to_features(2)
            grouped_attention_pe(pe)
            to_features(3, lambda c: queries_pe(pe, c))
            turned_keys_pe(pe, KEYS_LATER)
            turn_parts(pe)
            cross_pe(pe)
            to_features(4)
            experts_pe(pe)

        @block.scalar
        def _(act):
            act.dma_start(XT[:, :, 512:1024], W["xT"][:, :, 512:1024]).then_inc(s_w["xT1"], 16)
            act.dma_start(ctxT[:], W["ctxT"]).then_inc(s_w["ctxT"], 16)
            act.dma_start(ident[:], W["ident"]).then_inc(s_w["ident"], 16)
            act.dma_start(biases[:], W["biases"]).then_inc(s_w["bias0"], 16)

            def from_features(layer):
                for c in range(NCH):
                    act.wait_ge(*filled(("xt", layer, c)))
                    act.activation(XT[:, :, 2 * c * P:(2 * c + 2) * P].rearrange("p k (i t) -> p i k t", i=2),
                                   at(("xt", layer, c)).rearrange("p (i k t) -> p i k t", i=2, k=KD),
                                   ACT.Copy).then_inc(free_of(("xt", layer, c)), 1)

            for n in range(G):
                act.wait_ge(*filled(("lat", n)))
                act.activation(kvlatT[:, n * 512:n * 512 + 512], at(("lat", n))[0:64, :], ACT.Copy)\
                   .then_inc(free_of(("lat", n)), 1)
            for m in range(KD):
                for n in range(G):
                    act.wait_ge(*filled(("kx", m, n)))
                    act.activation(kx[:, m, n * 512:n * 512 + 512], at(("kx", m, n)), ACT.Identity, bias=bk_lx[:, m:m + 1])\
                       .then_inc(free_of(("kx", m, n)), 1)
            for j in range(2):
                act.wait_ge(*filled("cT", j))
                act.activation(chT[:, j * 512:j * 512 + 512], at("cT", j)[0:HC, :], ACT.Identity,
                               bias=beta, scale=gamma).then_inc(free_of("cT", j), 1)
            def key_features(b):
                act.wait_ge(*filled(("kp", b, 1)))
                act.activation(kp[:, b, 512:1024], at(("kp", b, 1)), ACT.Relu).then_inc(free_of(("kp", b, 1)), 1)

            for b in range(NB // 2):
                key_features(b)
            for which, dst in enumerate((qT, kT)):
                for j in range(2):
                    act.wait_ge(*filled(("qkT", which), j))
                    act.activation(dst[:, j * 512:j * 512 + 512], at(("qkT", which), j)[0:HC, :], ACT.Copy)\
                       .then_inc(free_of(("qkT", which), j), 1)
            for b in range(NB // 2, NB):
                key_features(b)
            act.wait_ge(signal("S_less_max"), 1)
            act.activation(S, S, ACT.Exp).then_inc(signal("S_exp"), 1)
            for j in range(2):
                act.wait_ge(*filled("PT", j))
                act.activation(PT[:, 4 * j:4 * j + 4, :].rearrange("p b t -> p (b t)"), at("PT", j), ACT.Copy)\
                   .then_inc(free_of("PT", j), 1)
            for j in range(2):
                act.wait_ge(*filled("oT", j))
                act.activation(oT[:, j * 512:j * 512 + 512], at("oT", j)[0:HC, :], ACT.Copy).then_inc(free_of("oT", j), 1)
            for n in range(G):
                act.wait_ge(*filled(("zT", n)))
                act.activation(zT[:, n * 512:n * 512 + 512], at(("zT", n))[0:64, :], ACT.Copy).then_inc(free_of(("zT", n)), 1)
            from_features(0)
            for m in range(KD):
                for n in range(G):
                    act.wait_ge(*filled(("qx", m, n)))
                    act.activation(qx[:, m, n * 512:n * 512 + 512], at(("qx", m, n)), ACT.Identity, bias=bq_lx[:, m:m + 1])\
                       .then_inc(free_of(("qx", m, n)), 1)
            for n in range(G):
                for c in range(0, CH, 2):
                    act.wait_ge(*filled(("qp", c, n)))
                    act.activation(qp[:, c, n * 512:n * 512 + 512], at(("qp", c, n)), ACT.Relu)\
                       .then_inc(free_of(("qp", c, n)), 1)
            for c in range(NCH):
                act.wait_ge(*filled(("aT", c)))
                act.activation(aT[:, :, 2 * c * P:(2 * c + 2) * P].rearrange("p k (i t) -> p i k t", i=2),
                               at(("aT", c)).rearrange("p (i k t) -> p i k t", i=2, k=KD),
                               ACT.Copy).then_inc(free_of(("aT", c)), 1)
            from_features(1)
            act.wait_ge(*read("gate"))
            act.activation(pr, lg, ACT.Exp).then_inc(signal("gate_exp"), 1)
            context_act(act)
            for j in range(2):
                act.wait_ge(*filled("combT", j))
                act.activation(combT[:, j * 512:j * 512 + 512], at("combT", j)[0:E, :], ACT.Copy)\
                   .then_inc(free_of("combT", j), 1)
            with act.Fori(0, E // 2) as trip:
                for w in range(2):
                    act.wait_ge(*filled(("y2", w, NCH - 1), trip=trip - 1))
                    for m in range(KD):
                        for n in range(G):
                            act.wait_ge(*filled(("h1", w, m, n), trip=trip))
                            act.activation(hT[:, w * KD + m, n * 512:n * 512 + 512], at(("h1", w, m, n)), ACT.Gelu,
                                           bias=f1b[:, w, m:m + 1]).then_inc(free_of(("h1", w, m, n)), 1)
            turned_keys_act(act, KEYS_FIRST)
            turned_values_act(act)
            from_features(2)
            grouped_attention_act(act)
            from_features(3)
            turned_keys_act(act, KEYS_LATER)
            queries_act(act)
            cross_act(act)
            from_features(4)
            experts_act(act)

        @block.vector
        def _(dve):
            steps = [0]

            def then(ins):
                steps[0] += 1
                ins.then_inc(s_dve, 1)
                dve.wait_ge(s_dve, steps[0])

            def both(*instructions):
                for ins in instructions:
                    steps[0] += 1
                    ins.then_inc(s_dve, 1)
                dve.wait_ge(s_dve, steps[0])

            def stats(c):
                both(*[dve.bn_stats(st[:, b, :], H[:, b, :]) for b in (2 * c, 2 * c + 1)])
                both(*[dve.bn_aggr(mv[:, b, :], st[:, b, :]) for b in (2 * c, 2 * c + 1)])
                dve.tensor_scalar(ve[:, 2 * c:2 * c + 2], mv[:, 2 * c:2 * c + 2, 1], LN_EPS, None, ALU.add)\
                   .then_inc(var_ready, 1)

            def normalise(layer, c):
                dve.wait_ge(rstd_ready, layer * NCH + c + 1)
                for b in (2 * c, 2 * c + 1):
                    dve.tensor_scalar(X[:, b, :], H[:, b, :], mv[:, b, 0:1], rstd[:, b:b + 1], ALU.subtract, ALU.mult)\
                       .then_inc(x_ready, 1)

            def add_residual(layer, nth, c):
                dve.wait_ge(*filled(("y", layer, c)))
                dve.wait_ge(xb_ready, nth * NCH + c + 1)
                dve.tensor_tensor(H[:, 2 * c:2 * c + 2, :].rearrange("p b n -> p (b n)"), at(("y", layer, c)),
                                  XB[:, 2 * c:2 * c + 2, :].rearrange("p b n -> p (b n)"), ALU.add)\
                   .then_inc(free_of(("y", layer, c)), 1)
                dve.wait_ge(*read(("y", layer, c)))

            def norm_layer(layer, chunk_before_norm=None):
                for c in range(NCH):
                    if chunk_before_norm:
                        chunk_before_norm(c)
                    stats(c)
                    if c:
                        normalise(layer, c - 1)
                normalise(layer, NCH - 1)

            dve.wait_ge(s_w["w_la"], 16)
            dve.wait_ge(*filled("c"))
            cp = at("c")[:, 0:NB * HC].rearrange("p (b n) -> p b n", b=NB)
            then(dve.tensor_reduce(s1, cp, AX, ALU.add))
            dve.scalar_tensor_tensor(xc, s1.unsqueeze(2).to_broadcast([P, NB, HC]), -1.0 / HC, cp, ALU.mult, ALU.add)\
               .then_inc(free_of("c"), 1)
            dve.wait_ge(*read("c"))
            then(dve.tensor_tensor(sq, xc, xc, ALU.mult))
            then(dve.tensor_reduce(vl, sq, AX, ALU.add))
            dve.tensor_scalar(vl, vl, 1.0 / HC, LN_EPS, ALU.mult, ALU.add).then_inc(signal("latent_var"), 1)
            dve.wait_ge(signal("latent_rstd"), 1)
            dve.tensor_tensor(xc, xc, rl.unsqueeze(2).to_broadcast([P, NB, HC]), ALU.mult).then_inc(signal("cn_ready"), 1)
            for b in range(NB // 2):
                dve.wait_ge(*filled(("v", b)))
                dve.tensor_tensor(v_aug_h[:, 2 * b:2 * b + 2, :, 0:HD],
                                  at(("v", b)).rearrange("p (i h e) -> p i h e", i=2, h=NH),
                                  bv_lx.rearrange("p (h e) -> p h e", h=NH).unsqueeze(1).to_broadcast([P, 2, NH, HD]),
                                  ALU.add).then_inc(free_of(("v", b)), 1)
            for j in range(3):
                dve.wait_ge(*filled(("qkv", j)))
                nb = min(NB, 3 * j + 3) - 3 * j
                pq = at(("qkv", j))[:, 0:nb * 160].rearrange("p (b n) -> p b n", b=nb)
                bs = slice(3 * j, 3 * j + nb)
                then(dve.tensor_tensor(t1[:, bs, :], pq[:, :, 0:64], cosq.unsqueeze(1).to_broadcast([P, nb, 64]), ALU.mult))
                then(dve.tensor_tensor(t2[:, bs, :], pq[:, :, 64:128], sinq.unsqueeze(1).to_broadcast([P, nb, 64]), ALU.mult))
                dve.tensor_copy(v_la[:, bs, :], pq[:, :, 128:160]).then_inc(free_of(("qkv", j)), 1)
            dve.tensor_tensor(t1, t1, t2, ALU.add).then_inc(signal("rope_ready"), 1)
            for b in range(NB):
                dve.wait_ge(*filled(("kp", b, 0)))
                dve.tensor_scalar(kp[:, b, 0:512], at(("kp", b, 0)), 0.0, None, ALU.max).then_inc(free_of(("kp", b, 0)), 1)
            for j in range(2):
                dve.wait_ge(*filled("S", j))
                dve.scalar_tensor_tensor(S[:, 4 * j:4 * j + 4, :], at("S", j).rearrange("p (b t) -> p b t", b=4),
                                         float(HC) ** -0.5, causal.unsqueeze(1).to_broadcast([P, 4, P]),
                                         ALU.mult, ALU.add).then_inc(free_of("S", j), 1)
            for j in range(2):
                dve.wait_ge(*read("S", j))
            then(dve.tensor_reduce(r1, S, AX, ALU.max))
            dve.tensor_tensor(S, S, r1.unsqueeze(2).to_broadcast([P, NB, P]), ALU.subtract)\
               .then_inc(signal("S_less_max"), 1)

            def mask_heads(b):
                dve.wait_ge(*filled(("kv", b)))
                dve.tensor_tensor(kvm[:, b, :], at(("kv", b))[:, 0:CH * AUG], bdmask, ALU.mult)\
                   .then_inc(free_of(("kv", b)), 1)

            dve.wait_ge(signal("S_exp"), 1)
            then(dve.tensor_reduce(r2, S, AX, ALU.add))
            then(dve.reciprocal(r2, r2))
            dve.tensor_tensor(S, S, r2.unsqueeze(2).to_broadcast([P, NB, P]), ALU.mult).then_inc(signal("P_ready"), 1)
            for b in range(KV_LATE[0]):
                mask_heads(b)
            dve.wait_ge(slots_stored, 16)

            norm_layer(0, lambda c: add_residual(0, 0, c))
            for b in KV_LATE:
                mask_heads(b)
            for n in range(G):
                for c in range(1, CH, 2):
                    dve.wait_ge(*filled(("qp", c, n)))
                    dve.tensor_scalar(qp[:, c, n * 512:n * 512 + 512], at(("qp", c, n)), 0.0, None, ALU.max)\
                       .then_inc(free_of(("qp", c, n)), 1)
            for b in range(NB):
                dve.wait_ge(*filled(("ox", b)))
                po = at(("ox", b))[:, 0:CH * AUG].rearrange("p (h e) -> p h e", e=HD + 1)
                then(dve.tensor_scalar(den[:, b, :], po[:, :, HD], 1e-8, None, ALU.add))
                then(dve.reciprocal(rden[:, b, :], den[:, b, :]))
                dve.tensor_tensor(a_x[:, b, :].rearrange("p (h e) -> p h e", h=NH), po[:, :, 0:HD],
                                  rden[:, b, :].unsqueeze(2).to_broadcast([P, NH, HD]), ALU.mult)\
                   .then_inc(free_of(("ox", b)), 1)
            norm_layer(1, lambda c: add_residual(1, 1, c))
            dve.wait_ge(*filled("gate"))
            pg = at("gate")[:, 0:NB * E].rearrange("p (b e) -> p b e", b=NB)
            then(dve.tensor_reduce(gm, pg, AX, ALU.max))
            dve.tensor_tensor(lg, pg, gm.unsqueeze(2).to_broadcast([P, NB, E]), ALU.subtract).then_inc(free_of("gate"), 1)
            dve.wait_ge(*read("gate"))
            dve.wait_ge(signal("gate_exp"), 1)
            then(dve.tensor_reduce(gs, pr, AX, ALU.add))
            then(dve.reciprocal(gs, gs))
            then(dve.tensor_tensor(pr, pr, gs.unsqueeze(2).to_broadcast([P, NB, E]), ALU.mult))
            rank_experts(dve, then, pr, GT, GE, tri, rank, 0)
            then(dve.scalar_tensor_tensor(comb, rank, 1.5, pr, ALU.is_lt, ALU.mult))
            then(dve.tensor_reduce(gr, comb, AX, ALU.add))
            then(dve.reciprocal(gr, gr))
            then(dve.tensor_tensor(comb, comb, gr.unsqueeze(2).to_broadcast([P, NB, E]), ALU.mult))
            dve.tensor_tensor(comb, comb, alpha.unsqueeze(1).to_broadcast([P, NB, E]), ALU.mult)\
               .then_inc(signal("comb_ready"), 1)
            dve.wait_ge(signal("comb_ready"), 1)
            count = [0]
            context_dve(dve, count)
            for c in range(NCH):
                dve.wait_ge(*filled(("yb", c)))
                dve.tensor_tensor(H[:, 2 * c:2 * c + 2, :].rearrange("p b n -> p (b n)"), at(("yb", c)),
                                  X[:, 2 * c:2 * c + 2, :].rearrange("p b n -> p (b n)"), ALU.add)\
                   .then_inc(free_of(("yb", c)), 1)
            for c in range(NCH):
                dve.wait_ge(*read(("yb", c)))
                dve.wait_ge(*read(("k2", c)))
            values_dve(dve, count)
            dve.wait_ge(signal("parts_zero"), 1)
            with dve.Fori(0, E // 2) as trip:
                quantise_keys(dve, trip, 0)
                quantise_keys(dve, trip, 1)
                for w in range(2):
                    for c in range(NCH):
                        dve.wait_ge(*filled(("y2", w, c), trip=trip))
                        dve.wait_ge(*read(("y2", 1 - w, c), trip=trip - 1 + w))
                        for i in range(2):
                            b = 2 * c + i
                            ins = dve.scalar_tensor_tensor(H[:, b, :], at(("y2", w, c))[:, i * D:i * D + D],
                                                           comb[:, b, bass.ds(2 * trip + w, 1)],
                                                           H[:, b, :], ALU.mult, ALU.add)
                        ins.then_inc(free_of(("y2", w, c)), 1)
            for c in range(NCH):
                dve.wait_ge(*read(("y2", 1, c), trip=E // 2 - 1))
            norm_layer(2)

            def then_in_loop(ins, h, which, trip):
                sems = (raw_ready, recip_ready)
                ins.then_inc(sems[1 - which], 1)
                dve.wait_ge(sems[1 - which], KV * trip + h + 1 - (0 if which else 2))

            last_output = grouped_attention_dve(dve, then_in_loop)
            norm_layer(3, last_output)
            dve.wait_ge(signal("query_parts_zero"), 1)
            for q in range(NB // QB):
                quantise_queries(dve, count, q)
            for b in DVE_TURNS:
                dve.wait_ge(*filled(("qspT", b)))
                dve.tensor_copy(qspT[:, :, b * P:b * P + P], at(("qspT", b)).bitcast(BF16).rearrange("p (j t) -> p j t", j=PAIRS))\
                   .then_inc(free_of(("qspT", b)), 1)
            for b in range(NB):
                dve.wait_ge(*read(("qspT", b)))
            cross_dve(dve)
            norm_layer(4, lambda c: add_residual(4, 3, c))
            add_experts = experts_dve(dve, then)
            norm_layer(5, add_experts)

        @block.gpsimd
        def _(pool):
            pool.memset(H[:, 0, :], 0.0).then_inc(signal("zeros_ready"), 1)
            pool.memset(XT_flat[:, KD * N:], 0.0).then_inc(signal("spare_ready"), 1)
            pool.memset(kspT[:].rearrange("p b n -> p (b n)").bitcast(F32), 0.0).then_inc(signal("parts_zero"), 1)
            pool.memset(neghalf[:], -0.5).then_inc(signal("neghalf_ready"), 1)
            pool.memset(v_aug_h[:, :, :, HD:HD + 1], 1.0).then_inc(signal("ones_ready"), 1)
            pool.wait_ge(s_w["w_la"], 16)
            pool.tensor_tensor(Wsum, W_kv, W_res, ALU.add).then_inc(wsum_ready, 1)
            pool.wait_ge(s_w["x"], 16)
            pool.wait_ge(s_w["bias0"], 16)
            pool.wait_ge(signal("neghalf_ready"), 1)

            def plus_bias(nth, c):
                pool.tensor_tensor(XB[:, 2 * c:2 * c + 2, :], X[:, 2 * c:2 * c + 2, :],
                                   biases[:, nth, :].unsqueeze(1).to_broadcast([P, 2, D]), ALU.add).then_inc(xb_ready, 1)

            def norm_layer(layer, nth=None):
                for c in range(NCH + 1):
                    if c < NCH:
                        pool.wait_ge(var_ready, layer * NCH + c + 1)
                        pool.tensor_tensor(rstd[:, 2 * c:2 * c + 2], ve[:, 2 * c:2 * c + 2], neghalf[:, 0:2], ALU.pow)\
                            .then_inc(rstd_ready, 1)
                    if c and nth is not None:
                        pool.wait_ge(x_ready, layer * NB + 2 * c)
                        plus_bias(nth, c - 1)

            for c in range(NCH):
                plus_bias(0, c)
            pool.wait_ge(signal("latent_var"), 1)
            pool.tensor_tensor(rl, vl, neghalf[:], ALU.pow).then_inc(signal("latent_rstd"), 1)
            for b in range(0, NB, 2):
                pool.wait_ge(*read(("v", b // 2)))
            pool.wait_ge(signal("ones_ready"), 1)
            pool.tensor_tensor(v_aug, v_aug, mask.unsqueeze(2).to_broadcast([P, NB, NH * (HD + 1)]), ALU.mult)\
                .then_inc(signal("values_masked"), 1)
            norm_layer(0, 1)
            norm_layer(1)
            pool.wait_ge(*filled(("v2", KD - 1, G - 1)))
            pool.memset(ctxT[:], 0.0).then_inc(signal("query_parts_zero"), 1)
            pool.wait_ge(s_w["late"], 16)
            pool.tensor_scalar(kws[:], kw, DH ** -0.5, None, ALU.mult).then_inc(signal("kws_ready"), 1)
            pool.wait_ge(signal("kws_ready"), 1)
            pool.wait_ge(s_w["w_qkv"], 32)
            for h in range(KV):
                wq = w_qkv[:, h, :, 0:GRP * DH].rearrange("p k (g c) -> p k g c", g=GRP)
                for k in range(KD):
                    ins = pool.tensor_tensor(wq[:, k], wq[:, k], kws[:, h * GRP:h * GRP + GRP].unsqueeze(2).to_broadcast([P, GRP, DH]),
                                       ALU.mult)
                ins.then_inc(w_scaled, 1)
            bq = b_qkv[:, :, 0:GRP * DH].rearrange("p h (g c) -> p h g c", g=GRP)
            pool.tensor_tensor(bq, bq, kws[:].rearrange("p (h g) -> p h g", h=KV).unsqueeze(3).to_broadcast([P, KV, GRP, DH]),
                               ALU.mult).then_inc(w_scaled, 1)
            norm_layer(2, 2)
            grouped_attention_pool(pool)
            norm_layer(3, 3)
            norm_layer(4)
            experts_pool(pool)
            norm_layer(5)

        @block.sync
        def _(sp):
            first = la["Wqkv"][0]
            sp.dma_start(w_la[:, 0:first], W["w_la"][:, 0:first]).then_inc(s_w["w_first"], 16)
            sp.dma_start(XT[:, :, 0:512], W["xT"][:, :, 0:512]).then_inc(s_w["xT0"], 16)
            sp.dma_start(w_la[:, first:], W["w_la"][:, first:]).then_inc(s_w["w_la"], 16)
            sp.dma_start(w_lx, W["w_lx"]).then_inc(s_w["w_lx"], 16)
            sp.dma_start(X[:], W["x"]).then_inc(s_w["x"], 16)
            sp.wait_ge(signal("zeros_ready"), 1)
            sp.dma_start(x_slots.rearrange("(t p) n -> p t n", p=P), H[:, 0:1, :].to_broadcast([P, SLOT_TILES, D]))\
              .then_inc(slots_stored, 16)
            sp.dma_start(w_xk, W["w_xk"]).then_inc(s_w["w_xx"], 16)
            sp.dma_start(w_xx[:], W["w_xx"]).then_inc(s_w["w_xx"], 16)
            for e in range(E):
                w = e % 2
                if e >= 2:
                    sp.wait_ge(*filled(("y2", w, NCH - 1), trip=e // 2 - 1))
                    sp.wait_ge(*read(("h1", w, KD - 1, G - 1), trip=e // 2 - 1))
                sp.dma_start(f1[:, w], W["fc1"][:, e]).then_inc(fc_loaded[w], 16)
                sp.dma_start(f2[:, w], W["fc2"][:, e]).then_inc(fc_loaded[w], 16)
                sp.dma_start(f1b[:, w], W["fc1_b"][:, e]).then_inc(fc_loaded[w], 16)
            sp.dma_start(late[:], W["late"]).then_inc(s_w["late"], 16)
            sp.wait_ge(*filled(("y", 1, NCH - 1)))
            sp.dma_start(w_qkv, W["w_qkv"]).then_inc(s_w["w_qkv"], 16)
            sp.dma_start(b_qkv, W["b_qkv"]).then_inc(s_w["w_qkv"], 16)
            sp.dma_start(WoT1, W["WoT1"]).then_inc(s_w["WoT1"], 16)
            sp.wait_ge(banks.full[B_Y], base[B_Y] + NB)
            sp.dma_start(W_gu, W["w_gu"]).then_inc(s_w["w_gu"], 16)
            sp.dma_start(W_dn, W["w_dn"]).then_inc(s_w["w_dn"], 16)
            sp.wait_ge(banks.full[XS + 2], base2[XS + 2] + NB * HX // 2)
            sp.dma_start(W_sh, W["w_sh"]).then_inc(s_w["w_sh"], 16)
            sp.dma_start(W_sd, W["w_sd"]).then_inc(s_w["w_sh"], 16)
            experts_sp(sp)
            for b in range(NB):
                sp.wait_ge(x_ready, 5 * NB + b + 1)
                sp.dma_start(out[b], X[:, b, :]).then_inc(s_out, 16)
            sp.wait_ge(s_out, 16 * NB)


def column_table(parts):
    table, at = {}, 0
    for name, a in parts:
        table[name] = (at, at + a.shape[1])
        at += a.shape[1]
    return table, at


def side_by_side(np, parts):
    table, width = column_table(parts)
    whole = np.zeros((P, width), np.float32)
    for name, a in parts:
        whole[:a.shape[0], table[name][0]:table[name][1]] = a
    return whole, table, width


def lay_out(np, i):
    NB, _, D = i["x"].shape
    KD = D // P
    rows = lambda w: np.concatenate([w[k * P:(k + 1) * P] for k in range(w.shape[0] // P)], axis=1)
    over = lambda v: np.broadcast_to(v[None, :], (P, v.shape[0]))
    cols = lambda v: v.reshape(-1, P).T
    T = {"NB": NB, "D": D}
    A = {}
    A["xT"] = rows(i["x"].reshape(NB * P, D).T).reshape(P, KD, NB * P)
    A["ctxT"] = rows(i["ctx_2048"].reshape(NB * P, D).T).reshape(P, KD, NB * P)
    A["x"] = i["x"].transpose(1, 0, 2)
    A["ident"] = np.eye(P, dtype=np.float32)
    A["biases"] = np.stack([over(i[n]) for n in ("L0_attn_b_out_res", "L0_xattn_bo", "L1_attn_bo", "L1_xattn_bp")], axis=1)
    HC = i["L0_attn_W_compress"].shape[0]
    half = np.r_[HC // 2:HC, 0:HC // 2]
    Wq, Wk, Wv = i["L0_attn_W_q_comp"], i["L0_attn_W_kv_comp"][:HC], i["L0_attn_W_kv_comp"][HC:]
    t = np.arange(P, dtype=np.float32)[:, None]
    f = t * (1.0 / 10000.0 ** (np.arange(0, HC, 2, dtype=np.float32) / HC))[None, :].astype(np.float32)
    cos, sin = np.cos(f).astype(np.float32), np.sin(f).astype(np.float32)
    cos, sin = np.concatenate([cos, cos], 1), np.concatenate([-sin, sin], 1)
    E = i["L0_ffn_gate_w"].shape[1]
    heads = np.zeros((P, 8 * 34), np.float32)
    heads.reshape(2, P // 2, 8, 2, 17)[0, :, :, 0] = 1
    heads.reshape(2, P // 2, 8, 2, 17)[1, :, :, 1] = 1
    la = [("WkvT", rows(i["L0_attn_W_to_kv"].T)), ("WcT", i["L0_attn_W_compress"].T),
          ("Wqkv", np.concatenate([Wq.T, Wk.T, Wq[half].T, Wk[half].T, Wv.T], axis=1)),
          ("Wc2lT", i["L0_attn_W_comp2lat"].T), ("W_kv", i["L0_attn_W_to_kv"]), ("W_res", i["L0_attn_W_out_res"].T),
          ("gamma", i["L0_attn_ln_gamma"][:, None]), ("beta", i["L0_attn_ln_beta"][:, None]),
          ("cos", np.concatenate([cos, cos], 1)), ("sin", np.concatenate([sin, sin], 1)),
          ("causal", np.where(np.tril(np.ones((P, P), bool)), 0.0, -1e30).astype(np.float32)),
          ("bv_lx", over(i["L0_xattn_bv"])), ("mask", i["mask_BxS2_ff1"].T),
          ("bq_lx", cols(i["L0_xattn_bq"])), ("bk_lx", cols(i["L0_xattn_bk"])), ("bdmask", heads),
          ("gate_w", rows(i["L0_ffn_gate_w"])), ("alpha", over(i["L0_ffn_alpha"])),
          ("tri", np.broadcast_to(np.tril(np.ones((E, E), np.float32), -1).reshape(1, -1), (P, E * E))),
          ("fc2_b", i["L0_ffn_fc2_b"])]
    A["w_la"], T["la"], T["la_cols"] = side_by_side(np, la)
    BDk, BDq = np.zeros((P, 8 * 64), np.float32), np.zeros((P, P), np.float32)
    for h in range(8):
        BDk[h * 16:h * 16 + 16, h * 64:h * 64 + 64] = i["L0_xattn_Wkf"].T
        BDq[h * 16:h * 16 + 16, h % 2 * 64:h % 2 * 64 + 64] = i["L0_xattn_Wqf"].T
    lx = [("WqT", rows(i["L0_xattn_Wq"].T)), ("WkT", rows(i["L0_xattn_Wk"].T)), ("WvT", rows(i["L0_xattn_Wv"].T)),
          ("WoT", rows(i["L0_xattn_Wo"].T)), ("BDk", BDk), ("BDq", BDq)]
    A["w_lx"], T["lx"], T["lx_cols"] = side_by_side(np, lx)
    KV, GRP, DH = 8, 4, 64
    head = lambda n: i[n].reshape(KV, -1, DH, D)
    whole = np.concatenate([head("L1_attn_Wq"), head("L1_attn_Wk"), head("L1_attn_Wv")], axis=1)
    A["w_qkv"] = whole.reshape(KV, (GRP + 2) * DH, KD, P).transpose(3, 0, 2, 1)
    bias = np.concatenate([i[n].reshape(KV, -1) for n in ("L1_attn_bq", "L1_attn_bk", "L1_attn_bv")], axis=1)
    A["b_qkv"] = np.broadcast_to(bias[None], (P,) + bias.shape)
    A["WoT1"] = i["L1_attn_Wo"].T.reshape(KV * 2, P, D).transpose(1, 0, 2)
    f = t * (1.0 / 10000.0 ** (np.arange(0, DH, 2, dtype=np.float32) / DH))[None, :].astype(np.float32)
    cos, sin = np.cos(f).astype(np.float32), np.sin(f).astype(np.float32)
    late = [("cos", np.concatenate([cos, cos], 1)), ("sin", np.concatenate([-sin, sin], 1)),
            ("causal", dict(la)["causal"]), ("kw", over(i["L1_attn_key_weights"])),
            ("router", rows(i["L1_ffn_router_w"].T)), ("tri", dict(la)["tri"]),
            ("earlier", np.triu(np.ones((P, P), np.float32), 1)), ("ones", np.ones((P, P), np.float32)),
            ("tile_no", over(np.arange((NB * P + E * (P - 1)) // P, dtype=np.float32)))]
    A["late"], T["lt"], T["late_cols"] = side_by_side(np, late)
    bkv = i["L1_xattn_bkv"]
    xk = [("Wk", rows(i["L1_xattn_Wkv"][:, :D])), ("Wv", rows(i["L1_xattn_Wkv"][:, D:])), ("bk", over(bkv[:D])),
          ("bv", cols(bkv[D:]))]
    A["w_xk"], T["xk"], T["xk_cols"] = side_by_side(np, xk)
    xx = [("Wq", rows(i["L1_xattn_Wq"])), ("Wp", rows(i["L1_xattn_Wp"])), ("bq", over(i["L1_xattn_bq"]))]
    A["w_xx"], T["xx"], T["xx_cols"] = side_by_side(np, xx)
    by_rows = lambda w: w.reshape(w.shape[0], -1, P, w.shape[2]).transpose(2, 0, 1, 3)
    by_depth = lambda w: w.reshape(w.shape[0], -1, P, w.shape[2]).transpose(2, 1, 0, 3)
    A["w_gu"], A["w_dn"] = by_depth(i["L1_ffn_gate_up_proj"]), by_depth(i["L1_ffn_down_proj"])
    A["w_sh"] = np.concatenate([i["L1_ffn_shared_gate_w"], i["L1_ffn_shared_up_w"]], axis=1).reshape(KD, P, -1).transpose(1, 0, 2)
    A["w_sd"] = i["L1_ffn_shared_down_w"].reshape(-1, P, D).transpose(1, 0, 2)
    A["fc1"], A["fc2"] = by_rows(i["L0_ffn_fc1_w"]), by_rows(i["L0_ffn_fc2_w"])
    A["fc1_b"] = i["L0_ffn_fc1_b"].reshape(E, KD, P).transpose(2, 0, 1)
    return T, {n: np.ascontiguousarray(a) for n, a in A.items()}


def kernel(**inputs):
    import numpy as np
    import concourse.bacc as bacc
    from concourse.bass_utils import run_bass_kernel_spmd as run

    inputs = {n: np.asarray(a) for n, a in inputs.items()}
    T, arrays = lay_out(np, inputs)
    nc = bacc.Bacc("TRN2", target_bir_lowering=False, num_devices=1)
    W = {n: nc.dram_tensor("in_" + n, a.shape, mybir.dt.from_np(a.dtype), kind="ExternalInput").ap() for n, a in arrays.items()}
    out = nc.dram_tensor("out", inputs["x"].shape, F32, kind="ExternalOutput").ap()
    build(nc, T, W, out)
    return run(nc, [{"in_" + n: a for n, a in arrays.items()}], core_ids=[0]).results[0]["out"]
```
